# Optimizing a Trainium2 kernel written in Bass

```python
import numpy as np
import jax
import jax.numpy as jnp

def _softmax(x, axis=-1):
    return jax.nn.softmax(x, axis=axis)

def _gelu(x):
    return jax.nn.gelu(x, approximate=True)

def _silu(x):
    return jax.nn.silu(x)

def _sigmoid(x):
    return jax.nn.sigmoid(x)

def _layernorm(x, axis=-1, eps=1e-05):
    m = jnp.mean(x, axis=axis, keepdims=True)
    v = jnp.var(x, axis=axis, keepdims=True)
    return (x - m) / jnp.sqrt(v + eps)

def _scatter_add(tgt, idx, src, axis=0):
    return tgt.at[idx].add(src)

def _segment_sum(src, seg, n):
    return jax.ops.segment_sum(src, seg, n)
kernel_name = 'mk_lm_tower_d1_tok_ids512_r4_bbf968'

def setup_inputs(seed: int=0):
    np.random.seed(seed)
    _w = jnp.asarray

    def _rec_inputs():
        import jax
        import jax.numpy as jnp
        _rk = jax.random.key(seed)
        x = jax.random.randint(jax.random.fold_in(_rk, 1), (32, 256), 0, 31983, jnp.int32)
        return x
    x = _rec_inputs()

    def _L0_tok_setup():
        import jax, jax.numpy as jnp
        import numpy as np
        B, S, D, H, K, F, L, V = (2, 512, 128, 8, 64, 512, 4, 8000)

        def _forward(x, emb, pos, Wq, bq, Wk, bk, Wv, bv, Wo, bo, W1, b1, W2, b2):
            b, s = x.shape
            h = emb[x] + pos[:s][None]
            causal = jnp.triu(jnp.ones((s, s), dtype=bool), 1)
            scale = 1.0 / jnp.sqrt(jnp.float32(K))

            def layer(h, p):
                wq, bq_, wk, bk_, wv, bv_, wo, bo_, w1, b1_, w2, b2_ = p
                q = (h @ wq + bq_).reshape(b, s, H, K).transpose(0, 2, 1, 3)
                k = (h @ wk + bk_).reshape(b, s, H, K).transpose(0, 2, 1, 3)
                v = (h @ wv + bv_).reshape(b, s, H, K).transpose(0, 2, 1, 3)
                scores = jnp.einsum('bhqk,bhsk->bhqs', q, k) * scale
                scores = jnp.where(causal, -jnp.inf, scores)
                attn = jax.nn.softmax(scores, axis=-1)
                o = jnp.einsum('bhqs,bhsk->bhqk', attn, v)
                o = o.transpose(0, 2, 1, 3).reshape(b, s, H * K)
                h = h + (o @ wo + bo_)
                ff = jax.nn.relu(h @ w1 + b1_) @ w2 + b2_
                return (h + ff, None)
            h, _ = jax.lax.scan(layer, h, (Wq, bq, Wk, bk, Wv, bv, Wo, bo, W1, b1, W2, b2))
            return h
        key = jax.random.key(seed)
        ks = jax.random.split(key, 10)
        s = 0.02
        HK = H * K
        return {'x': jax.random.randint(ks[0], (B, S), 0, V, dtype=jnp.int64), 'emb': jax.random.normal(ks[1], (V, D), jnp.float32) * s, 'pos': jax.random.normal(ks[2], (S, D), jnp.float32) * s, 'Wq': jax.random.normal(ks[3], (L, D, HK), jnp.float32) * s, 'bq': jnp.zeros((L, HK), jnp.float32), 'Wk': jax.random.normal(ks[4], (L, D, HK), jnp.float32) * s, 'bk': jnp.zeros((L, HK), jnp.float32), 'Wv': jax.random.normal(ks[5], (L, D, HK), jnp.float32) * s, 'bv': jnp.zeros((L, HK), jnp.float32), 'Wo': jax.random.normal(ks[6], (L, HK, D), jnp.float32) * s, 'bo': jnp.zeros((L, D), jnp.float32), 'W1': jax.random.normal(ks[7], (L, D, F), jnp.float32) * s, 'b1': jnp.zeros((L, F), jnp.float32), 'W2': jax.random.normal(ks[8], (L, F, D), jnp.float32) * s, 'b2': jnp.zeros((L, D), jnp.float32)}
    _L0_tok_all = _L0_tok_setup()
    _L0_tok_in = {k: v for k, v in _L0_tok_all.items() if k in ('emb', 'pos', 'Wq', 'bq', 'Wk', 'bk', 'Wv', 'bv', 'Wo', 'bo', 'W1', 'b1', 'W2', 'b2')}
    del _L0_tok_all

    def _L0_attn_setup():
        import jax, jax.numpy as jnp
        import numpy as np
        import math
        B_, T_, D_, S_, K_ = (4, 2048, 128, 64, 5)
        R_MIN, R_MAX, PHASE_MAX = (0.8, 0.99, 2.0 * math.pi)

        def _layernorm(x, w, b, eps=1e-05):
            mu = jnp.mean(x, axis=-1, keepdims=True)
            var = jnp.mean(jnp.square(x - mu), axis=-1, keepdims=True)
            return (x - mu) * jax.lax.rsqrt(var + eps) * w + b

        def _binop_diag(a, b):
            a_l, a_s = a
            b_l, b_s = b
            return (a_l * b_l, b_l * a_s + b_s)
        key = jax.random.key(seed)
        ks = jax.random.split(key, 12)
        x = jax.random.normal(ks[0], (B_, T_, D_), dtype=jnp.float32)
        ln_w = jnp.ones((D_,), jnp.float32)
        ln_b = jnp.zeros((D_,), jnp.float32)
        W_in = jax.random.normal(ks[1], (2 * S_, D_), jnp.float32) / math.sqrt(D_)
        conv_w = jax.random.normal(ks[2], (S_, S_, K_), jnp.float32) / math.sqrt(S_ * K_)
        conv_b = jnp.zeros((S_,), jnp.float32)
        u1 = jax.random.uniform(ks[3], (S_,), jnp.float32)
        nu_log = jnp.log(-0.5 * jnp.log(u1 * (R_MAX + R_MIN) * (R_MAX - R_MIN) + R_MIN ** 2))
        u2 = jax.random.uniform(ks[4], (S_,), jnp.float32)
        theta_log = jnp.log(PHASE_MAX * u2)
        L_mod = jnp.exp(-jnp.exp(nu_log))
        gamma_log = jnp.log(jnp.sqrt(1.0 - jnp.square(L_mod)))
        B_re = jax.random.normal(ks[5], (S_, S_), jnp.float32) / math.sqrt(2 * S_)
        B_im = jax.random.normal(ks[6], (S_, S_), jnp.float32) / math.sqrt(2 * S_)
        C_re = jax.random.normal(ks[7], (S_, S_), jnp.float32) / math.sqrt(S_)
        C_im = jax.random.normal(ks[8], (S_, S_), jnp.float32) / math.sqrt(S_)
        W_out = jax.random.normal(ks[9], (D_, S_), jnp.float32) / math.sqrt(S_)
        b_out = jnp.zeros((D_,), jnp.float32)
        return dict(x=x, ln_w=ln_w, ln_b=ln_b, W_in=W_in, conv_w=conv_w, conv_b=conv_b, nu_log=nu_log, theta_log=theta_log, gamma_log=gamma_log, B_re=B_re, B_im=B_im, C_re=C_re, C_im=C_im, W_out=W_out, b_out=b_out)
    _L0_attn_all = _L0_attn_setup()
    _L0_attn_in = {k: v for k, v in _L0_attn_all.items() if k in ('ln_w', 'ln_b', 'W_in', 'conv_w', 'conv_b', 'nu_log', 'theta_log', 'gamma_log', 'B_re', 'B_im', 'C_re', 'C_im', 'W_out', 'b_out')}
    del _L0_attn_all

    def _L0_ffn_setup():
        import jax, jax.numpy as jnp
        import numpy as np
        B, S, H, E, K = (8, 1024, 128, 8, 2)
        key = jax.random.key(seed)
        ks = jax.random.split(key, 7)
        s_h = 1.0 / np.sqrt(H)
        s_2h = 1.0 / np.sqrt(2 * H)
        return {'x': jax.random.normal(ks[0], (B, S, H), dtype=jnp.float32), 'gate_w': jax.random.uniform(ks[1], (H, E), minval=-s_h, maxval=s_h, dtype=jnp.float32), 'gate_b': jax.random.uniform(ks[2], (E,), minval=-s_h, maxval=s_h, dtype=jnp.float32), 'w1': jax.random.uniform(ks[3], (E, H, 2 * H), minval=-s_h, maxval=s_h, dtype=jnp.float32), 'b1': jax.random.uniform(ks[4], (E, 2 * H), minval=-s_h, maxval=s_h, dtype=jnp.float32), 'w2': jax.random.uniform(ks[5], (E, 2 * H, H), minval=-s_2h, maxval=s_2h, dtype=jnp.float32), 'b2': jax.random.uniform(ks[6], (E, H), minval=-s_2h, maxval=s_2h, dtype=jnp.float32)}
    _L0_ffn_all = _L0_ffn_setup()
    _L0_ffn_in = {k: v for k, v in _L0_ffn_all.items() if k in ('gate_w', 'gate_b', 'w1', 'b1', 'w2', 'b2')}
    del _L0_ffn_all
    return {'x': x, 'L0_tok_emb': _L0_tok_in['emb'], 'L0_tok_pos': _L0_tok_in['pos'], 'L0_tok_Wq': _L0_tok_in['Wq'], 'L0_tok_bq': _L0_tok_in['bq'], 'L0_tok_Wk': _L0_tok_in['Wk'], 'L0_tok_bk': _L0_tok_in['bk'], 'L0_tok_Wv': _L0_tok_in['Wv'], 'L0_tok_bv': _L0_tok_in['bv'], 'L0_tok_Wo': _L0_tok_in['Wo'], 'L0_tok_bo': _L0_tok_in['bo'], 'L0_tok_W1': _L0_tok_in['W1'], 'L0_tok_b1': _L0_tok_in['b1'], 'L0_tok_W2': _L0_tok_in['W2'], 'L0_tok_b2': _L0_tok_in['b2'], 'L0_attn_ln_w': _L0_attn_in['ln_w'], 'L0_attn_ln_b': _L0_attn_in['ln_b'], 'L0_attn_W_in': _L0_attn_in['W_in'], 'L0_attn_conv_w': _L0_attn_in['conv_w'], 'L0_attn_conv_b': _L0_attn_in['conv_b'], 'L0_attn_nu_log': _L0_attn_in['nu_log'], 'L0_attn_theta_log': _L0_attn_in['theta_log'], 'L0_attn_gamma_log': _L0_attn_in['gamma_log'], 'L0_attn_B_re': _L0_attn_in['B_re'], 'L0_attn_B_im': _L0_attn_in['B_im'], 'L0_attn_C_re': _L0_attn_in['C_re'], 'L0_attn_C_im': _L0_attn_in['C_im'], 'L0_attn_W_out': _L0_attn_in['W_out'], 'L0_attn_b_out': _L0_attn_in['b_out'], 'L0_ffn_gate_w': _L0_ffn_in['gate_w'], 'L0_ffn_gate_b': _L0_ffn_in['gate_b'], 'L0_ffn_w1': _L0_ffn_in['w1'], 'L0_ffn_b1': _L0_ffn_in['b1'], 'L0_ffn_w2': _L0_ffn_in['w2'], 'L0_ffn_b2': _L0_ffn_in['b2']}

def reference(x, L0_tok_emb, L0_tok_pos, L0_tok_Wq, L0_tok_bq, L0_tok_Wk, L0_tok_bk, L0_tok_Wv, L0_tok_bv, L0_tok_Wo, L0_tok_bo, L0_tok_W1, L0_tok_b1, L0_tok_W2, L0_tok_b2, L0_attn_ln_w, L0_attn_ln_b, L0_attn_W_in, L0_attn_conv_w, L0_attn_conv_b, L0_attn_nu_log, L0_attn_theta_log, L0_attn_gamma_log, L0_attn_B_re, L0_attn_B_im, L0_attn_C_re, L0_attn_C_im, L0_attn_W_out, L0_attn_b_out, L0_ffn_gate_w, L0_ffn_gate_b, L0_ffn_w1, L0_ffn_b1, L0_ffn_w2, L0_ffn_b2):
    import jax
    import jax.numpy as jnp

    def _L0_tok_ref(x, emb, pos, Wq, bq, Wk, bk, Wv, bv, Wo, bo, W1, b1, W2, b2):
        import jax, jax.numpy as jnp
        import numpy as np
        B, S, D, H, K, F, L, V = (2, 512, 128, 8, 64, 512, 4, 8000)

        def _forward(x, emb, pos, Wq, bq, Wk, bk, Wv, bv, Wo, bo, W1, b1, W2, b2):
            b, s = x.shape
            h = emb[x] + pos[:s][None]
            causal = jnp.triu(jnp.ones((s, s), dtype=bool), 1)
            scale = 1.0 / jnp.sqrt(jnp.float32(K))

            def layer(h, p):
                wq, bq_, wk, bk_, wv, bv_, wo, bo_, w1, b1_, w2, b2_ = p
                q = (h @ wq + bq_).reshape(b, s, H, K).transpose(0, 2, 1, 3)
                k = (h @ wk + bk_).reshape(b, s, H, K).transpose(0, 2, 1, 3)
                v = (h @ wv + bv_).reshape(b, s, H, K).transpose(0, 2, 1, 3)
                scores = jnp.einsum('bhqk,bhsk->bhqs', q, k) * scale
                scores = jnp.where(causal, -jnp.inf, scores)
                attn = jax.nn.softmax(scores, axis=-1)
                o = jnp.einsum('bhqs,bhsk->bhqk', attn, v)
                o = o.transpose(0, 2, 1, 3).reshape(b, s, H * K)
                h = h + (o @ wo + bo_)
                ff = jax.nn.relu(h @ w1 + b1_) @ w2 + b2_
                return (h + ff, None)
            h, _ = jax.lax.scan(layer, h, (Wq, bq, Wk, bk, Wv, bv, Wo, bo, W1, b1, W2, b2))
            return h
        return _forward(x, emb, pos, Wq, bq, Wk, bk, Wv, bv, Wo, bo, W1, b1, W2, b2)

    def _L0_attn_ref(x, ln_w, ln_b, W_in, conv_w, conv_b, nu_log, theta_log, gamma_log, B_re, B_im, C_re, C_im, W_out, b_out):
        import jax, jax.numpy as jnp
        import numpy as np
        import math
        B_, T_, D_, S_, K_ = (4, 2048, 128, 64, 5)
        R_MIN, R_MAX, PHASE_MAX = (0.8, 0.99, 2.0 * math.pi)

        def _layernorm(x, w, b, eps=1e-05):
            mu = jnp.mean(x, axis=-1, keepdims=True)
            var = jnp.mean(jnp.square(x - mu), axis=-1, keepdims=True)
            return (x - mu) * jax.lax.rsqrt(var + eps) * w + b

        def _binop_diag(a, b):
            a_l, a_s = a
            b_l, b_s = b
            return (a_l * b_l, b_l * a_s + b_s)
        r = x
        h = _layernorm(x, ln_w, ln_b)
        h = h @ W_in.T
        xg, v = jnp.split(h, 2, axis=-1)
        pad = (K_ - 1) // 2
        vc = jax.lax.conv_general_dilated(v.transpose(0, 2, 1), conv_w, window_strides=(1,), padding=[(pad, pad)], dimension_numbers=('NCH', 'OIH', 'NCH'))
        v = vc.transpose(0, 2, 1) + conv_b
        L_mod = jnp.exp(-jnp.exp(nu_log))
        theta = jnp.exp(theta_log)
        Lam = (L_mod * jnp.cos(theta) + 1j * (L_mod * jnp.sin(theta))).astype(jnp.complex64)
        Bn = (B_re + 1j * B_im).astype(jnp.complex64) * jnp.exp(gamma_log)[:, None]
        Be = v.astype(jnp.complex64) @ Bn.T
        L_el = jnp.broadcast_to(Lam, Be.shape)
        _, states = jax.lax.associative_scan(_binop_diag, (L_el, Be), axis=1)
        Cc = (C_re + 1j * C_im).astype(jnp.complex64)
        y = (states @ Cc.T).real
        out = jax.nn.gelu(xg, approximate=False) * y
        return out @ W_out.T + b_out + r

    def _L0_ffn_ref(x, gate_w, gate_b, w1, b1, w2, b2):
        import jax, jax.numpy as jnp
        import numpy as np
        B, S, H, E, K = (8, 1024, 128, 8, 2)
        logits = jnp.einsum('bsh,he->bse', x, gate_w) + gate_b
        topk_vals, topk_idx = jax.lax.top_k(logits, K)
        topk_weights = jax.nn.softmax(topk_vals, axis=-1)
        mask = jax.nn.one_hot(topk_idx, E, dtype=topk_weights.dtype)
        weights = jnp.einsum('bske,bsk->bse', mask, topk_weights)
        h = jax.nn.relu(jnp.einsum('bsh,ehf->bsef', x, w1) + b1)
        expert_out = jnp.einsum('bsef,efh->bseh', h, w2) + b2
        return jnp.einsum('bseh,bse->bsh', expert_out, weights)
    h = _L0_tok_ref(x, L0_tok_emb, L0_tok_pos, L0_tok_Wq, L0_tok_bq, L0_tok_Wk, L0_tok_bk, L0_tok_Wv, L0_tok_bv, L0_tok_Wo, L0_tok_bo, L0_tok_W1, L0_tok_b1, L0_tok_W2, L0_tok_b2)
    h = h + _L0_attn_ref(_layernorm(h, axis=-1), L0_attn_ln_w, L0_attn_ln_b, L0_attn_W_in, L0_attn_conv_w, L0_attn_conv_b, L0_attn_nu_log, L0_attn_theta_log, L0_attn_gamma_log, L0_attn_B_re, L0_attn_B_im, L0_attn_C_re, L0_attn_C_im, L0_attn_W_out, L0_attn_b_out)
    h = h + _L0_ffn_ref(_layernorm(h, axis=-1), L0_ffn_gate_w, L0_ffn_gate_b, L0_ffn_w1, L0_ffn_b1, L0_ffn_w2, L0_ffn_b2)
    return h

_drawn_inputs = setup_inputs


def setup_inputs(seed=0):
    import zlib

    import numpy as np

    out = dict(_drawn_inputs(seed))
    spreads = {'L0_tok_bq': (0.0, 2.0),
     'L0_tok_bk': (0.0, 2.0),
     'L0_tok_bv': (0.0, 0.1),
     'L0_tok_bo': (0.0, 0.1),
     'L0_tok_b1': (0.0, 0.1),
     'L0_tok_b2': (0.0, 0.1),
     'L0_attn_ln_w': (1.0, 0.2),
     'L0_attn_ln_b': (0.0, 0.1),
     'L0_attn_conv_b': (0.0, 0.1),
     'L0_attn_b_out': (0.0, 0.1)}
    factors = {'L0_tok_Wq': 200.0, 'L0_tok_Wk': 200.0, 'L0_ffn_b1': 4.899, 'L0_ffn_b2': 3.058}
    for name, (base, spread) in spreads.items():
        noise = np.random.default_rng([zlib.crc32(name.encode()), seed]).standard_normal(out[name].shape)
        drawn = base * np.exp(spread * noise) if base else spread * noise
        out[name] = jnp.asarray(drawn.astype(out[name].dtype))
    for name, factor in factors.items():
        out[name] = (out[name] * factor).astype(out[name].dtype)
    return out
```

```python
from contextlib import ExitStack

import concourse.bass as bass
from concourse import mybir

F32 = mybir.dt.float32
F32R = mybir.dt.float32r
I32 = mybir.dt.int32
U32 = mybir.dt.uint32
ALU = mybir.AluOpType
ACT = mybir.ActivationFunctionType
AX = mybir.AxisListType

P = 128
SEQ = 256
PAIR = 2 * SEQ
HEAD = 64
MASKED = -1.0e30
DMA = 16


class Pools:

    def __init__(self, nc, ctx, prefix):
        self.nc, self.ctx, self.prefix = nc, ctx, prefix

    def sbuf(self, name, shape, dtype=F32):
        return self.ctx.enter_context(self.nc.sbuf_tensor(f"{self.prefix}_{name}", shape, dtype))

    def bank(self, name):
        return self.ctx.enter_context(self.nc.psum_tensor(f"{self.prefix}_ps_{name}", [P, 512], F32))

    def sem(self, name):
        return self.ctx.enter_context(self.nc.semaphore(f"{self.prefix}_{name}"))


def settled(engine, value):
    return value if isinstance(value, int) else engine.to_reg(value)


def columns(tensor, start, count):
    return tensor[:, bass.ds(start, count)]


def embed_stage(nc, hT, ident, ids, emb, pos):
    vocab = emb.shape[0]
    n_tiles = ids.shape[0] * ids.shape[1] // P
    RING = 4
    with ExitStack() as ctx:
        pool = Pools(nc, ctx, "emb")
        ids_i = pool.sbuf("ids_i", [n_tiles, P], I32)
        ids_f = pool.sbuf("ids_f", [n_tiles, P])
        wrap = pool.sbuf("wrap", [n_tiles, P])
        index = pool.sbuf("index", [P, n_tiles], U32)
        index_now = [pool.sbuf(f"index_now{t}", [P, 1], U32) for t in range(RING)]
        rows = [pool.sbuf(f"rows{t}", [P, P]) for t in range(RING)]
        pos_rows = pool.sbuf("pos_rows", [P, 2, P])
        posT = pool.sbuf("posT", [P, SEQ])
        turned = [pool.bank(f"turned{t}") for t in range(RING)]
        setup_ps = pool.bank("setup_ps")
        pos_ps = pool.bank("pos_ps")

        ids_in = pool.sem("ids_in")
        pos_in = pool.sem("pos_in")
        ident_made = pool.sem("ident_made")
        ids_ready = pool.sem("ids_ready")
        setup_turned = pool.sem("setup_turned")
        setup_copied = pool.sem("setup_copied")
        index_copied = pool.sem("index_copied")
        gathered = [pool.sem(f"gathered{t}") for t in range(RING)]
        rows_turned = pool.sem("rows_turned")
        bank_free = pool.sem("bank_free")
        block = ctx.enter_context(nc.Block())

        @block.sync
        def _(sp):
            sp.dma_start(ids_i[:, :], ids.rearrange("b (t p) -> (b t) p", p=P)).then_inc(ids_in, DMA)
            sp.dma_start(pos_rows[:, :, :], pos[0:SEQ, :].rearrange("(t p) d -> p t d", p=P)).then_inc(pos_in, DMA)

        @block.gpsimd
        def _(pool_e):
            pool_e.memset(ident[:, :], 0.0).then_inc(ident_made, 1)
            pool_e.wait_ge(ident_made, 1)
            pool_e.affine_select(out=ident[:, :], in_=ident[:, :], compare_op=ALU.not_equal, fill=1.0,
                                 base=0, pattern=[[-1, P]], channel_multiplier=1).then_inc(ident_made, 1)
            pool_e.wait_ge(setup_copied, 1)
            with pool_e.Fori(0, n_tiles // RING) as i:
                for t in range(RING):
                    pool_e.wait_ge(rows_turned, i * RING + (t + 1))
                    pool_e.tensor_copy(index_now[t][:, :], columns(index, i * RING + t, 1)).then_inc(index_copied, 1)
                    count = settled(pool_e, i * RING + (t + 1))
                    pool_e.wait_ge(ident_made, 2)
                    pool_e.wait_ge(index_copied, count)
                    pool_e.indirect_dma_start(
                        rows[t][:, :], None, emb,
                        bass.IndirectOffsetOnAxis(ap=index_now[t][:, 0:1], axis=0)).then_inc(gathered[t], DMA)

        @block.vector
        def _(dve):
            step = [0]

            def chained(instruction):
                step[0] += 1
                instruction.then_inc(ids_ready, 1)
                dve.wait_ge(ids_ready, step[0])

            dve.wait_ge(ids_in, DMA)
            chained(dve.tensor_copy(ids_f[:, :], ids_i[:, :]))
            chained(dve.tensor_scalar(wrap[:, :], ids_f[:, :], 0.0, float(vocab), ALU.is_lt, ALU.mult))
            chained(dve.tensor_tensor(ids_f[:, :], ids_f[:, :], wrap[:, :], ALU.add))
            dve.tensor_scalar(ids_f[:, :], ids_f[:, :], 0.0, float(vocab - 1), ALU.max, ALU.min).then_inc(ids_ready, 1)
            dve.wait_ge(setup_turned, 1)
            dve.tensor_copy(index[:, :], setup_ps[:, 0:n_tiles]).then_inc(setup_copied, 1)
            dve.wait_ge(setup_turned, 2)
            dve.tensor_copy(posT[:, :], pos_ps[:, 0:SEQ]).then_inc(setup_copied, 1)
            dve.wait_ge(setup_copied, 2)
            with dve.Fori(0, n_tiles // RING) as i:
                for t in range(RING):
                    dve.wait_ge(rows_turned, i * RING + (t + 1 + RING))
                    half = t % 2 * P
                    dve.tensor_tensor(columns(hT, i * (RING * P) + t * P, P), turned[t][:, 0:P],
                                      posT[:, half:half + P], ALU.add).then_inc(bank_free, 1)

        @block.tensor
        def _(pe):
            pe.wait_ge(ident_made, 2)
            pe.wait_ge(ids_ready, 4)
            pe.transpose(setup_ps[:, 0:n_tiles], ids_f[:, :], ident[0:n_tiles, 0:n_tiles]).then_inc(setup_turned, 1)
            pe.wait_ge(pos_in, DMA)
            pe.transpose(pos_ps[:, 0:P], pos_rows[:, 0, :], ident[:, :])
            pe.transpose(pos_ps[:, P:2 * P], pos_rows[:, 1, :], ident[:, :]).then_inc(setup_turned, 1)
            pe.transpose(turned[0][:, 0:P], ident[:, :], ident[:, :]).then_inc(rows_turned, RING)
            pe.transpose(turned[1][:, 0:P], ident[:, :], ident[:, :]).then_inc(bank_free, RING)
            with pe.Fori(0, n_tiles // RING) as i:
                for t in range(RING):
                    pe.wait_ge(gathered[t], i * DMA + DMA)
                    pe.wait_ge(bank_free, i * RING + (t + 1))
                    pe.transpose(turned[t][:, 0:P], rows[t][:, :], ident[:, :]).then_inc(rows_turned, 1)


def layers_stage(nc, hT, ident, weights):
    Wq, bq, Wk, bk, Wv, bv, Wo, bo, W1, b1, W2, b2 = weights
    L, _, HK = Wq.shape
    FF = W1.shape[2]
    PAIRS = hT.shape[1] // PAIR
    JS = HK // P
    FS = FF // P
    UNITS = 2 * JS
    assert UNITS == 8 and FS == 4 and PAIRS % 2 == 0 and PAIRS >= 4
    SCALE = -float(HEAD) ** -0.5

    PROJ = [("k", 0), ("q", 0), ("k", 1), ("q", 1), ("k", 2), ("q", 2), ("k", 3), ("q", 3),
            ("v", 0), ("v", 1), ("v", 2), ("v", 3)]
    FEED = [("f", f) for f in range(FS)]
    SLOTS = {0: PROJ[0:2], 1: PROJ[2:4], 2: PROJ[4:6], 3: PROJ[6:8], 4: PROJ[8:10],
             5: FEED[0:2], 6: FEED[2:4], 7: PROJ[10:12]}
    EARLY = 10
    PER_PAIR = len(PROJ) + FS
    PER_LAYER = PAIRS * PER_PAIR

    def piece_base(layer, i):
        if isinstance(i, int) and i == 0:
            return layer * (PER_LAYER // 2) + len(PROJ) // 2
        return layer * (PER_LAYER // 2) + i * (PER_PAIR // 2) + (len(PROJ) - PER_PAIR // 2)

    def position(kind, has_prev):
        if kind[0] == "f":
            return EARLY + kind[1]
        at = PROJ.index(kind)
        return at + (FS if has_prev and at >= EARLY else 0)

    with ExitStack() as ctx:
        pool = Pools(nc, ctx, "lay")
        raw = {n: pool.sbuf(f"raw_{n}", [P, HK]) for n in ("q", "k", "v", "1", "o", "2")}
        w_hi = {n: pool.sbuf(f"w_hi_{n}", [P, HK], F32R) for n in ("q", "k", "v", "1")}
        w_lo = {n: pool.sbuf(f"w_lo_{n}", [P, HK], F32R) for n in ("q", "k", "v", "1")}
        w_whole = {n: pool.sbuf(f"w_{n}", [P, HK]) for n in ("o", "2")}
        N_BIAS = 4 * JS * L + 2 * L
        bias_rows = pool.sbuf("bias_rows", [N_BIAS, P])
        biasT = pool.sbuf("biasT", [P, N_BIAS])
        bias4 = pool.sbuf("bias4", [P, 4, JS])
        bias2 = pool.sbuf("bias2", [P, 2])
        bias_o = pool.sbuf("bias_o", [P, 1])
        mask = pool.sbuf("mask", [P, 2 * P])
        h_hi = [pool.sbuf(f"h_hi{p}", [P, PAIR], F32R) for p in range(2)]
        h_lo = [pool.sbuf(f"h_lo{p}", [P, PAIR], F32R) for p in range(2)]
        Q = [pool.sbuf(f"Q{p}", [P, JS, PAIR]) for p in range(2)]
        K = [[pool.sbuf(f"K{p}{h}", [P, JS, PAIR]) for h in range(2)] for p in range(2)]
        V = [[pool.sbuf(f"V{p}{t}", [P, HK]) for t in range(4)] for p in range(2)]
        probs = [pool.sbuf(f"probs{p}", [P, 6 * P]) for p in range(2)]
        least = [pool.sbuf(f"least{p}", [P, 4]) for p in range(2)]
        sums = [pool.sbuf(f"sums{p}", [P, 4]) for p in range(2)]
        inverse = [pool.sbuf(f"inverse{p}", [P, 4]) for p in range(2)]
        probsT = [pool.sbuf(f"probsT{p}", [P, 6 * P]) for p in range(2)]
        O = pool.sbuf("O", [P, JS, PAIR])
        c_hi = pool.sbuf("c_hi", [P, PAIR], F32R)
        c_lo = pool.sbuf("c_lo", [P, PAIR], F32R)
        hidden = pool.sbuf("hidden", [P, FS, PAIR])

        score_ps = [pool.bank(f"score{b}") for b in range(2)]
        turn_ps = [pool.bank(f"turn{b}") for b in range(2)]
        head_ps = pool.bank("head")
        piece_ps = [pool.bank(f"piece{b}") for b in range(2)]
        sum_ps = pool.bank("sum")

        bias_in = pool.sem("bias_in")
        zeroed = pool.sem("zeroed")
        K_zeroed = pool.sem("K_zeroed")
        bias_turned = pool.sem("bias_turned")
        setup_done = pool.sem("setup_done")
        weights_in = pool.sem("weights_in")
        weights_split = pool.sem("weights_split")
        weights_moved = pool.sem("weights_moved")
        hi_made = pool.sem("hi_made")
        bias_done = pool.sem("bias_done")
        bias_o_ps = pool.sem("bias_o_ps")
        h_hi_made = pool.sem("h_hi_made")
        h_lo_made = pool.sem("h_lo_made")
        pieces = pool.sem("pieces")
        piece_free = [pool.sem(f"piece_free{b}") for b in range(2)]
        scored = pool.sem("scored")
        masked = pool.sem("masked")
        exped = pool.sem("exped")
        inverted = pool.sem("inverted")
        normed = pool.sem("normed")
        turned = pool.sem("turned")
        turned_out = [pool.sem(f"turned_out{b}") for b in range(2)]
        headed = pool.sem("headed")
        O_made = pool.sem("O_made")
        projected = pool.sem("projected")
        h1_made = pool.sem("h1_made")
        c_hi_made = pool.sem("c_hi_made")
        c_lo_made = pool.sem("c_lo_made")
        fed = pool.sem("fed")
        h2_made = pool.sem("h2_made")
        block = ctx.enter_context(nc.Block())

        def wait_piece(eng, base, at):
            eng.wait_ge(pieces, base * 2 + (at + 1))

        def wait_copied(eng, base, at):
            eng.wait_ge(piece_free[at % 2], base + (at // 2 + 1))

        def wait_projection(eng, layer, i, kind):
            if isinstance(i, int) and i == 0:
                wait_copied(eng, layer * (PER_LAYER // 2), PROJ.index(kind))
            elif isinstance(i, int) and i == 1:
                wait_copied(eng, piece_base(layer, 0), position(kind, False))
            else:
                wait_copied(eng, piece_base(layer, i - 1), position(kind, True))

        def each_pair(eng, layer, pair):
            pair(0, 0)
            pair(1, 1)
            with eng.Fori(1, PAIRS // 2 - 1) as r:
                pair(r * 2, 0)
                pair(r * 2 + 1, 1)
            pair(PAIRS - 2, 0)
            pair(PAIRS - 1, 1)

        def is_pair(i, which):
            return isinstance(i, int) and i == which

        PARTS = [(0, 2 * P), (2 * P, 4 * P), (4 * P, 5 * P), (5 * P, 6 * P)]

        @block.sync
        def _(sp):
            n = JS * L
            for at, b in enumerate((bq, bk, bv, b1)):
                sp.dma_start(bias_rows[at * n:(at + 1) * n, :],
                             b.rearrange("l (j p) -> (l j) p", p=P)).then_inc(bias_in, DMA)
            for at, b in enumerate((bo, b2)):
                sp.dma_start(bias_rows[4 * n + at * L:4 * n + (at + 1) * L, :], b).then_inc(bias_in, DMA)
            with sp.Fori(0, L) as layer:
                sp.wait_ge(weights_split, layer + 1)
                sp.wait_ge(weights_moved, layer + 1)
                for name, w in (("q", Wq), ("k", Wk), ("v", Wv), ("1", W1)):
                    sp.dma_start(raw[name][:, :], w[bass.ds(layer, 1), :, :].rearrange("l p n -> p (l n)"))\
                      .then_inc(weights_in, DMA)
                for name, w in (("o", Wo), ("2", W2)):
                    sp.dma_start(raw[name][:, :].rearrange("p (j d) -> p j d", d=P),
                                 w[bass.ds(layer, 1), :, :].rearrange("l (j p) d -> p (l j) d", p=P))\
                      .then_inc(weights_in, DMA)

        @block.gpsimd
        def _(gp):
            gp.memset(mask[:, :], 0.0).then_inc(zeroed, 1)
            gp.wait_ge(zeroed, 1)
            gp.affine_select(out=mask[:, P:2 * P], in_=mask[:, P:2 * P], compare_op=ALU.is_ge,
                             fill=MASKED, base=0, pattern=[[-1, P]], channel_multiplier=1).then_inc(zeroed, 1)
            with gp.Fori(0, L) as layer:
                with gp.Fori(0, PAIRS) as i:
                    unit = layer * (PAIRS * UNITS) + i * UNITS
                    for k in range(UNITS):
                        count = settled(gp, unit + (k + 1))
                        gp.wait_ge(zeroed, 2)
                        gp.wait_ge(inverted, count)
                        for q, (a, b) in enumerate(PARTS):
                            gp.tensor_scalar(probs[k % 2][:, a:b], probs[k % 2][:, a:b],
                                             inverse[k % 2][:, q:q + 1], 1.0, ALU.mult, ALU.mult)\
                              .then_inc(normed, 1)

        @block.tensor
        def _(pe):
            def three_passes(out, lhs_hi, lhs_lo, rhs_hi, rhs_lo):
                pe.matmul(out, lhs_hi, rhs_hi, start=True, stop=False)
                pe.matmul(out, lhs_hi, rhs_lo, start=False, stop=False)
                return pe.matmul(out, lhs_lo, rhs_hi, start=False, stop=True)

            def piece(kind, at, base, parity, first=False):
                if not first:
                    pe.wait_ge(piece_free[at % 2], base + at // 2)
                bank = piece_ps[at % 2][:, :]
                name, n = kind
                if name == "v":
                    cols = slice(n * P, (n + 1) * P)
                    last = three_passes(bank, h_hi[parity][:, cols], h_lo[parity][:, cols],
                                        w_hi["v"][:, :], w_lo["v"][:, :])
                else:
                    cols = slice(n * P, (n + 1) * P)
                    hi, lo = (c_hi, c_lo) if name == "f" else (h_hi[parity], h_lo[parity])
                    w = "1" if name == "f" else name
                    last = three_passes(bank, w_hi[w][:, cols], w_lo[w][:, cols], hi[:, :], lo[:, :])
                last.then_inc(pieces, 1)

            def scores(layer, i, k, parity):
                j, s = k // 2, k % 2 * SEQ
                unit = layer * (PAIRS * UNITS) + i * UNITS + k
                if s == 0:
                    wait_projection(pe, layer, i, ("k", j))
                    wait_projection(pe, layer, i, ("q", j))
                if not (is_pair(i, 0) and k == 0):
                    pe.wait_ge(masked, unit * 4)
                early, late = Q[parity][:, j, s:s + P], Q[parity][:, j, s + P:s + SEQ]
                for h in range(2):
                    pe_last = pe.matmul(score_ps[0][:, h * SEQ:(h + 1) * SEQ], late,
                                        K[parity][h][:, j, s:s + SEQ], start=True, stop=True)
                pe_last.then_inc(scored, 1)
                for h in range(2):
                    pe_last = pe.matmul(score_ps[1][:, h * P:(h + 1) * P], early,
                                        K[parity][h][:, j, s:s + P], start=True, stop=True)
                pe_last.then_inc(scored, 1)

            def turn(layer, i, k):
                unit = layer * (PAIRS * UNITS) + i * UNITS + k
                own = probs[k % 2]
                pe.wait_ge(normed, unit * 4 + 2)
                if not (is_pair(i, 0) and k == 0):
                    pe.wait_ge(turned_out[1], unit)
                for h in range(2):
                    last = pe.transpose(turn_ps[1][:, h * P:(h + 1) * P],
                                        own[:, h * SEQ + P:(h + 1) * SEQ], ident[:, :])
                last.then_inc(turned, 1)
                if not (is_pair(i, 0) and k == 0):
                    pe.wait_ge(turned_out[0], unit)
                for h in range(2):
                    pe.transpose(turn_ps[0][:, h * SEQ + P:(h + 1) * SEQ],
                                 own[:, h * SEQ:h * SEQ + P], ident[:, :])
                pe.wait_ge(normed, unit * 4 + 4)
                for h in range(2):
                    last = pe.transpose(turn_ps[0][:, h * SEQ:h * SEQ + P],
                                        own[:, (4 + h) * P:(5 + h) * P], ident[:, :])
                last.then_inc(turned, 1)

            def values(layer, i, k, parity):
                j, s = k // 2, k % 2
                unit = layer * (PAIRS * UNITS) + i * UNITS + k
                if k < 2:
                    wait_projection(pe, layer, i, ("v", 2 * s))
                    wait_projection(pe, layer, i, ("v", 2 * s + 1))
                if s == 0 and not (is_pair(i, 0) and k == 0):
                    pe.wait_ge(O_made, layer * (PAIRS * JS) + i * JS + j)
                pe.wait_ge(turned_out[1], unit + 1)
                pe.wait_ge(turned_out[0], unit + 1)
                PT = probsT[k % 2]
                at = s * SEQ
                for h in range(2):
                    cols = slice((2 * j + h) * HEAD, (2 * j + h + 1) * HEAD)
                    pe.matmul(head_ps[h * HEAD:(h + 1) * HEAD, at:at + SEQ], V[parity][2 * s][:, cols],
                              PT[:, h * SEQ:(h + 1) * SEQ], start=True, stop=False)
                for h in range(2):
                    cols = slice((2 * j + h) * HEAD, (2 * j + h + 1) * HEAD)
                    last = pe.matmul(head_ps[h * HEAD:(h + 1) * HEAD, at + P:at + SEQ],
                                     V[parity][2 * s + 1][:, cols], PT[:, (4 + h) * P:(5 + h) * P],
                                     start=False, stop=True)
                if s == 1:
                    last.then_inc(headed, 1)

            def output_projection(layer, i, js):
                for j in js:
                    if j == 0:
                        if is_pair(i, 0):
                            pe.wait_ge(bias_done, layer * 2 + 2)
                        else:
                            pe.wait_ge(h2_made, layer * PAIRS + i + PAIRS)
                    pe.wait_ge(O_made, layer * (PAIRS * JS) + i * JS + (j + 1))
                    last = pe.matmul(sum_ps[:, :], w_whole["o"][:, j * P:(j + 1) * P], O[:, j, :],
                                     start=(j == 0), stop=(j == JS - 1))
                if js[-1] == JS - 1:
                    last.then_inc(projected, 1)

            def feed_sum(layer, i, fs, base, has_prev=True):
                for f in fs:
                    if f == 0:
                        pe.wait_ge(h1_made, layer * PAIRS + i + 1)
                    wait_copied(pe, base, position(("f", f), True) if has_prev else f)
                    last = pe.matmul(sum_ps[:, :], w_whole["2"][:, f * P:(f + 1) * P], hidden[:, f, :],
                                     start=(f == 0), stop=(f == FS - 1))
                if fs[-1] == FS - 1:
                    last.then_inc(fed, 1)

            def wait_c(layer, i):
                pe.wait_ge(c_hi_made, layer * PAIRS + i + 1)
                pe.wait_ge(c_lo_made, layer * PAIRS + i + 1)

            def wait_h(layer, i):
                pe.wait_ge(h_hi_made, layer * PAIRS + i + 1)
                pe.wait_ge(h_lo_made, layer * PAIRS + i + 1)

            pe.wait_ge(bias_in, 6 * DMA)
            pe.transpose(sum_ps[:, 0:N_BIAS], bias_rows[:, :], ident[0:N_BIAS, 0:N_BIAS]).then_inc(bias_turned, 1)
            pe.wait_ge(K_zeroed, 4)
            with pe.Fori(0, L) as layer:
                pe.wait_ge(weights_split, layer + 2)
                pe.wait_ge(weights_moved, layer + 2)
                pe.wait_ge(bias_done, layer * 2 + 1)
                for j in range(JS):
                    last = pe.matmul(sum_ps[:, 0:1], w_whole["o"][:, j * P:(j + 1) * P], bias4[:, 2, j:j + 1],
                                     start=(j == 0), stop=(j == JS - 1))
                last.then_inc(bias_o_ps, 1)
                wait_h(layer, 0)
                for at, kind in enumerate(PROJ):
                    piece(kind, at, layer * (PER_LAYER // 2), 0, first=at < 2)

                def pair(i, parity):
                    has_prev = not is_pair(i, 0)
                    has_next = not is_pair(i, PAIRS - 1)
                    base = piece_base(layer, i)
                    at = 0
                    if has_next:
                        wait_h(layer, i + 1)
                    for k in range(UNITS):
                        run = [x for x in SLOTS[k] if (x[0] == "f" and has_prev) or (x[0] != "f" and has_next)]
                        if run and run[0] == FEED[0]:
                            wait_c(layer, i - 1)
                        scores(layer, i, k, parity)
                        if run:
                            piece(run[0], at, base, 1 - parity)
                            at += 1
                        if k > 0:
                            turn(layer, i, k - 1)
                        elif has_prev:
                            turn(layer, i - 1, UNITS - 1)
                        if has_prev:
                            if k in (2, 3):
                                output_projection(layer, i - 1, [2 * (k - 2), 2 * (k - 2) + 1])
                            if k in (6, 7):
                                feed_sum_at = base if has_next else base - EARLY // 2
                                feed_sum(layer, i - 1, [2 * (k - 6), 2 * (k - 6) + 1], feed_sum_at)
                        if k >= 2:
                            values(layer, i, k - 2, parity)
                        elif has_prev:
                            values(layer, i - 1, UNITS - 2 + k, 1 - parity)
                        if run:
                            piece(run[1], at, base, 1 - parity)
                            at += 1

                each_pair(pe, layer, pair)
                last_pair = PAIRS - 1
                turn(layer, last_pair, UNITS - 1)
                values(layer, last_pair, UNITS - 2, 1)
                values(layer, last_pair, UNITS - 1, 1)
                output_projection(layer, last_pair, list(range(JS)))
                wait_c(layer, last_pair)
                drain_base = piece_base(layer, last_pair) + FS // 2
                for f in range(FS):
                    piece(FEED[f], f, drain_base, 1)
                feed_sum(layer, last_pair, list(range(FS)), drain_base, has_prev=False)

        def feed_piece(eng, layer, f, at, base):
            wait_piece(eng, base, at)
            return piece_ps[at % 2][:, :], bias4[:, 3, f:f + 1]

        @block.vector
        def _(dve):
            def take_piece(kind, at, base, parity):
                name, n = kind
                bank = piece_ps[at % 2]
                if name == "k":
                    wait_piece(dve, base, at)
                    dve.tensor_scalar(K[parity][0][0:HEAD, n, :], bank[0:HEAD, :], bias4[0:HEAD, 1, n:n + 1],
                                      None, ALU.add)
                    dve.tensor_scalar(K[parity][1][HEAD:P, n, :], bank[HEAD:P, :], bias4[HEAD:P, 1, n:n + 1],
                                      None, ALU.add).then_inc(piece_free[at % 2], 1)
                elif kind == ("v", 3):
                    wait_piece(dve, base, at)
                    dve.tensor_copy(V[parity][n][:, :], bank[:, :]).then_inc(piece_free[at % 2], 1)
                elif name == "f" and n % 2 == 1:
                    wait_piece(dve, base, at)
                    dve.tensor_scalar(hidden[:, n, :], bank[:, :], bias4[:, 3, n:n + 1], 0.0, ALU.add, ALU.max)\
                       .then_inc(piece_free[at % 2], 1)

            def mask_scores(layer, i, k):
                unit = layer * (PAIRS * UNITS) + i * UNITS + k
                for q, (a, b) in enumerate(PARTS):
                    if q % 2 == 0:
                        count = settled(dve, unit * 2 + (q // 2 + 1))
                        dve.wait_ge(zeroed, 2)
                        dve.wait_ge(scored, count)
                    bank = score_ps[q // 2]
                    width = b - a
                    own = q % 2 * width
                    dve.tensor_tensor_reduce(
                        out=probs[k % 2][:, a:b], in0=bank[:, own:own + width], in1=mask[:, 2 * P - width:2 * P],
                        scale=SCALE, scalar=3.0e38, op0=ALU.add, op1=ALU.min,
                        accum_out=least[k % 2][:, q:q + 1]).then_inc(masked, 1)

            def invert(layer, i, k):
                unit = layer * (PAIRS * UNITS) + i * UNITS + k
                dve.wait_ge(exped, unit * 4 + 4)
                dve.reciprocal(inverse[k % 2][:, :], sums[k % 2][:, :]).then_inc(inverted, 1)

            def take_turned(layer, i, k):
                unit = layer * (PAIRS * UNITS) + i * UNITS + k
                dve.wait_ge(turned, unit * 2 + 2)
                dve.tensor_copy(probsT[k % 2][:, 0:4 * P], turn_ps[0][:, :]).then_inc(turned_out[0], 1)

            def take_heads(layer, i, j):
                dve.wait_ge(headed, layer * (PAIRS * JS) + i * JS + (j + 1))
                dve.tensor_copy(O[:, j, :], head_ps[:, :]).then_inc(O_made, 1)

            def residual_1(layer, i):
                h = columns(hT, i * PAIR, PAIR)
                dve.wait_ge(projected, layer * PAIRS + i + 1)
                dve.scalar_tensor_tensor(out=h, in0=sum_ps[:, :], scalar=bias_o[:, 0:1], in1=h,
                                         op0=ALU.add, op1=ALU.add).then_inc(h1_made, 1)

            def split_c(layer, i):
                dve.wait_ge(c_hi_made, layer * PAIRS + i + 1)
                dve.tensor_tensor(c_lo[:, :], columns(hT, i * PAIR, PAIR), c_hi[:, :].bitcast(F32),
                                  ALU.subtract).then_inc(c_lo_made, 1)

            def residual_2(layer, i):
                h = columns(hT, i * PAIR, PAIR)
                dve.wait_ge(fed, layer * PAIRS + i + 1)
                dve.scalar_tensor_tensor(out=h, in0=sum_ps[:, :], scalar=bias2[:, 1:2], in1=h,
                                         op0=ALU.add, op1=ALU.add).then_inc(h2_made, 1)

            def split_h(layer, i, parity):
                dve.wait_ge(h_hi_made, layer * PAIRS + i + 1)
                dve.tensor_tensor(h_lo[parity][:, :], columns(hT, i * PAIR, PAIR),
                                  h_hi[parity][:, :].bitcast(F32), ALU.subtract).then_inc(h_lo_made, 1)

            for p in range(2):
                dve.memset(K[p][0][HEAD:P, :, :], 0.0).then_inc(K_zeroed, 1)
                dve.memset(K[p][1][0:HEAD, :, :], 0.0).then_inc(K_zeroed, 1)
            dve.wait_ge(K_zeroed, 4)
            dve.wait_ge(zeroed, 2)
            dve.wait_ge(bias_turned, 1)
            dve.tensor_copy(biasT[:, :], sum_ps[:, 0:N_BIAS]).then_inc(setup_done, 1)
            dve.memset(bias_o[:, :], 0.0).then_inc(h2_made, PAIRS)
            dve.memset(least[0][:, :], 0.0).then_inc(weights_split, 1)
            dve.wait_ge(setup_done, 1)
            with dve.Fori(0, L) as layer:
                n = JS * L
                dve.wait_ge(h2_made, layer * PAIRS + PAIRS)
                by_kind = biasT[:, 0:4 * n].rearrange("p (t n) -> p t n", t=4)
                dve.tensor_copy(bias4[:, :, :], by_kind[:, :, bass.ds(layer * JS, JS)])
                ends = biasT[:, 4 * n:N_BIAS].rearrange("p (t l) -> p t l", t=2)
                dve.tensor_copy(bias2[:, :], ends[:, :, bass.ds(layer, 1)].rearrange("p t l -> p (t l)"))\
                   .then_inc(bias_done, 1)
                dve.wait_ge(bias_done, layer * 2 + 1)
                dve.wait_ge(weights_in, layer * (6 * DMA) + 6 * DMA)
                for m, name in enumerate(w_hi):
                    dve.tensor_copy(w_hi[name][:, :], raw[name][:, :]).then_inc(hi_made, 1)
                for m, name in enumerate(w_hi):
                    dve.wait_ge(hi_made, layer * 4 + (m + 1))
                    last = dve.tensor_tensor(w_lo[name][:, :], raw[name][:, :], w_hi[name][:, :].bitcast(F32),
                                             ALU.subtract)
                last.then_inc(weights_split, 1)
                for i in range(2):
                    split_h(layer, i, i)
                dve.wait_ge(bias_o_ps, layer + 1)
                dve.tensor_scalar(bias_o[:, :], sum_ps[:, 0:1], bias2[:, 0:1], None, ALU.add).then_inc(bias_done, 1)
                dve.wait_ge(bias_done, layer * 2 + 2)
                for at, kind in enumerate(PROJ):
                    take_piece(kind, at, layer * (PER_LAYER // 2), 0)

                def pair(i, parity):
                    has_prev = not is_pair(i, 0)
                    has_next = not is_pair(i, PAIRS - 1)
                    base = piece_base(layer, i)
                    at = 0
                    for k in range(UNITS):
                        run = [x for x in SLOTS[k] if (x[0] == "f" and has_prev) or (x[0] != "f" and has_next)]
                        mask_scores(layer, i, k)
                        if run:
                            take_piece(run[0], at, base, 1 - parity)
                            at += 1
                        if k > 0:
                            take_turned(layer, i, k - 1)
                        elif has_prev:
                            take_turned(layer, i - 1, UNITS - 1)
                        invert(layer, i, k)
                        if k == 3 and has_prev:
                            residual_1(layer, i - 1)
                        if k == 4 and has_prev:
                            split_c(layer, i - 1)
                        if k == 5 and not is_pair(i, PAIRS - 1) and not is_pair(i, PAIRS - 2):
                            split_h(layer, i + 2, parity)
                        if k % 2 == 1:
                            if k >= 3:
                                take_heads(layer, i, (k - 3) // 2)
                            elif has_prev:
                                take_heads(layer, i - 1, JS - 1)
                        if run:
                            take_piece(run[1], at, base, 1 - parity)
                            at += 1
                        if k == 7 and has_prev:
                            residual_2(layer, i - 1)

                each_pair(dve, layer, pair)
                last_pair = PAIRS - 1
                take_turned(layer, last_pair, UNITS - 1)
                take_heads(layer, last_pair, JS - 1)
                residual_1(layer, last_pair)
                split_c(layer, last_pair)
                drain_base = piece_base(layer, last_pair) + FS // 2
                for f in range(FS):
                    take_piece(FEED[f], f, drain_base, 1)
                residual_2(layer, last_pair)

        @block.scalar
        def _(act):
            def take_piece(kind, at, base, parity):
                name, n = kind
                bank = piece_ps[at % 2]
                if name == "q":
                    wait_piece(act, base, at)
                    act.activation(Q[parity][:, n, :], bank[:, :], ACT.Identity, bias=bias4[:, 0, n:n + 1])\
                       .then_inc(piece_free[at % 2], 1)
                elif name == "v" and n < 3:
                    wait_piece(act, base, at)
                    act.activation(V[parity][n][:, :], bank[:, :], ACT.Copy).then_inc(piece_free[at % 2], 1)
                elif name == "f" and n % 2 == 0:
                    wait_piece(act, base, at)
                    act.activation(hidden[:, n, :], bank[:, :], ACT.Relu, bias=bias4[:, 3, n:n + 1])\
                       .then_inc(piece_free[at % 2], 1)

            def exponentials(layer, i, k):
                unit = layer * (PAIRS * UNITS) + i * UNITS + k
                for q, (a, b) in enumerate(PARTS):
                    act.wait_ge(masked, unit * 4 + (q + 1))
                    own = probs[k % 2][:, a:b]
                    act.activation(own, own, ACT.Exp, bias=least[k % 2][:, q:q + 1], scale=-1.0,
                                   accum_out=sums[k % 2][:, q:q + 1]).then_inc(exped, 1)

            def take_turned(layer, i, k):
                unit = layer * (PAIRS * UNITS) + i * UNITS + k
                act.wait_ge(turned, unit * 2 + 1)
                act.activation(probsT[k % 2][:, 4 * P:6 * P], turn_ps[1][:, 0:2 * P], ACT.Copy)\
                   .then_inc(turned_out[1], 1)

            def split_c(layer, i):
                act.wait_ge(h1_made, layer * PAIRS + i + 1)
                act.activation(c_hi[:, :], columns(hT, i * PAIR, PAIR), ACT.Copy).then_inc(c_hi_made, 1)

            def split_h(layer, i, parity):
                act.wait_ge(h2_made, layer * PAIRS + i + 1)
                act.activation(h_hi[parity][:, :], columns(hT, i * PAIR, PAIR), ACT.Copy).then_inc(h_hi_made, 1)

            act.activation(sums[0][:, :], ident[:, 0:4], ACT.Copy).then_inc(weights_moved, 1)
            with act.Fori(0, L) as layer:
                act.wait_ge(weights_in, layer * (6 * DMA) + 6 * DMA)
                act.wait_ge(h2_made, layer * PAIRS + PAIRS)
                act.activation(w_whole["o"][:, :], raw["o"][:, :], ACT.Copy)
                act.activation(w_whole["2"][:, :], raw["2"][:, :], ACT.Copy).then_inc(weights_moved, 1)
                for i in range(2):
                    split_h(layer, i, i)
                act.wait_ge(bias_done, layer * 2 + 1)
                for at, kind in enumerate(PROJ):
                    take_piece(kind, at, layer * (PER_LAYER // 2), 0)

                def pair(i, parity):
                    has_prev = not is_pair(i, 0)
                    has_next = not is_pair(i, PAIRS - 1)
                    base = piece_base(layer, i)
                    at = 0
                    for k in range(UNITS):
                        run = [x for x in SLOTS[k] if (x[0] == "f" and has_prev) or (x[0] != "f" and has_next)]
                        if k == 4 and has_prev:
                            split_c(layer, i - 1)
                        exponentials(layer, i, k)
                        if run:
                            take_piece(run[0], at, base, 1 - parity)
                            at += 1
                        if k > 0:
                            take_turned(layer, i, k - 1)
                        elif has_prev:
                            take_turned(layer, i - 1, UNITS - 1)
                        if k == 4 and not is_pair(i, PAIRS - 1) and not is_pair(i, PAIRS - 2):
                            split_h(layer, i + 2, parity)
                        if run:
                            take_piece(run[1], at, base, 1 - parity)
                            at += 1

                each_pair(act, layer, pair)
                last_pair = PAIRS - 1
                take_turned(layer, last_pair, UNITS - 1)
                split_c(layer, last_pair)
                drain_base = piece_base(layer, last_pair) + FS // 2
                for f in range(FS):
                    take_piece(FEED[f], f, drain_base, 1)


class Skewed:

    def __init__(self, pairs, unroll, depth):
        self.pairs, self.unroll, self.depth = pairs, unroll, depth

    def run(self, eng, step):
        head = -(-self.depth // self.unroll) * self.unroll
        for i in range(head):
            step(i, i % self.unroll)
        with eng.Fori(head // self.unroll, self.pairs // self.unroll) as r:
            for u in range(self.unroll):
                step(r * self.unroll + u, u)
        for i in range(self.pairs, self.pairs + self.depth):
            step(i, i % self.unroll)

    def has(self, i, lag, back=0):
        return not isinstance(i, int) or back <= i - lag < self.pairs


def norm_stage(nc, prefix, hT, X, ident, eps, recurrent=None, gate=None):
    PAIRS = hT.shape[1] // PAIR
    T = PAIR // P
    NORMS = 2 if recurrent else 1
    skew = Skewed(PAIRS, 4, 4 if gate else 2)
    with ExitStack() as ctx:
        pool = Pools(nc, ctx, prefix)
        centre = pool.sbuf("centre", [P, P])
        mean = pool.sbuf("mean", [P, 1])
        ones = pool.sbuf("ones", [P, P])
        eps_of = [pool.sbuf(f"eps{n}", [P, 1]) for n in range(2)]
        c = [pool.sbuf(f"c{u}", [P, PAIR]) for u in range(4)]
        squared = [pool.sbuf(f"squared{p}", [P, PAIR]) for p in range(2)]
        root = [pool.sbuf(f"root{p}", [P, 2 * T]) for p in range(2)]
        inverse = [pool.sbuf(f"inverse{p}", [P, 2 * T]) for p in range(2)]
        diag = [[pool.sbuf(f"diag{n}{p}", [P, PAIR]) for p in range(2)] for n in range(NORMS)]
        x1 = [pool.sbuf(f"x1{p}", [P, PAIR]) for p in range(2)]
        x2 = [pool.sbuf(f"x2{p}", [P, PAIR]) for p in range(2)]
        c_ps = [pool.bank(f"c{p}") for p in range(2)]
        v_ps = [pool.bank(f"v{p}") for p in range(2)]
        spread_ps = [pool.bank(f"spread{n}") for n in range(NORMS)]
        made = pool.sem("made")
        vectors_in = pool.sem("vectors_in")
        centred = pool.sem("centred")
        c_out = pool.sem("c_out")
        squares = pool.sem("squares")
        varied = pool.sem("varied")
        roots = pool.sem("roots")
        inverses = pool.sem("inverses")
        diagonal = [pool.sem(f"diagonal{n}") for n in range(NORMS)]
        spread = [pool.sem(f"spread{n}") for n in range(NORMS)]
        x_made = [pool.sem(f"x_made{n}") for n in range(NORMS)]
        h_added = pool.sem("h_added")
        X_made = pool.sem("X_made")
        if recurrent:
            w_dram, b_dram = recurrent
            w_col = pool.sbuf("w_col", [P, 1])
            b_col = pool.sbuf("b_col", [P, 1])
        if gate:
            gate_w, gate_b, logits = gate
            E = gate_w.shape[1]
            gate_sb = pool.sbuf("gate_sb", [P, E])
            gate_col = pool.sbuf("gate_col", [E, 1])
            rowed = [pool.sbuf(f"rowed{p}", [E, PAIR]) for p in range(2)]
            l_ps = pool.bank("l")
            t_ps = pool.bank("t")
            l_made = pool.sem("l_made")
            l_out = pool.sem("l_out")
            t_made = pool.sem("t_made")
            t_out = pool.sem("t_out")
        block = ctx.enter_context(nc.Block())

        @block.sync
        def _(sp):
            if recurrent:
                sp.dma_start(w_col[:, :], w_dram.rearrange("(p o) -> p o", o=1)).then_inc(vectors_in, DMA)
                sp.dma_start(b_col[:, :], b_dram.rearrange("(p o) -> p o", o=1)).then_inc(vectors_in, DMA)
            if gate:
                sp.dma_start(gate_sb[:, :], gate_w).then_inc(vectors_in, DMA)
                sp.dma_start(gate_col[:, :], gate_b.rearrange("(p o) -> p o", o=1)).then_inc(vectors_in, DMA)

        @block.gpsimd
        def _(gp):
            if recurrent:
                def step(i, u):
                    if skew.has(i, 2):
                        gp.wait_ge(x_made[0], i - 1)
                        h = columns(hT, (i - 2) * PAIR, PAIR)
                        gp.tensor_tensor(h, h, x1[u % 2][:, :], ALU.add).then_inc(h_added, 1)

                skew.run(gp, step)

        @block.tensor
        def _(pe):
            pe.wait_ge(made, 5)
            pe.wait_ge(vectors_in, 2 * DMA)

            def step(i, u):
                p = u % 2
                if skew.has(i, 0):
                    if skew.has(i, 0, 2):
                        pe.wait_ge(c_out, i - 1)
                    pe.matmul(c_ps[p][:, :], centre[:, :], columns(hT, i * PAIR, PAIR),
                              start=True, stop=True).then_inc(centred, 1)
                if skew.has(i, 2):
                    for n in range(NORMS):
                        if skew.has(i, 2, 1):
                            pe.wait_ge(x_made[n], i - 2)
                        pe.wait_ge(diagonal[n], i - 1)
                        pe.matmul(spread_ps[n][:, :], ones[:, :], diag[n][p][:, :],
                                  start=True, stop=True).then_inc(spread[n], 1)
                if skew.has(i, 1):
                    if skew.has(i, 1, 2):
                        pe.wait_ge(roots, i - 2)
                    pe.wait_ge(squares, i)
                    for t in range(T):
                        last = pe.matmul(v_ps[1 - p][:, t:t + 1], squared[1 - p][:, t * P:(t + 1) * P],
                                         mean[:, :], start=True, stop=True)
                    last.then_inc(varied, 1)
                if gate and skew.has(i, 3):
                    if skew.has(i, 3, 1):
                        pe.wait_ge(l_out, i - 3)
                    pe.wait_ge(x_made[0], i - 2)
                    pe.matmul(l_ps[0:E, :], gate_sb[:, :], columns(X, (i - 3) * PAIR, PAIR),
                              start=True, stop=True).then_inc(l_made, 1)
                if gate and skew.has(i, 4):
                    count = settled(pe, i - 3)
                    count_out = settled(pe, i - 4)
                    pe.wait_ge(vectors_in, 2 * DMA)
                    if skew.has(i, 4, 1):
                        pe.wait_ge(t_out, count_out)
                    pe.wait_ge(l_out, count)
                    for t in range(T):
                        last = pe.transpose(t_ps[:, t * E:(t + 1) * E], rowed[p][:, t * P:(t + 1) * P],
                                            ident[0:E, 0:E])
                    last.then_inc(t_made, 1)

            skew.run(pe, step)

        @block.vector
        def _(dve):
            dve.memset(mean[:, :], 1.0 / P).then_inc(made, 1)
            dve.memset(ones[:, :], 1.0).then_inc(made, 1)
            dve.memset(eps_of[0][:, :], eps).then_inc(made, 1)
            dve.memset(eps_of[1][:, :], eps * eps).then_inc(made, 1)
            dve.tensor_scalar(centre[:, :], ident[:, :], 1.0 / P, None, ALU.subtract).then_inc(made, 1)

            def step(i, u):
                p = u % 2
                if skew.has(i, 2):
                    x_to = [x1[p][:, :] if recurrent else columns(X, (i - 2) * PAIR, PAIR), x2[p][:, :]]
                    if recurrent and skew.has(i, 2, 2):
                        dve.wait_ge(h_added, i - 3)
                        dve.wait_ge(X_made, i - 3)
                    for n in range(NORMS):
                        dve.wait_ge(spread[n], i - 1)
                        dve.tensor_tensor(x_to[n], spread_ps[n][:, :], c[(u + 2) % 4][:, :], ALU.mult)\
                           .then_inc(x_made[n], 1)
                if skew.has(i, 0):
                    dve.wait_ge(centred, i + 1)
                    if skew.has(i, 0, 4):
                        dve.wait_ge(squares, i - 3)
                        for n in range(NORMS):
                            dve.wait_ge(x_made[n], i - 3)
                    dve.tensor_copy(c[u][:, :], c_ps[p][:, :]).then_inc(c_out, 1)
                if skew.has(i, 1):
                    dve.wait_ge(roots, i)
                    if skew.has(i, 1, 2):
                        for n in range(NORMS):
                            dve.wait_ge(diagonal[n], i - 2)
                    dve.reciprocal(inverse[1 - p][:, 0:NORMS * T], root[1 - p][:, 0:NORMS * T]).then_inc(inverses, 1)
                    dve.wait_ge(inverses, i)
                    if skew.has(i, 1, 2):
                        dve.wait_ge(spread[0], i - 2)
                    for t in range(T):
                        last = dve.tensor_scalar(diag[0][1 - p][:, t * P:(t + 1) * P], ident[:, :],
                                                 inverse[1 - p][:, t:t + 1], None, ALU.mult)
                    last.then_inc(diagonal[0], 1)
                if gate and skew.has(i, 4):
                    dve.wait_ge(t_made, i - 3)
                    dve.tensor_copy(logits[:, bass.ds((i - 4) * (T * E), T * E)], t_ps[:, 0:T * E])\
                       .then_inc(t_out, 1)

            skew.run(dve, step)

        @block.scalar
        def _(act):
            act.wait_ge(made, 5)
            act.wait_ge(vectors_in, 2 * DMA)

            def step(i, u):
                p = u % 2
                if skew.has(i, 1):
                    act.wait_ge(varied, i)
                    if skew.has(i, 1, 2):
                        act.wait_ge(inverses, i - 2)
                    for n in range(NORMS):
                        last = act.activation(root[1 - p][:, n * T:(n + 1) * T], v_ps[1 - p][:, 0:T], ACT.Sqrt,
                                              bias=eps_of[n][:, :], scale=1.0 + n * eps)
                    last.then_inc(roots, 1)
                if skew.has(i, 0):
                    act.wait_ge(c_out, i + 1)
                    if skew.has(i, 0, 2):
                        act.wait_ge(varied, i - 1)
                    act.activation(squared[p][:, :], c[u][:, :], ACT.Square).then_inc(squares, 1)
                if recurrent and skew.has(i, 1):
                    act.wait_ge(inverses, i)
                    if skew.has(i, 1, 2):
                        act.wait_ge(spread[1], i - 2)
                    for t in range(T):
                        last = act.activation(diag[1][1 - p][:, t * P:(t + 1) * P], ident[:, :], ACT.Copy,
                                              scale=inverse[1 - p][:, T + t:T + t + 1])
                    last.then_inc(diagonal[1], 1)
                if recurrent and skew.has(i, 2):
                    act.wait_ge(x_made[1], i - 1)
                    act.activation(columns(X, (i - 2) * PAIR, PAIR), x2[p][:, :], ACT.Identity,
                                   bias=b_col[:, :], scale=w_col[:, :]).then_inc(X_made, 1)
                if gate and skew.has(i, 3):
                    act.wait_ge(l_made, i - 2)
                    if skew.has(i, 3, 2):
                        act.wait_ge(t_made, i - 4)
                    act.activation(rowed[1 - p][:, :], l_ps[0:E, :], ACT.Identity, bias=gate_col[:, :])\
                       .then_inc(l_out, 1)

            skew.run(act, step)


def recurrent_stage(nc, hT, X, ident, weights):
    W_in, conv_w, conv_b, nu_log, theta_log, gamma_log, B_re, B_im, C_re, C_im, W_out, b_out = weights
    N = B_re.shape[0]
    TAPS = conv_w.shape[2]
    BEFORE = (TAPS - 1) // 2
    PADDED = SEQ + TAPS - 1
    PAIRS = hT.shape[1] // PAIR
    TWO_PI_HI = 6.28125
    TWO_PI_LO = 0.0019353071795864769
    skew = Skewed(PAIRS, 4, 3)
    with ExitStack() as ctx:
        pool = Pools(nc, ctx, "rec")
        w_in = pool.sbuf("w_in", [P, P])
        w_inT = pool.sbuf("w_inT", [P, P])
        w_out = pool.sbuf("w_out", [P, N])
        w_outT = pool.sbuf("w_outT", [P, P])
        B = pool.sbuf("B", [P, N])
        BT = pool.sbuf("BT", [N, P])
        conv = pool.sbuf("conv", [N, N, TAPS])
        conv_bias = pool.sbuf("conv_bias", [N, 1])
        taps = [pool.sbuf(f"taps{t}", [P, P]) for t in range(3)]
        C_rows = [pool.sbuf(f"C_rows{t}", [N, P]) for t in range(2)]
        C_cos = pool.sbuf("C_cos", [P, N])
        C_sin = pool.sbuf("C_sin", [P, N])
        out_bias = pool.sbuf("out_bias", [P, 1])
        nu = pool.sbuf("nu", [P, 1])
        theta = pool.sbuf("theta", [P, 1])
        gamma = pool.sbuf("gamma", [P, 1])
        tiny = [pool.sbuf(f"tiny{t}", [P, 1]) for t in range(8)]
        turns_i = pool.sbuf("turns_i", [P, 1], I32)
        sign = pool.sbuf("sign", [P, 1])
        cos = pool.sbuf("cos", [P, 2, SEQ])
        sin = pool.sbuf("sin", [P, 2, SEQ])
        part = [pool.sbuf(f"part{t}", [P, SEQ]) for t in range(2)]
        decay = pool.sbuf("decay", [P, 2, SEQ])
        bias_B = pool.sbuf("bias_B", [P, 1])
        bias_im = pool.sbuf("bias_im", [P, 1])
        bias_re = pool.sbuf("bias_re", [P, 1])

        v_pad = [pool.sbuf(f"v_pad{u}", [P, 2, PADDED]) for u in range(2)]
        gated = [pool.sbuf(f"gated{u}", [N, PAIR]) for u in range(4)]
        Bv = [pool.sbuf(f"Bv{u}", [P, PAIR]) for u in range(2)]
        Bv_turned = [pool.sbuf(f"Bv_turned{u}", [P, PAIR]) for u in range(2)]
        drive_c = pool.sbuf("drive_c", [P, PAIR])
        drive_s = [pool.sbuf(f"drive_s{u}", [P, PAIR]) for u in range(2)]
        drive = pool.sbuf("drive", [P, PAIR])
        state = [pool.sbuf(f"state{u}", [P, PAIR]) for u in range(2)]
        state_c = [pool.sbuf(f"state_c{u}", [P, PAIR]) for u in range(2)]
        state_s = [pool.sbuf(f"state_s{u}", [P, PAIR]) for u in range(2)]
        product = [pool.sbuf(f"product{u}", [P, PAIR]) for u in range(2)]
        in_ps = [pool.bank(f"in{u}") for u in range(2)]
        B_ps = [pool.bank(f"B{u}") for u in range(2)]
        y_ps = [pool.bank(f"y{u}") for u in range(2)]
        o_ps = [pool.bank(f"o{u}") for u in range(2)]

        loaded = pool.sem("loaded")
        exped = pool.sem("exped")
        chain = pool.sem("chain")
        sined = pool.sem("sined")
        folded = pool.sem("folded")
        angles = pool.sem("angles")
        tabled = pool.sem("tabled")
        zeroed = pool.sem("zeroed")
        projected = pool.sem("projected")
        gelued = pool.sem("gelued")
        v_low = pool.sem("v_low")
        v_high = pool.sem("v_high")
        driven = pool.sem("driven")
        Bv_made = pool.sem("Bv_made")
        cos_made = pool.sem("cos_made")
        sin_made = pool.sem("sin_made")
        drive_made = pool.sem("drive_made")
        scanned = pool.sem("scanned")
        state_c_made = pool.sem("state_c_made")
        state_s_made = pool.sem("state_s_made")
        y_made = pool.sem("y_made")
        product_made = pool.sem("product_made")
        o_made = pool.sem("o_made")
        h_made = pool.sem("h_made")
        LOADS = 17
        block = ctx.enter_context(nc.Block())

        def column(v):
            return v.rearrange("(p o) -> p o", o=1)

        @block.sync
        def _(sp):
            for dst, src in (
                (w_in[:, :], W_in), (w_out[:, :], W_out), (B[0:N, :], B_re), (B[N:P, :], B_im),
                (conv[:, :, :], conv_w), (conv_bias[:, :], column(conv_b)),
                (C_rows[0][:, 0:N], C_re), (C_rows[0][:, N:P], C_im),
                (C_rows[1][:, 0:N], C_im), (C_rows[1][:, N:P], C_re), (out_bias[:, :], column(b_out)),
                (nu[0:N, :], column(nu_log)), (nu[N:P, :], column(nu_log)),
                (theta[0:N, :], column(theta_log)), (theta[N:P, :], column(theta_log)),
                (gamma[0:N, :], column(gamma_log)), (gamma[N:P, :], column(gamma_log)),
            ):
                sp.dma_start(dst, src).then_inc(loaded, DMA)

        @block.gpsimd
        def _(gp):
            for u in range(2):
                gp.memset(v_pad[u][:, :, :], 0.0).then_inc(zeroed, 1)
                gp.memset(product[u][:, :], 0.0).then_inc(zeroed, 1)
            gp.memset(w_outT[:, :], 0.0).then_inc(zeroed, 1)
            gp.memset(taps[2][:, :], 0.0).then_inc(zeroed, 1)
            gp.wait_ge(tabled, 3)

            def step(i, u):
                p = u % 2
                if skew.has(i, 2):
                    gp.wait_ge(Bv_made, (i - 1) * 3)
                    if skew.has(i, 2, 2):
                        gp.wait_ge(drive_made, i - 3)
                    gp.tensor_tensor(drive_s[p][:, :], Bv_turned[p][:, :],
                                     sin[:, :, :].rearrange("p s t -> p (s t)"), ALU.mult).then_inc(sin_made, 1)
                    gp.wait_ge(scanned, i - 1)
                    if skew.has(i, 2, 2):
                        gp.wait_ge(y_made, i - 3)
                    gp.tensor_tensor(state_s[p][:, :], state[p][:, :],
                                     sin[:, :, :].rearrange("p s t -> p (s t)"), ALU.mult).then_inc(state_s_made, 1)

            skew.run(gp, step)

        @block.scalar
        def _(act):
            act.wait_ge(loaded, LOADS * DMA)
            act.activation(tiny[0][:, :], nu[:, :], ACT.Exp).then_inc(exped, 1)
            act.activation(theta[:, :], theta[:, :], ACT.Exp).then_inc(exped, 1)
            act.activation(gamma[:, :], gamma[:, :], ACT.Exp).then_inc(exped, 1)
            act.wait_ge(exped, 3)
            act.activation(nu[:, :], tiny[0][:, :], ACT.Exp, scale=-1.0).then_inc(exped, 1)
            act.wait_ge(angles, 1)
            act.activation(tiny[1][:, :], theta[:, :], ACT.Sin, scale=0.5).then_inc(sined, 1)
            act.activation(tiny[2][:, :], theta[:, :], ACT.Sin, scale=0.25).then_inc(sined, 1)
            act.wait_ge(tabled, 3)

            def step(i, u):
                p = u % 2
                if skew.has(i, 0):
                    act.wait_ge(projected, i + 1)
                    if skew.has(i, 0, 4):
                        act.wait_ge(product_made, i - 3)
                    act.activation(gated[u][:, :], in_ps[p][0:N, :], ACT.Gelu).then_inc(gelued, 1)
                    act.wait_ge(v_low, i + 1)
                    act.activation(v_pad[p][N:P, :, BEFORE - 1:BEFORE - 1 + SEQ],
                                   v_pad[p][0:N, :, BEFORE:BEFORE + SEQ], ACT.Copy).then_inc(v_high, 1)
                if skew.has(i, 1):
                    q = 1 - p
                    act.wait_ge(driven, i)
                    if skew.has(i, 1, 2):
                        act.wait_ge(cos_made, i - 2)
                        act.wait_ge(sin_made, i - 2)
                    act.activation(Bv[q][:, :], B_ps[q][:, :], ACT.Identity, bias=bias_B[:, :]).then_inc(Bv_made, 1)
                    act.activation(Bv_turned[q][0:N, :], B_ps[q][N:P, :], ACT.Identity,
                                   bias=bias_im[N:P, :]).then_inc(Bv_made, 1)
                    act.activation(Bv_turned[q][N:P, :], B_ps[q][0:N, :], ACT.Identity,
                                   bias=bias_re[0:N, :], scale=-1.0).then_inc(Bv_made, 1)

            skew.run(act, step)

        @block.tensor
        def _(pe):
            pe.wait_ge(loaded, LOADS * DMA)
            pe.transpose(in_ps[0][:, 0:P], w_in[:, :], ident[:, :]).then_inc(folded, 1)
            pe.transpose(in_ps[1][0:N, 0:P], w_out[:, :], ident[:, :]).then_inc(folded, 1)
            pe.transpose(y_ps[0][:, 0:N], C_rows[0][:, :], ident[0:N, 0:N]).then_inc(folded, 1)
            pe.transpose(y_ps[1][:, 0:N], C_rows[1][:, :], ident[0:N, 0:N]).then_inc(folded, 1)
            pe.wait_ge(tabled, 1)
            pe.transpose(B_ps[0][0:N, 0:P], B[:, :], ident[:, :]).then_inc(folded, 1)
            pe.wait_ge(tabled, 2)
            for k in range(TAPS):
                bank, at = (o_ps[0], k * P) if k < 4 else (o_ps[1], 0)
                last = pe.matmul(bank[0:N, at:at + P], conv[:, :, k], BT[:, :], start=True, stop=True)
            pe.matmul(B_ps[1][:, 0:1], BT[:, :], conv_bias[:, :], start=True, stop=True).then_inc(folded, 1)
            pe.wait_ge(tabled, 3)

            def step(i, u):
                p = u % 2
                q = 1 - p
                if skew.has(i, 3):
                    if skew.has(i, 3, 2):
                        pe.wait_ge(product_made, i - 4)
                    pe.wait_ge(state_c_made, i - 2)
                    pe.wait_ge(state_s_made, i - 2)
                    pe.matmul(y_ps[q][0:N, :], C_cos[:, :], state_c[q][:, :], start=True, stop=False)
                    pe.matmul(y_ps[q][0:N, :], C_sin[:, :], state_s[q][:, :], start=False, stop=True)\
                      .then_inc(y_made, 1)
                if skew.has(i, 0):
                    if skew.has(i, 0, 2):
                        pe.wait_ge(gelued, i - 1)
                        pe.wait_ge(v_high, i - 1)
                        pe.wait_ge(v_low, i - 1)
                    pe.matmul(in_ps[p][:, :], w_inT[:, :], columns(X, i * PAIR, PAIR),
                              start=True, stop=True).then_inc(projected, 1)
                if skew.has(i, 3):
                    if skew.has(i, 3, 2):
                        pe.wait_ge(h_made, i - 4)
                    pe.wait_ge(product_made, i - 2)
                    pe.matmul(o_ps[q][:, :], w_outT[:, :], product[q][:, :], start=True, stop=True)\
                      .then_inc(o_made, 1)
                if skew.has(i, 1):
                    if skew.has(i, 1, 2):
                        pe.wait_ge(Bv_made, (i - 2) * 3)
                    pe.wait_ge(v_high, i)
                    pe.wait_ge(v_low, i)
                    for t in range(3):
                        last = pe.matmul(B_ps[q][:, :], taps[t][:, :], v_pad[q][:, :, 2 * t:2 * t + SEQ],
                                         start=(t == 0), stop=(t == 2))
                    last.then_inc(driven, 1)

            skew.run(pe, step)

        @block.vector
        def _(dve):
            count = [0]

            def chained(instruction):
                count[0] += 1
                instruction.then_inc(chain, 1)
                dve.wait_ge(chain, count[0])

            dve.wait_ge(exped, 4)
            dve.tensor_scalar(B[:, :], B[:, :], gamma[:, 0:1], None, ALU.mult).then_inc(tabled, 1)
            chained(dve.tensor_scalar(tiny[3][:, :], theta[:, :], 1.0 / (TWO_PI_HI + TWO_PI_LO), None, ALU.mult))
            chained(dve.tensor_copy(turns_i[:, :], tiny[3][:, :]))
            chained(dve.tensor_copy(tiny[3][:, :], turns_i[:, :]))
            chained(dve.tensor_scalar(tiny[4][:, :], tiny[3][:, :], TWO_PI_HI, None, ALU.mult))
            chained(dve.tensor_tensor(theta[:, :], theta[:, :], tiny[4][:, :], ALU.subtract))
            chained(dve.tensor_scalar(tiny[4][:, :], tiny[3][:, :], TWO_PI_LO, None, ALU.mult))
            dve.tensor_tensor(theta[:, :], theta[:, :], tiny[4][:, :], ALU.subtract).then_inc(angles, 1)
            dve.wait_ge(sined, 2)
            half_sin, quarter_sin, half_cos, c_step, s_step, spare = (tiny[t] for t in (1, 2, 3, 4, 5, 6))
            chained(dve.tensor_tensor(spare[:, :], quarter_sin[:, :], quarter_sin[:, :], ALU.mult))
            chained(dve.tensor_scalar(half_cos[:, :], spare[:, :], -2.0, 1.0, ALU.mult, ALU.add))
            chained(dve.scalar_tensor_tensor(out=s_step[:, :], in0=half_sin[:, :], scalar=2.0,
                                             in1=half_cos[:, :], op0=ALU.mult, op1=ALU.mult))
            chained(dve.tensor_tensor(spare[:, :], half_sin[:, :], half_sin[:, :], ALU.mult))
            chained(dve.tensor_scalar(c_step[:, :], spare[:, :], -2.0, 1.0, ALU.mult, ALU.add))
            chained(dve.memset(cos[:, 0, 0:1], 1.0))
            chained(dve.memset(sin[:, 0, 0:1], 0.0))
            width = 1
            while width < SEQ:
                c0, s0 = cos[:, 0, 0:width], sin[:, 0, 0:width]
                c1, s1 = cos[:, 0, width:2 * width], sin[:, 0, width:2 * width]
                chained(dve.tensor_scalar(part[0][:, 0:width], s0, s_step[:, 0:1], None, ALU.mult))
                chained(dve.scalar_tensor_tensor(out=c1, in0=c0, scalar=c_step[:, 0:1],
                                                 in1=part[0][:, 0:width], op0=ALU.mult, op1=ALU.subtract))
                chained(dve.tensor_scalar(part[1][:, 0:width], c0, s_step[:, 0:1], None, ALU.mult))
                chained(dve.scalar_tensor_tensor(out=s1, in0=s0, scalar=c_step[:, 0:1],
                                                 in1=part[1][:, 0:width], op0=ALU.mult, op1=ALU.add))
                chained(dve.tensor_tensor(spare[:, :], s_step[:, :], s_step[:, :], ALU.mult))
                chained(dve.scalar_tensor_tensor(out=s_step[:, :], in0=s_step[:, :], scalar=2.0,
                                                 in1=c_step[:, :], op0=ALU.mult, op1=ALU.mult))
                chained(dve.tensor_scalar(c_step[:, :], spare[:, :], -2.0, 1.0, ALU.mult, ALU.add))
                width *= 2
            chained(dve.tensor_copy(cos[:, 1, :], cos[:, 0, :]))
            chained(dve.tensor_copy(sin[:, 1, :], sin[:, 0, :]))
            chained(dve.memset(decay[:, :, :], 1.0))
            chained(dve.tensor_scalar(decay[:, :, :], decay[:, :, :], nu[:, 0:1], None, ALU.mult))
            chained(dve.memset(decay[:, :, 0:1], 0.0))
            dve.wait_ge(folded, 5)
            dve.tensor_copy(BT[:, :], B_ps[0][0:N, 0:P]).then_inc(tabled, 1)
            dve.wait_ge(zeroed, 6)
            dve.tensor_copy(w_inT[:, :], in_ps[0][:, 0:P])
            dve.tensor_copy(w_outT[0:N, :], in_ps[1][0:N, 0:P])
            dve.tensor_copy(C_cos[0:N, :], y_ps[0][0:N, 0:N])
            dve.tensor_scalar(C_cos[N:P, :], y_ps[0][N:P, 0:N], -1.0, None, ALU.mult)
            dve.tensor_scalar(C_sin[:, :], y_ps[1][:, 0:N], -1.0, None, ALU.mult)
            dve.wait_ge(folded, 6)
            for k in range(TAPS):
                bank, at = (o_ps[0], k * P) if k < 4 else (o_ps[1], 0)
                low = k % 2 * N
                dve.tensor_copy(taps[k // 2][low:low + N, :], bank[0:N, at:at + P])
            dve.tensor_copy(bias_B[:, :], B_ps[1][:, 0:1])
            for low in (0, N):
                dve.tensor_copy(bias_im[low:low + N, :], B_ps[1][N:P, 0:1])
                last = dve.tensor_scalar(bias_re[low:low + N, :], B_ps[1][0:N, 0:1], -1.0, None, ALU.mult)
            last.then_inc(tabled, 1)

            cos_flat = cos[:, :, :].rearrange("p s t -> p (s t)")
            decay_flat = decay[:, :, :].rearrange("p s t -> p (s t)")

            def step(i, u):
                p = u % 2
                q = 1 - p
                if skew.has(i, 3):
                    dve.wait_ge(y_made, i - 2)
                    if skew.has(i, 3, 2):
                        dve.wait_ge(o_made, i - 4)
                    dve.tensor_tensor(product[q][0:N, :], y_ps[q][0:N, :], gated[(u + 1) % 4][:, :], ALU.mult)\
                       .then_inc(product_made, 1)
                if skew.has(i, 0):
                    dve.wait_ge(projected, i + 1)
                    dve.tensor_copy(v_pad[p][0:N, :, BEFORE:BEFORE + SEQ],
                                    in_ps[p][N:P, :].rearrange("p (s t) -> p s t", s=2)).then_inc(v_low, 1)
                if skew.has(i, 2):
                    dve.wait_ge(Bv_made, (i - 1) * 3)
                    dve.tensor_tensor(drive_c[:, :], Bv[p][:, :], cos_flat, ALU.mult).then_inc(cos_made, 1)
                    dve.wait_ge(cos_made, i - 1)
                    dve.wait_ge(sin_made, i - 1)
                    dve.tensor_tensor(drive[:, :], drive_c[:, :], drive_s[p][:, :], ALU.add).then_inc(drive_made, 1)
                    dve.wait_ge(drive_made, i - 1)
                    if skew.has(i, 2, 2):
                        dve.wait_ge(state_s_made, i - 3)
                    dve.tensor_tensor_scan(state[p][:, :], decay_flat, drive[:, :], 0.0, ALU.mult, ALU.add)\
                       .then_inc(scanned, 1)
                    dve.wait_ge(scanned, i - 1)
                    if skew.has(i, 2, 2):
                        dve.wait_ge(y_made, i - 3)
                    dve.tensor_tensor(state_c[p][:, :], state[p][:, :], cos_flat, ALU.mult)\
                       .then_inc(state_c_made, 1)
                if skew.has(i, 3):
                    dve.wait_ge(o_made, i - 2)
                    h = columns(hT, (i - 3) * PAIR, PAIR)
                    dve.scalar_tensor_tensor(out=h, in0=o_ps[q][:, :], scalar=out_bias[:, 0:1], in1=h,
                                             op0=ALU.add, op1=ALU.add).then_inc(h_made, 1)

            skew.run(dve, step)


def routing_stage(nc, logits, routes, tiles, E):
    with ExitStack() as ctx:
        pool = Pools(nc, ctx, "rou")
        W = tiles * E
        rank_i = pool.sbuf("rank_i", [P, W], I32)
        rank = pool.sbuf("rank", [P, W])
        reaches = pool.sbuf("reaches", [P, W])
        taken = pool.sbuf("taken", [P, W])
        rest = pool.sbuf("rest", [P, W])
        second = pool.sbuf("second", [P, W])
        top = [pool.sbuf(f"top{n}", [P, tiles]) for n in range(2)]
        best = pool.sbuf("best", [P, tiles])
        gap = pool.sbuf("gap", [P, tiles])
        ratio = pool.sbuf("ratio", [P, tiles])
        total = pool.sbuf("total", [P, tiles])
        share = [pool.sbuf(f"share{n}", [P, tiles]) for n in range(2)]
        ranked = pool.sem("ranked")
        chain = pool.sem("chain")
        gaps = pool.sem("gaps")
        ratios = pool.sem("ratios")
        block = ctx.enter_context(nc.Block())

        def by_tile(x):
            return x[:, :].rearrange("p (t e) -> p t e", e=E)

        def spread(x):
            return x[:, :].unsqueeze(2).to_broadcast([P, tiles, E])

        @block.gpsimd
        def _(gp):
            gp.iota(by_tile(rank_i), pattern=[[0, tiles], [-1, E]], base=E, channel_multiplier=0).then_inc(ranked, 1)

        @block.scalar
        def _(act):
            act.wait_ge(gaps, 1)
            act.activation(ratio[:, :], gap[:, :], ACT.Exp).then_inc(ratios, 1)

        @block.vector
        def _(dve):
            count = [0]

            def chained(instruction):
                count[0] += 1
                instruction.then_inc(chain, 1)
                dve.wait_ge(chain, count[0])

            def take_best(values, n, out):
                chained(dve.tensor_reduce(top[n][:, :], by_tile(values), AX.X, ALU.max))
                chained(dve.tensor_tensor(by_tile(reaches), by_tile(values), spread(top[n]), ALU.is_equal))
                chained(dve.tensor_tensor(reaches[:, :], reaches[:, :], rank[:, :], ALU.mult))
                chained(dve.tensor_reduce(best[:, :], by_tile(reaches), AX.X, ALU.max))
                chained(dve.tensor_tensor(by_tile(out), by_tile(rank), spread(best), ALU.is_equal))

            dve.wait_ge(ranked, 1)
            chained(dve.tensor_copy(rank[:, :], rank_i[:, :]))
            take_best(logits, 0, taken)
            chained(dve.scalar_tensor_tensor(out=rest[:, :], in0=taken[:, :], scalar=-3.0e38, in1=logits[:, :],
                                             op0=ALU.mult, op1=ALU.add))
            take_best(rest, 1, second)
            dve.tensor_tensor(gap[:, :], top[1][:, :], top[0][:, :], ALU.subtract).then_inc(gaps, 1)
            dve.wait_ge(ratios, 1)
            chained(dve.tensor_scalar(total[:, :], ratio[:, :], 1.0, None, ALU.add))
            chained(dve.reciprocal(share[0][:, :], total[:, :]))
            chained(dve.tensor_tensor(share[1][:, :], share[0][:, :], ratio[:, :], ALU.mult))
            chained(dve.tensor_tensor(by_tile(taken), by_tile(taken), spread(share[0]), ALU.mult))
            chained(dve.tensor_tensor(by_tile(second), by_tile(second), spread(share[1]), ALU.mult))
            chained(dve.tensor_tensor(routes[:, :], taken[:, :], second[:, :], ALU.add))


def experts_stage(nc, hT, X, routes, ident, weights, out):
    w1, b1, w2, b2 = weights
    E, D, F2 = w1.shape
    FS = F2 // P
    T = PAIR // P
    PAIRS = hT.shape[1] // PAIR
    assert FS == 2 and T * E <= P
    out_v = out.rearrange("(i t p) d -> i p t d", t=T, p=P)
    with ExitStack() as ctx:
        pool = Pools(nc, ctx, "exp")
        w1_raw = pool.sbuf("w1_raw", [P, E, F2])
        w1_hi = pool.sbuf("w1_hi", [P, E, F2], F32R)
        w1_lo = pool.sbuf("w1_lo", [P, E, F2], F32R)
        w2_sb = pool.sbuf("w2", [P, E, FS, P])
        b1_rows = pool.sbuf("b1_rows", [E * FS, P])
        b1_col = pool.sbuf("b1_col", [P, E * FS])
        b2_tiles = pool.sbuf("b2_tiles", [P, T, P])
        x_hi = [pool.sbuf(f"x_hi{p}", [P, PAIR], F32R) for p in range(2)]
        x_lo = [pool.sbuf(f"x_lo{p}", [P, PAIR], F32R) for p in range(2)]
        h_now = [pool.sbuf(f"h_now{p}", [P, PAIR]) for p in range(2)]
        route_now = [pool.sbuf(f"route_now{p}", [P, P]) for p in range(2)]
        routeT = [pool.sbuf(f"routeT{p}", [P, P]) for p in range(2)]
        hidden = [[pool.sbuf(f"hidden{p}{f}", [P, PAIR]) for f in range(FS)] for p in range(2)]
        total = [pool.sbuf(f"total{p}", [P, T, P]) for p in range(2)]
        hidden_ps = [[pool.bank(f"hidden{p}{f}") for f in range(FS)] for p in range(2)]
        y_ps = [pool.bank(f"y{p}") for p in range(2)]
        start_ps = pool.bank("start")
        route_ps = pool.bank("route")

        weights_in = pool.sem("weights_in")
        zeroed = pool.sem("zeroed")
        b2_in = pool.sem("b2_in")
        b1_turned = pool.sem("b1_turned")
        hi_made = pool.sem("hi_made")
        ready = pool.sem("ready")
        x_hi_made = pool.sem("x_hi_made")
        x_lo_made = pool.sem("x_lo_made")
        now_made = pool.sem("now_made")
        route_turned = pool.sem("route_turned")
        routeT_made = pool.sem("routeT_made")
        started = pool.sem("started")
        start_out = pool.sem("start_out")
        hidden_run = pool.sem("hidden_run")
        hidden_out = pool.sem("hidden_out")
        y_run = pool.sem("y_run")
        y_added = pool.sem("y_added")
        stored = [pool.sem(f"stored{p}") for p in range(2)]
        block = ctx.enter_context(nc.Block())

        def rounds(eng, pair):
            pair(0, 0)
            pair(1, 1)
            with eng.Fori(1, PAIRS // 2) as r:
                pair(r * 2, 0)
                pair(r * 2 + 1, 1)

        def known(i):
            return isinstance(i, int)

        @block.sync
        def _(sp):
            sp.dma_start(w1_raw[:, :, :], w1.rearrange("e d f -> d e f")).then_inc(weights_in, DMA)
            sp.dma_start(b1_rows[:, :], b1.rearrange("e (f p) -> (e f) p", p=P)).then_inc(weights_in, DMA)
            for e in range(E):
                sp.dma_start(w2_sb[:, e, :, :], w2[e].rearrange("(f p) d -> p f d", p=P)).then_inc(weights_in, DMA)
            sp.wait_ge(zeroed, 3)
            for t in range(T):
                sp.dma_start(b2_tiles[t * E:(t + 1) * E, t, :], b2).then_inc(b2_in, DMA)

            def pair(i, p):
                sp.wait_ge(y_added, i * (E * T) + E * T)
                sp.dma_start(out_v[bass.ds(i, 1), :, :, :].rearrange("i p t d -> p (i t) d"),
                             total[p][:, :, :]).then_inc(stored[p], DMA)

            rounds(sp, pair)
            for p in range(2):
                sp.wait_ge(stored[p], PAIRS // 2 * DMA)

        @block.gpsimd
        def _(gp):
            gp.memset(b2_tiles[:, :, :], 0.0).then_inc(zeroed, 1)
            for p in range(2):
                gp.memset(route_now[p][:, :], 0.0).then_inc(zeroed, 1)
            gp.wait_ge(zeroed, 3)

            def pair(i, p):
                if not known(i):
                    gp.wait_ge(started, i - 1)
                    gp.wait_ge(y_added, i * (E * T) - E * T)
                gp.tensor_copy(h_now[p][:, :], columns(hT, i * PAIR, PAIR)).then_inc(now_made, 1)
                gp.tensor_copy(route_now[p][:, 0:T * E], columns(routes, i * (T * E), T * E)).then_inc(now_made, 1)

            rounds(gp, pair)

        @block.tensor
        def _(pe):
            def begin(i, p):
                pe.wait_ge(now_made, i * 2 + 2)
                if not (known(i) and i == 0):
                    pe.wait_ge(routeT_made, i)
                pe.transpose(route_ps[:, 0:P], route_now[p][:, :], ident[:, :]).then_inc(route_turned, 1)

            def start(i, p):
                if not (known(i) and i == 0):
                    pe.wait_ge(start_out, i)
                pe.wait_ge(routeT_made, i + 1)
                for t in range(T):
                    tile = start_ps[:, t * P:(t + 1) * P]
                    pe.matmul(tile, routeT[p][:, :], b2_tiles[:, t, :], start=True, stop=False)
                    last = pe.matmul(tile, h_now[p][:, t * P:(t + 1) * P], ident[:, :], start=False, stop=True)
                last.then_inc(started, 1)

            def first(i, e, p, f):
                unit = i * E + e
                if f == 0 and e == 0:
                    pe.wait_ge(x_hi_made, i + 1)
                    pe.wait_ge(x_lo_made, i + 1)
                if not (known(i) and unit < 2):
                    pe.wait_ge(hidden_out, unit * 2 + (f - 3))
                cols = slice(f * P, (f + 1) * P)
                bank = hidden_ps[e % 2][f][:, :]
                pe.matmul(bank, w1_hi[:, e, cols], x_hi[p][:, :], start=True, stop=False)
                pe.matmul(bank, w1_hi[:, e, cols], x_lo[p][:, :], start=False, stop=False)
                pe.matmul(bank, w1_lo[:, e, cols], x_hi[p][:, :], start=False, stop=True).then_inc(hidden_run, 1)

            def second(i, e, tiles):
                unit = i * E + e
                if tiles[0] == 0:
                    pe.wait_ge(hidden_out, unit * 2 + 2)
                    if not (known(i) and unit < 2):
                        pe.wait_ge(y_added, unit * T + (T - 2 * T))
                for t in tiles:
                    for f in range(FS):
                        last = pe.matmul(y_ps[e % 2][:, t * P:(t + 1) * P],
                                         hidden[e % 2][f][:, t * P:(t + 1) * P], w2_sb[:, e, f, :],
                                         start=(f == 0), stop=(f == FS - 1))
                if tiles[-1] == T - 1:
                    last.then_inc(y_run, 1)

            pe.wait_ge(weights_in, (2 + E) * DMA)
            pe.transpose(start_ps[:, 0:E * FS], b1_rows[:, :], ident[0:E * FS, 0:E * FS]).then_inc(b1_turned, 1)
            pe.wait_ge(ready, 1)
            pe.wait_ge(b2_in, T * DMA)

            def pair(i, p):
                begin(i, p)
                for e in range(E):
                    before = (i, e - 1) if e > 0 else (None if known(i) and i == 0 else (i - 1, E - 1))
                    first(i, e, p, 0)
                    if before:
                        second(*before, [0, 1])
                    first(i, e, p, 1)
                    if e == 0:
                        start(i, p)
                    if before:
                        second(*before, [2, 3])

            rounds(pe, pair)
            second(PAIRS - 1, E - 1, list(range(T)))

        @block.scalar
        def _(act):
            act.wait_ge(ready, 1)

            def split(i, p):
                if not known(i):
                    act.wait_ge(hidden_run, i * (E * 2) - E * 2)
                act.activation(x_hi[p][:, :], columns(X, i * PAIR, PAIR), ACT.Copy).then_inc(x_hi_made, 1)

            split(0, 0)

            def pair(i, p):
                act.wait_ge(route_turned, i + 1)
                act.activation(routeT[p][:, :], route_ps[:, 0:P], ACT.Copy).then_inc(routeT_made, 1)
                for e in range(E):
                    unit = i * E + e
                    for f in range(FS):
                        act.wait_ge(hidden_run, unit * 2 + (f + 1))
                        if f == 0 and not (known(i) and unit < 2):
                            act.wait_ge(y_run, unit - 1)
                        act.activation(hidden[e % 2][f][:, :], hidden_ps[e % 2][f][:, :], ACT.Relu,
                                       bias=b1_col[:, e * FS + f:e * FS + f + 1]).then_inc(hidden_out, 1)
                    if e == 4 and not (known(i) and i == PAIRS - 1):
                        split(i + 1, 1 - p)

            pair(0, 0)
            with act.Fori(0, PAIRS // 2 - 1) as r:
                pair(r * 2 + 1, 1)
                pair(r * 2 + 2, 0)
            pair(PAIRS - 1, 1)

        @block.vector
        def _(dve):
            def split(i, p):
                dve.wait_ge(x_hi_made, i + 1)
                dve.tensor_tensor(x_lo[p][:, :], columns(X, i * PAIR, PAIR), x_hi[p][:, :].bitcast(F32),
                                  ALU.subtract).then_inc(x_lo_made, 1)

            def pair(i, p):
                dve.wait_ge(started, i + 1)
                dve.wait_ge(now_made, i * 2 + 2)
                if not (known(i) and i < 2):
                    dve.wait_ge(stored[p], (i - p) * (DMA // 2))
                dve.tensor_copy(total[p][:, :, :], start_ps[:, :].rearrange("p (t d) -> p t d", t=T))\
                   .then_inc(start_out, 1)
                for e in range(E):
                    unit = i * E + e
                    dve.wait_ge(y_run, unit + 1)
                    for t in range(T):
                        if e == 0:
                            if t == 0:
                                dve.wait_ge(start_out, i + 1)
                        else:
                            dve.wait_ge(y_added, unit * T + (t + 1 - T))
                        dve.scalar_tensor_tensor(
                            out=total[p][:, t, :], in0=y_ps[e % 2][:, t * P:(t + 1) * P],
                            scalar=route_by_tile(i, t, e, p), in1=total[p][:, t, :],
                            op0=ALU.mult, op1=ALU.add).then_inc(y_added, 1)
                    if e == 4 and not (known(i) and i == PAIRS - 1):
                        split(i + 1, 1 - p)

            def route_by_tile(i, t, e, p):
                return route_now[p][:, t * E + e:t * E + e + 1]

            dve.wait_ge(weights_in, (2 + E) * DMA)
            dve.tensor_copy(w1_hi[:, :, :], w1_raw[:, :, :]).then_inc(hi_made, 1)
            dve.wait_ge(hi_made, 1)
            dve.tensor_tensor(w1_lo[:, :, :], w1_raw[:, :, :], w1_hi[:, :, :].bitcast(F32), ALU.subtract)
            dve.wait_ge(b1_turned, 1)
            dve.tensor_copy(b1_col[:, :], start_ps[:, 0:E * FS]).then_inc(ready, 1)
            split(0, 0)
            pair(0, 0)
            with dve.Fori(0, PAIRS // 2 - 1) as r:
                pair(r * 2 + 1, 1)
                pair(r * 2 + 2, 0)
            pair(PAIRS - 1, 1)


def tower_program(nc, x, args, out):
    (emb, pos, Wq, bq, Wk, bk, Wv, bv, Wo, bo, W1, b1, W2, b2,
     ln_w, ln_b, W_in, conv_w, conv_b, nu_log, theta_log, gamma_log, B_re, B_im, C_re, C_im, W_out, b_out,
     gate_w, gate_b, e_w1, e_b1, e_w2, e_b2) = args
    tokens = x.shape[0] * x.shape[1]
    E = gate_w.shape[1]
    EPS = 1e-5
    with ExitStack() as ctx:
        whole = Pools(nc, ctx, "all")
        hT = whole.sbuf("hT", [P, tokens])
        ident = whole.sbuf("ident", [P, P])
        embed_stage(nc, hT, ident, x, emb, pos)
        layers_stage(nc, hT, ident, (Wq, bq, Wk, bk, Wv, bv, Wo, bo, W1, b1, W2, b2))
        X = whole.sbuf("X", [P, tokens])
        norm_stage(nc, "nr", hT, X, ident, EPS, recurrent=(ln_w, ln_b))
        recurrent_stage(nc, hT, X, ident, (W_in, conv_w, conv_b, nu_log, theta_log, gamma_log,
                                           B_re, B_im, C_re, C_im, W_out, b_out))
        logits = whole.sbuf("logits", [P, tokens // P * E])
        routes = whole.sbuf("routes", [P, tokens // P * E])
        norm_stage(nc, "ne", hT, X, ident, EPS, gate=(gate_w, gate_b, logits))
        routing_stage(nc, logits, routes, tokens // P, E)
        experts_stage(nc, hT, X, routes, ident, (e_w1, e_b1, e_w2, e_b2), out)


_INS = ["L0_tok_emb", "L0_tok_pos", "L0_tok_Wq", "L0_tok_bq", "L0_tok_Wk", "L0_tok_bk", "L0_tok_Wv", "L0_tok_bv",
        "L0_tok_Wo", "L0_tok_bo", "L0_tok_W1", "L0_tok_b1", "L0_tok_W2", "L0_tok_b2",
        "L0_attn_ln_w", "L0_attn_ln_b", "L0_attn_W_in", "L0_attn_conv_w", "L0_attn_conv_b", "L0_attn_nu_log",
        "L0_attn_theta_log", "L0_attn_gamma_log", "L0_attn_B_re", "L0_attn_B_im", "L0_attn_C_re", "L0_attn_C_im",
        "L0_attn_W_out", "L0_attn_b_out",
        "L0_ffn_gate_w", "L0_ffn_gate_b", "L0_ffn_w1", "L0_ffn_b1", "L0_ffn_w2", "L0_ffn_b2"]


def kernel(**inputs):
    import numpy as _np
    import concourse.bacc as _bacc
    from concourse import mybir as _mybir
    from concourse.bass_utils import run_bass_kernel_spmd as _run

    nc = _bacc.Bacc("TRN2", target_bir_lowering=False, num_devices=1)
    arrays, args = {}, []
    for name in ["x"] + _INS:
        a = _np.ascontiguousarray(inputs[name])
        arrays[f"in_{name}"] = a
        args.append(nc.dram_tensor(f"in_{name}", a.shape, _mybir.dt.from_np(a.dtype), kind="ExternalInput").ap())
    x = args[0]
    B, S = inputs["x"].shape
    D = inputs["L0_tok_emb"].shape[1]
    out = nc.dram_tensor("out", (B * S, D), _mybir.dt.float32, kind="ExternalOutput").ap()
    tower_program(nc, x, args[1:], out)
    r = _run(nc, [arrays], core_ids=[0])
    return r.results[0]["out"].reshape(B, S, D)
```

```python
from contextlib import ExitStack

import concourse.bass as bass
from concourse import mybir

F32 = mybir.dt.float32
F32R = mybir.dt.float32r
I32 = mybir.dt.int32
U32 = mybir.dt.uint32
ALU = mybir.AluOpType
ACT = mybir.ActivationFunctionType
AX = mybir.AxisListType

P = 128
SEQ = 256
PAIR = 2 * SEQ
HEAD = 64
MASKED = -1.0e30
DMA = 16


class Pools:

    def __init__(self, nc, ctx, prefix):
        self.nc, self.ctx, self.prefix = nc, ctx, prefix

    def sbuf(self, name, shape, dtype=F32):
        return self.ctx.enter_context(self.nc.sbuf_tensor(f"{self.prefix}_{name}", shape, dtype))

    def bank(self, name):
        return self.ctx.enter_context(self.nc.psum_tensor(f"{self.prefix}_ps_{name}", [P, 512], F32))

    def sem(self, name):
        return self.ctx.enter_context(self.nc.semaphore(f"{self.prefix}_{name}"))


def settled(engine, value):
    return value if isinstance(value, int) else engine.to_reg(value)


def columns(tensor, start, count):
    return tensor[:, bass.ds(start, count)]


def embed_stage(nc, hT, ident, ids, emb, pos):
    vocab = emb.shape[0]
    n_tiles = ids.shape[0] * ids.shape[1] // P
    RING = 4
    with ExitStack() as ctx:
        pool = Pools(nc, ctx, "emb")
        ids_i = pool.sbuf("ids_i", [n_tiles, P], I32)
        ids_f = pool.sbuf("ids_f", [n_tiles, P])
        wrap = pool.sbuf("wrap", [n_tiles, P])
        index = pool.sbuf("index", [P, n_tiles], U32)
        index_now = [pool.sbuf(f"index_now{t}", [P, 1], U32) for t in range(RING)]
        rows = [pool.sbuf(f"rows{t}", [P, P]) for t in range(RING)]
        pos_rows = pool.sbuf("pos_rows", [P, 2, P])
        posT = pool.sbuf("posT", [P, SEQ])
        turned = [pool.bank(f"turned{t}") for t in range(RING)]
        setup_ps = pool.bank("setup_ps")
        pos_ps = pool.bank("pos_ps")

        ids_in = pool.sem("ids_in")
        pos_in = pool.sem("pos_in")
        ident_made = pool.sem("ident_made")
        ids_ready = pool.sem("ids_ready")
        setup_turned = pool.sem("setup_turned")
        setup_copied = pool.sem("setup_copied")
        index_copied = pool.sem("index_copied")
        gathered = [pool.sem(f"gathered{t}") for t in range(RING)]
        rows_turned = pool.sem("rows_turned")
        bank_free = pool.sem("bank_free")
        block = ctx.enter_context(nc.Block())

        @block.sync
        def _(sp):
            sp.dma_start(ids_i[:, :], ids.rearrange("b (t p) -> (b t) p", p=P)).then_inc(ids_in, DMA)
            sp.dma_start(pos_rows[:, :, :], pos[0:SEQ, :].rearrange("(t p) d -> p t d", p=P)).then_inc(pos_in, DMA)

        @block.gpsimd
        def _(pool_e):
            pool_e.memset(ident[:, :], 0.0).then_inc(ident_made, 1)
            pool_e.wait_ge(ident_made, 1)
            pool_e.affine_select(out=ident[:, :], in_=ident[:, :], compare_op=ALU.not_equal, fill=1.0,
                                 base=0, pattern=[[-1, P]], channel_multiplier=1).then_inc(ident_made, 1)
            pool_e.wait_ge(setup_copied, 1)
            with pool_e.Fori(0, n_tiles // RING) as i:
                for t in range(RING):
                    pool_e.wait_ge(rows_turned, i * RING + (t + 1))
                    pool_e.tensor_copy(index_now[t][:, :], columns(index, i * RING + t, 1)).then_inc(index_copied, 1)
                    count = settled(pool_e, i * RING + (t + 1))
                    pool_e.wait_ge(ident_made, 2)
                    pool_e.wait_ge(index_copied, count)
                    pool_e.indirect_dma_start(
                        rows[t][:, :], None, emb,
                        bass.IndirectOffsetOnAxis(ap=index_now[t][:, 0:1], axis=0)).then_inc(gathered[t], DMA)

        @block.vector
        def _(dve):
            step = [0]

            def chained(instruction):
                step[0] += 1
                instruction.then_inc(ids_ready, 1)
                dve.wait_ge(ids_ready, step[0])

            dve.wait_ge(ids_in, DMA)
            chained(dve.tensor_copy(ids_f[:, :], ids_i[:, :]))
            chained(dve.tensor_scalar(wrap[:, :], ids_f[:, :], 0.0, float(vocab), ALU.is_lt, ALU.mult))
            chained(dve.tensor_tensor(ids_f[:, :], ids_f[:, :], wrap[:, :], ALU.add))
            dve.tensor_scalar(ids_f[:, :], ids_f[:, :], 0.0, float(vocab - 1), ALU.max, ALU.min).then_inc(ids_ready, 1)
            dve.wait_ge(setup_turned, 1)
            dve.tensor_copy(index[:, :], setup_ps[:, 0:n_tiles]).then_inc(setup_copied, 1)
            dve.wait_ge(setup_turned, 2)
            dve.tensor_copy(posT[:, :], pos_ps[:, 0:SEQ]).then_inc(setup_copied, 1)
            dve.wait_ge(setup_copied, 2)
            with dve.Fori(0, n_tiles // RING) as i:
                for t in range(RING):
                    dve.wait_ge(rows_turned, i * RING + (t + 1 + RING))
                    half = t % 2 * P
                    dve.tensor_tensor(columns(hT, i * (RING * P) + t * P, P), turned[t][:, 0:P],
                                      posT[:, half:half + P], ALU.add).then_inc(bank_free, 1)

        @block.tensor
        def _(pe):
            pe.wait_ge(ident_made, 2)
            pe.wait_ge(ids_ready, 4)
            pe.transpose(setup_ps[:, 0:n_tiles], ids_f[:, :], ident[0:n_tiles, 0:n_tiles]).then_inc(setup_turned, 1)
            pe.wait_ge(pos_in, DMA)
            pe.transpose(pos_ps[:, 0:P], pos_rows[:, 0, :], ident[:, :])
            pe.transpose(pos_ps[:, P:2 * P], pos_rows[:, 1, :], ident[:, :]).then_inc(setup_turned, 1)
            pe.transpose(turned[0][:, 0:P], ident[:, :], ident[:, :]).then_inc(rows_turned, RING)
            pe.transpose(turned[1][:, 0:P], ident[:, :], ident[:, :]).then_inc(bank_free, RING)
            with pe.Fori(0, n_tiles // RING) as i:
                for t in range(RING):
                    pe.wait_ge(gathered[t], i * DMA + DMA)
                    pe.wait_ge(bank_free, i * RING + (t + 1))
                    pe.transpose(turned[t][:, 0:P], rows[t][:, :], ident[:, :]).then_inc(rows_turned, 1)


def layers_stage(nc, hT, ident, weights):
    Wq, bq, Wk, bk, Wv, bv, Wo, bo, W1, b1, W2, b2 = weights
    L, _, HK = Wq.shape
    FF = W1.shape[2]
    PAIRS = hT.shape[1] // PAIR
    JS = HK // P
    FS = FF // P
    UNITS = 2 * JS
    assert UNITS == 8 and FS == 4 and PAIRS % 2 == 0 and PAIRS >= 4
    SCALE = -float(HEAD) ** -0.5

    PROJ = [("k", 0), ("q", 0), ("k", 1), ("q", 1), ("k", 2), ("q", 2), ("k", 3), ("q", 3),
            ("v", 0), ("v", 1), ("v", 2), ("v", 3)]
    FEED = [("f", f) for f in range(FS)]
    SLOTS = {0: PROJ[0:2], 1: PROJ[2:4], 2: PROJ[4:6], 3: PROJ[6:8], 4: PROJ[8:10],
             5: FEED[0:2], 6: FEED[2:4], 7: PROJ[10:12]}
    EARLY = 10
    PER_PAIR = len(PROJ) + FS
    TOTAL = L * PAIRS
    assert PAIRS & (PAIRS - 1) == 0 or TOTAL < 64

    def known(g, value):
        return isinstance(g, int) and g == value

    def piece_base(g):
        if known(g, 0):
            return len(PROJ) // 2
        return g * (PER_PAIR // 2) + (len(PROJ) - PER_PAIR // 2)

    def position(kind, has_prev):
        if kind[0] == "f":
            return EARLY + kind[1]
        at = PROJ.index(kind)
        return at + (FS if has_prev and at >= EARLY else 0)

    def pieces_of(k, has_prev, has_next):
        return [x for x in SLOTS[k] if (x[0] == "f" and has_prev) or (x[0] != "f" and has_next)]

    def residual(g):
        return columns(hT, g % PAIRS * PAIR, PAIR)

    with ExitStack() as ctx:
        pool = Pools(nc, ctx, "lay")
        raw = {n: pool.sbuf(f"raw_{n}", [P, HK]) for n in ("q", "k", "v", "1", "o", "2")}
        w_hi = {n: pool.sbuf(f"w_hi_{n}", [P, HK], F32R) for n in ("q", "k", "v", "1")}
        w_lo = {n: pool.sbuf(f"w_lo_{n}", [P, HK], F32R) for n in ("q", "k", "v", "1")}
        w_whole = {n: pool.sbuf(f"w_{n}", [P, HK]) for n in ("o", "2")}
        N_BIAS = 4 * JS * L + 2 * L
        bias_rows = pool.sbuf("bias_rows", [N_BIAS, P])
        biasT = pool.sbuf("biasT", [P, N_BIAS])
        bias_qkv = pool.sbuf("bias_qkv", [P, 3, JS])
        bias_1 = pool.sbuf("bias_1", [P, FS])
        bias_2 = pool.sbuf("bias_2", [P, 1])
        bias_o = pool.sbuf("bias_o", [P, 1])
        mask = pool.sbuf("mask", [P, 2 * P])
        h_hi = [pool.sbuf(f"h_hi{p}", [P, PAIR], F32R) for p in range(2)]
        h_lo = [pool.sbuf(f"h_lo{p}", [P, PAIR], F32R) for p in range(2)]
        Q = [pool.sbuf(f"Q{p}", [P, JS, PAIR]) for p in range(2)]
        K = [[pool.sbuf(f"K{p}{h}", [P, JS, PAIR]) for h in range(2)] for p in range(2)]
        V = [[pool.sbuf(f"V{p}{t}", [P, HK]) for t in range(4)] for p in range(2)]
        probs = [pool.sbuf(f"probs{p}", [P, 6 * P]) for p in range(2)]
        least = [pool.sbuf(f"least{p}", [P, 4]) for p in range(2)]
        sums = [pool.sbuf(f"sums{p}", [P, 4]) for p in range(2)]
        inverse = [pool.sbuf(f"inverse{p}", [P, 4]) for p in range(2)]
        probsT = [pool.sbuf(f"probsT{p}", [P, 6 * P]) for p in range(2)]
        O = pool.sbuf("O", [P, JS, PAIR])
        c_hi = pool.sbuf("c_hi", [P, PAIR], F32R)
        c_lo = pool.sbuf("c_lo", [P, PAIR], F32R)
        hidden = pool.sbuf("hidden", [P, FS, PAIR])

        score_ps = [pool.bank(f"score{b}") for b in range(2)]
        turn_ps = [pool.bank(f"turn{b}") for b in range(2)]
        head_ps = pool.bank("head")
        piece_ps = [pool.bank(f"piece{b}") for b in range(2)]
        sum_ps = pool.bank("sum")

        bias_in = pool.sem("bias_in")
        zeroed = pool.sem("zeroed")
        K_zeroed = pool.sem("K_zeroed")
        bias_turned = pool.sem("bias_turned")
        setup_done = pool.sem("setup_done")
        weights_in = pool.sem("weights_in")
        split_qk = pool.sem("split_qk")
        split_v = pool.sem("split_v")
        split_1 = pool.sem("split_1")
        moved_o = pool.sem("moved_o")
        moved_2 = pool.sem("moved_2")
        hi_made = pool.sem("hi_made")
        bias_o_run = pool.sem("bias_o_run")
        bias_o_made = pool.sem("bias_o_made")
        h_hi_made = pool.sem("h_hi_made")
        h_lo_made = pool.sem("h_lo_made")
        pieces = pool.sem("pieces")
        piece_free = [pool.sem(f"piece_free{b}") for b in range(2)]
        scored = pool.sem("scored")
        masked = pool.sem("masked")
        exped = pool.sem("exped")
        inverted = pool.sem("inverted")
        normed = pool.sem("normed")
        turned = pool.sem("turned")
        turned_out = [pool.sem(f"turned_out{b}") for b in range(2)]
        headed = pool.sem("headed")
        O_made = pool.sem("O_made")
        projected = pool.sem("projected")
        h1_made = pool.sem("h1_made")
        c_hi_made = pool.sem("c_hi_made")
        c_lo_made = pool.sem("c_lo_made")
        fed = pool.sem("fed")
        h2_made = pool.sem("h2_made")
        block = ctx.enter_context(nc.Block())

        def wait_piece(eng, base, at):
            eng.wait_ge(pieces, base * 2 + (at + 1))

        def wait_copied(eng, base, at):
            eng.wait_ge(piece_free[at % 2], base + (at // 2 + 1))

        def wait_projection(eng, g, kind):
            if known(g, 0):
                wait_copied(eng, 0, PROJ.index(kind))
            else:
                wait_copied(eng, piece_base(g - 1), position(kind, not known(g, 1)))

        def stream(eng, pair):
            pair(0, 0, "start", 0)
            with eng.Fori(0, L - 1) as layer:
                with eng.Fori(0, PAIRS // 2 - 1) as r:
                    pair(layer, layer * PAIRS + r * 2 + 1, "", 1)
                    pair(layer, layer * PAIRS + r * 2 + 2, "", 0)
                pair(layer, layer * PAIRS + PAIRS - 1, "last", 1)
                pair(layer + 1, layer * PAIRS + PAIRS, "first", 0)
            with eng.Fori(0, PAIRS // 2 - 1) as r:
                pair(L - 1, r * 2 + (TOTAL - PAIRS + 1), "", 1)
                pair(L - 1, r * 2 + (TOTAL - PAIRS + 2), "", 0)
            pair(L - 1, TOTAL - 1, "end", 1)

        PARTS = [(0, 2 * P), (2 * P, 4 * P), (4 * P, 5 * P), (5 * P, 6 * P)]

        @block.sync
        def _(sp):
            n = JS * L
            for at, b in enumerate((bq, bk, bv, b1)):
                sp.dma_start(bias_rows[at * n:(at + 1) * n, :],
                             b.rearrange("l (j p) -> (l j) p", p=P)).then_inc(bias_in, DMA)
            for at, b in enumerate((bo, b2)):
                sp.dma_start(bias_rows[4 * n + at * L:4 * n + (at + 1) * L, :], b).then_inc(bias_in, DMA)

            def load(layer):
                for name, w in (("q", Wq), ("k", Wk), ("v", Wv), ("1", W1)):
                    sp.dma_start(raw[name][:, :], w[bass.ds(layer, 1), :, :].rearrange("l p n -> p (l n)"))\
                      .then_inc(weights_in, DMA)
                for name, w in (("o", Wo), ("2", W2)):
                    sp.dma_start(raw[name][:, :].rearrange("p (j d) -> p j d", d=P),
                                 w[bass.ds(layer, 1), :, :].rearrange("l (j p) d -> p (l j) d", p=P))\
                      .then_inc(weights_in, DMA)

            load(0)
            with sp.Fori(1, L) as layer:
                sp.wait_ge(split_1, layer)
                sp.wait_ge(moved_2, layer)
                load(layer)

        @block.gpsimd
        def _(gp):
            gp.memset(mask[:, :], 0.0).then_inc(zeroed, 1)
            gp.wait_ge(zeroed, 1)
            gp.affine_select(out=mask[:, P:2 * P], in_=mask[:, P:2 * P], compare_op=ALU.is_ge,
                             fill=MASKED, base=0, pattern=[[-1, P]], channel_multiplier=1).then_inc(zeroed, 1)
            with gp.Fori(0, TOTAL) as g:
                for k in range(UNITS):
                    count = settled(gp, g * UNITS + (k + 1))
                    gp.wait_ge(zeroed, 2)
                    gp.wait_ge(inverted, count)
                    for q, (a, b) in enumerate(PARTS):
                        gp.tensor_scalar(probs[k % 2][:, a:b], probs[k % 2][:, a:b],
                                         inverse[k % 2][:, q:q + 1], 1.0, ALU.mult, ALU.mult)\
                          .then_inc(normed, 1)

        @block.tensor
        def _(pe):
            def three_passes(out, lhs_hi, lhs_lo, rhs_hi, rhs_lo):
                pe.matmul(out, lhs_hi, rhs_hi, start=True, stop=False)
                pe.matmul(out, lhs_hi, rhs_lo, start=False, stop=False)
                return pe.matmul(out, lhs_lo, rhs_hi, start=False, stop=True)

            def piece(kind, at, base, parity, first=False):
                if not first:
                    pe.wait_ge(piece_free[at % 2], base + at // 2)
                bank = piece_ps[at % 2][:, :]
                name, n = kind
                if name == "v":
                    cols = slice(n * P, (n + 1) * P)
                    last = three_passes(bank, h_hi[parity][:, cols], h_lo[parity][:, cols],
                                        w_hi["v"][:, :], w_lo["v"][:, :])
                else:
                    cols = slice(n * P, (n + 1) * P)
                    hi, lo = (c_hi, c_lo) if name == "f" else (h_hi[parity], h_lo[parity])
                    w = "1" if name == "f" else name
                    last = three_passes(bank, w_hi[w][:, cols], w_lo[w][:, cols], hi[:, :], lo[:, :])
                last.then_inc(pieces, 1)

            def scores(g, k, parity):
                j, s = k // 2, k % 2 * SEQ
                unit = g * UNITS + k
                if s == 0:
                    wait_projection(pe, g, ("k", j))
                    wait_projection(pe, g, ("q", j))
                if not (known(g, 0) and k == 0):
                    pe.wait_ge(masked, unit * 4)
                early, late = Q[parity][:, j, s:s + P], Q[parity][:, j, s + P:s + SEQ]
                for h in range(2):
                    pe_last = pe.matmul(score_ps[0][:, h * SEQ:(h + 1) * SEQ], late,
                                        K[parity][h][:, j, s:s + SEQ], start=True, stop=True)
                pe_last.then_inc(scored, 1)
                for h in range(2):
                    pe_last = pe.matmul(score_ps[1][:, h * P:(h + 1) * P], early,
                                        K[parity][h][:, j, s:s + P], start=True, stop=True)
                pe_last.then_inc(scored, 1)

            def turn(g, k):
                unit = g * UNITS + k
                own = probs[k % 2]
                pe.wait_ge(normed, unit * 4 + 2)
                if not (known(g, 0) and k == 0):
                    pe.wait_ge(turned_out[1], unit)
                for h in range(2):
                    last = pe.transpose(turn_ps[1][:, h * P:(h + 1) * P],
                                        own[:, h * SEQ + P:(h + 1) * SEQ], ident[:, :])
                last.then_inc(turned, 1)
                if not (known(g, 0) and k == 0):
                    pe.wait_ge(turned_out[0], unit)
                for h in range(2):
                    pe.transpose(turn_ps[0][:, h * SEQ + P:(h + 1) * SEQ],
                                 own[:, h * SEQ:h * SEQ + P], ident[:, :])
                pe.wait_ge(normed, unit * 4 + 4)
                for h in range(2):
                    last = pe.transpose(turn_ps[0][:, h * SEQ:h * SEQ + P],
                                        own[:, (4 + h) * P:(5 + h) * P], ident[:, :])
                last.then_inc(turned, 1)

            def values(g, k, parity):
                j, s = k // 2, k % 2
                unit = g * UNITS + k
                if k < 2:
                    wait_projection(pe, g, ("v", 2 * s))
                    wait_projection(pe, g, ("v", 2 * s + 1))
                if s == 0 and not (known(g, 0) and k == 0):
                    pe.wait_ge(O_made, g * JS + j)
                pe.wait_ge(turned_out[1], unit + 1)
                pe.wait_ge(turned_out[0], unit + 1)
                PT = probsT[k % 2]
                at = s * SEQ
                for h in range(2):
                    cols = slice((2 * j + h) * HEAD, (2 * j + h + 1) * HEAD)
                    pe.matmul(head_ps[h * HEAD:(h + 1) * HEAD, at:at + SEQ], V[parity][2 * s][:, cols],
                              PT[:, h * SEQ:(h + 1) * SEQ], start=True, stop=False)
                for h in range(2):
                    cols = slice((2 * j + h) * HEAD, (2 * j + h + 1) * HEAD)
                    last = pe.matmul(head_ps[h * HEAD:(h + 1) * HEAD, at + P:at + SEQ],
                                     V[parity][2 * s + 1][:, cols], PT[:, (4 + h) * P:(5 + h) * P],
                                     start=False, stop=True)
                if s == 1:
                    last.then_inc(headed, 1)

            def output_projection(g, sets, js):
                for j in js:
                    if j == 0:
                        pe.wait_ge(moved_o, sets)
                        pe.wait_ge(bias_o_made, sets)
                        pe.wait_ge(h2_made, g + PAIRS)
                    pe.wait_ge(O_made, g * JS + (j + 1))
                    last = pe.matmul(sum_ps[:, :], w_whole["o"][:, j * P:(j + 1) * P], O[:, j, :],
                                     start=(j == 0), stop=(j == JS - 1))
                if js[-1] == JS - 1:
                    last.then_inc(projected, 1)

            def run_bias_o(sets):
                pe.wait_ge(moved_o, sets)
                pe.wait_ge(split_qk, sets)
                for j in range(JS):
                    last = pe.matmul(sum_ps[:, 0:1], w_whole["o"][:, j * P:(j + 1) * P], bias_qkv[:, 2, j:j + 1],
                                     start=(j == 0), stop=(j == JS - 1))
                last.then_inc(bias_o_run, 1)

            def feed_sum(g, sets, fs, base, first_at):
                for f in fs:
                    if f == 0:
                        pe.wait_ge(h1_made, g + 1)
                        pe.wait_ge(moved_2, sets)
                    wait_copied(pe, base, first_at + f)
                    last = pe.matmul(sum_ps[:, :], w_whole["2"][:, f * P:(f + 1) * P], hidden[:, f, :],
                                     start=(f == 0), stop=(f == FS - 1))
                if fs[-1] == FS - 1:
                    last.then_inc(fed, 1)

            def wait_c(g):
                pe.wait_ge(c_hi_made, g + 1)
                pe.wait_ge(c_lo_made, g + 1)

            def wait_h(g):
                pe.wait_ge(h_hi_made, g + 1)
                pe.wait_ge(h_lo_made, g + 1)

            pe.wait_ge(bias_in, 6 * DMA)
            pe.transpose(sum_ps[:, 0:N_BIAS], bias_rows[:, :], ident[0:N_BIAS, 0:N_BIAS]).then_inc(bias_turned, 1)
            pe.wait_ge(K_zeroed, 4)
            run_bias_o(1)
            wait_h(0)
            pe.wait_ge(split_v, 1)
            for at, kind in enumerate(PROJ):
                piece(kind, at, 0, 0, first=at < 2)

            def pair(layer, g, place, parity):
                has_prev, has_next = place != "start", place != "end"
                base = piece_base(g)
                old_sets = layer + (0 if place == "first" else 1)
                new_sets = layer + (2 if place == "last" else 1)
                at = 0
                if has_next:
                    wait_h(g + 1)
                for k in range(UNITS):
                    run = pieces_of(k, has_prev, has_next)
                    scores(g, k, parity)
                    if run:
                        if run[0] == FEED[0]:
                            wait_c(g - 1)
                            pe.wait_ge(split_1, old_sets)
                        elif run[0] == PROJ[0]:
                            pe.wait_ge(split_qk, new_sets)
                        elif run[0] == PROJ[EARLY - 2]:
                            pe.wait_ge(split_v, new_sets)
                        piece(run[0], at, base, 1 - parity)
                        at += 1
                    if k > 0:
                        turn(g, k - 1)
                    elif has_prev:
                        turn(g - 1, UNITS - 1)
                    if has_prev:
                        if k in (2, 3):
                            output_projection(g - 1, old_sets, [2 * (k - 2), 2 * (k - 2) + 1])
                        if k == 6 and place == "first":
                            pe.wait_ge(bias_o_made, layer + 1)
                        if k in (6, 7):
                            feed_sum(g - 1, old_sets, [2 * (k - 6), 2 * (k - 6) + 1], base, EARLY if has_next else 0)
                    if k >= 2:
                        values(g, k - 2, parity)
                    elif has_prev:
                        values(g - 1, UNITS - 2 + k, 1 - parity)
                    if run:
                        piece(run[1], at, base, 1 - parity)
                        at += 1
                    if k == 5 and place == "first":
                        run_bias_o(layer + 1)

            stream(pe, pair)
            g, sets = TOTAL - 1, L
            turn(g, UNITS - 1)
            values(g, UNITS - 2, 1)
            values(g, UNITS - 1, 1)
            output_projection(g, sets, list(range(JS)))
            wait_c(g)
            drain_base = piece_base(g) + FS // 2
            for f in range(FS):
                piece(FEED[f], f, drain_base, 1)
            feed_sum(g, sets, list(range(FS)), drain_base, 0)

        @block.vector
        def _(dve):
            def take_piece(kind, at, base, parity):
                name, n = kind
                bank = piece_ps[at % 2]
                if name == "k":
                    wait_piece(dve, base, at)
                    dve.tensor_scalar(K[parity][0][0:HEAD, n, :], bank[0:HEAD, :], bias_qkv[0:HEAD, 1, n:n + 1],
                                      None, ALU.add)
                    dve.tensor_scalar(K[parity][1][HEAD:P, n, :], bank[HEAD:P, :], bias_qkv[HEAD:P, 1, n:n + 1],
                                      None, ALU.add).then_inc(piece_free[at % 2], 1)
                elif kind == ("v", 3):
                    wait_piece(dve, base, at)
                    dve.tensor_copy(V[parity][n][:, :], bank[:, :]).then_inc(piece_free[at % 2], 1)
                elif name == "f" and n % 2 == 1:
                    wait_piece(dve, base, at)
                    dve.tensor_scalar(hidden[:, n, :], bank[:, :], bias_1[:, n:n + 1], 0.0, ALU.add, ALU.max)\
                       .then_inc(piece_free[at % 2], 1)

            def mask_scores(g, k):
                unit = g * UNITS + k
                for q, (a, b) in enumerate(PARTS):
                    if q % 2 == 0:
                        count = settled(dve, unit * 2 + (q // 2 + 1))
                        dve.wait_ge(zeroed, 2)
                        dve.wait_ge(scored, count)
                    bank = score_ps[q // 2]
                    width = b - a
                    own = q % 2 * width
                    dve.tensor_tensor_reduce(
                        out=probs[k % 2][:, a:b], in0=bank[:, own:own + width], in1=mask[:, 2 * P - width:2 * P],
                        scale=SCALE, scalar=3.0e38, op0=ALU.add, op1=ALU.min,
                        accum_out=least[k % 2][:, q:q + 1]).then_inc(masked, 1)

            def invert(g, k):
                unit = g * UNITS + k
                dve.wait_ge(exped, unit * 4 + 4)
                dve.reciprocal(inverse[k % 2][:, :], sums[k % 2][:, :]).then_inc(inverted, 1)

            def take_turned(g, k):
                unit = g * UNITS + k
                dve.wait_ge(turned, unit * 2 + 2)
                dve.tensor_copy(probsT[k % 2][:, 0:4 * P], turn_ps[0][:, :]).then_inc(turned_out[0], 1)

            def take_heads(g, j):
                dve.wait_ge(headed, g * JS + (j + 1))
                dve.tensor_copy(O[:, j, :], head_ps[:, :]).then_inc(O_made, 1)

            def residual_1(g):
                h = residual(g)
                dve.wait_ge(projected, g + 1)
                dve.scalar_tensor_tensor(out=h, in0=sum_ps[:, :], scalar=bias_o[:, 0:1], in1=h,
                                         op0=ALU.add, op1=ALU.add).then_inc(h1_made, 1)

            def split_c(g):
                dve.wait_ge(c_hi_made, g + 1)
                dve.tensor_tensor(c_lo[:, :], residual(g), c_hi[:, :].bitcast(F32),
                                  ALU.subtract).then_inc(c_lo_made, 1)

            def residual_2(g):
                h = residual(g)
                dve.wait_ge(fed, g + 1)
                dve.scalar_tensor_tensor(out=h, in0=sum_ps[:, :], scalar=bias_2[:, 0:1], in1=h,
                                         op0=ALU.add, op1=ALU.add).then_inc(h2_made, 1)

            def split_h(g, parity):
                dve.wait_ge(h_hi_made, g + 1)
                dve.tensor_tensor(h_lo[parity][:, :], residual(g),
                                  h_hi[parity][:, :].bitcast(F32), ALU.subtract).then_inc(h_lo_made, 1)

            n_j = JS * L
            by_kind = biasT[:, 0:4 * n_j].rearrange("p (t n) -> p t n", t=4)

            def split(layer, name):
                order = list(w_hi).index(name)
                dve.tensor_copy(w_hi[name][:, :], raw[name][:, :]).then_inc(hi_made, 1)
                dve.wait_ge(hi_made, layer * len(w_hi) + (order + 1))
                return dve.tensor_tensor(w_lo[name][:, :], raw[name][:, :], w_hi[name][:, :].bitcast(F32),
                                         ALU.subtract)

            def change_qk(layer, last_read=None):
                dve.wait_ge(weights_in, layer * (6 * DMA) + 6 * DMA)
                if last_read:
                    wait_copied(dve, *last_read)
                dve.tensor_copy(bias_qkv[:, :, :], by_kind[:, 0:3, bass.ds(layer * JS, JS)])
                split(layer, "q")
                split(layer, "k").then_inc(split_qk, 1)
                dve.wait_ge(split_qk, layer + 1)

            def change_v(layer):
                split(layer, "v").then_inc(split_v, 1)

            def change_1(layer, last_read=None):
                if last_read:
                    wait_copied(dve, *last_read)
                dve.tensor_copy(bias_1[:, :], by_kind[:, 3, bass.ds(layer * JS, JS)])
                dve.tensor_copy(bias_2[:, :], columns(biasT, layer + (4 * n_j + L), 1))
                split(layer, "1").then_inc(split_1, 1)
                dve.wait_ge(split_1, layer + 1)

            def make_bias_o(layer):
                dve.wait_ge(bias_o_run, layer + 1)
                dve.tensor_tensor(bias_o[:, :], sum_ps[:, 0:1], columns(biasT, layer + 4 * n_j, 1), ALU.add)\
                   .then_inc(bias_o_made, 1)
                dve.wait_ge(bias_o_made, layer + 1)

            for p in range(2):
                dve.memset(K[p][0][HEAD:P, :, :], 0.0).then_inc(K_zeroed, 1)
                dve.memset(K[p][1][0:HEAD, :, :], 0.0).then_inc(K_zeroed, 1)
            dve.memset(bias_o[:, :], 0.0).then_inc(h2_made, PAIRS)
            dve.wait_ge(h2_made, PAIRS)
            dve.wait_ge(K_zeroed, 4)
            dve.wait_ge(zeroed, 2)
            dve.wait_ge(bias_turned, 1)
            dve.tensor_copy(biasT[:, :], sum_ps[:, 0:N_BIAS]).then_inc(setup_done, 1)
            dve.wait_ge(setup_done, 1)
            change_qk(0)
            for g in range(2):
                split_h(g, g)
            change_v(0)
            change_1(0)
            make_bias_o(0)
            for at, kind in enumerate(PROJ):
                take_piece(kind, at, 0, 0)

            def pair(layer, g, place, parity):
                has_prev, has_next = place != "start", place != "end"
                base = piece_base(g)
                at = 0
                if place == "last":
                    change_qk(layer + 1, last_read=(piece_base(g - 1), PROJ.index(("q", JS - 1))))
                for k in range(UNITS):
                    run = pieces_of(k, has_prev, has_next)
                    mask_scores(g, k)
                    if run:
                        take_piece(run[0], at, base, 1 - parity)
                        at += 1
                    if k > 0:
                        take_turned(g, k - 1)
                    elif has_prev:
                        take_turned(g - 1, UNITS - 1)
                    invert(g, k)
                    if k == 1 and place == "last":
                        change_v(layer + 1)
                    if k == 3 and has_prev:
                        residual_1(g - 1)
                    if k == 4 and has_prev:
                        split_c(g - 1)
                    if k == 5 and has_next:
                        split_h(g + 2, parity)
                    if k % 2 == 1:
                        if k >= 3:
                            take_heads(g, (k - 3) // 2)
                        elif has_prev:
                            take_heads(g - 1, JS - 1)
                    if run:
                        take_piece(run[1], at, base, 1 - parity)
                        at += 1
                    if k == 5 and place == "first":
                        make_bias_o(layer)
                    if k == 7 and has_prev:
                        residual_2(g - 1)
                if place == "first":
                    dve.wait_ge(h2_made, g + PAIRS)
                    change_1(layer, last_read=(base, EARLY + 2))

            stream(dve, pair)
            g = TOTAL - 1
            take_turned(g, UNITS - 1)
            take_heads(g, JS - 1)
            residual_1(g)
            split_c(g)
            drain_base = piece_base(g) + FS // 2
            for f in range(FS):
                take_piece(FEED[f], f, drain_base, 1)
            residual_2(g)

        @block.scalar
        def _(act):
            def take_piece(kind, at, base, parity):
                name, n = kind
                bank = piece_ps[at % 2]
                if name == "q":
                    wait_piece(act, base, at)
                    act.activation(Q[parity][:, n, :], bank[:, :], ACT.Identity, bias=bias_qkv[:, 0, n:n + 1])\
                       .then_inc(piece_free[at % 2], 1)
                elif name == "v" and n < 3:
                    wait_piece(act, base, at)
                    act.activation(V[parity][n][:, :], bank[:, :], ACT.Copy).then_inc(piece_free[at % 2], 1)
                elif name == "f" and n % 2 == 0:
                    wait_piece(act, base, at)
                    act.activation(hidden[:, n, :], bank[:, :], ACT.Relu, bias=bias_1[:, n:n + 1])\
                       .then_inc(piece_free[at % 2], 1)

            def exponentials(g, k):
                unit = g * UNITS + k
                for q, (a, b) in enumerate(PARTS):
                    act.wait_ge(masked, unit * 4 + (q + 1))
                    own = probs[k % 2][:, a:b]
                    act.activation(own, own, ACT.Exp, bias=least[k % 2][:, q:q + 1], scale=-1.0,
                                   accum_out=sums[k % 2][:, q:q + 1]).then_inc(exped, 1)

            def take_turned(g, k):
                unit = g * UNITS + k
                act.wait_ge(turned, unit * 2 + 1)
                act.activation(probsT[k % 2][:, 4 * P:6 * P], turn_ps[1][:, 0:2 * P], ACT.Copy)\
                   .then_inc(turned_out[1], 1)

            def split_c(g):
                act.wait_ge(h1_made, g + 1)
                act.activation(c_hi[:, :], residual(g), ACT.Copy).then_inc(c_hi_made, 1)

            def split_h(g, parity):
                act.wait_ge(h2_made, g + 1)
                act.activation(h_hi[parity][:, :], residual(g), ACT.Copy).then_inc(h_hi_made, 1)

            def move(layer, name, moved):
                act.activation(w_whole[name][:, :], raw[name][:, :], ACT.Copy).then_inc(moved, 1)

            act.wait_ge(weights_in, 6 * DMA)
            move(0, "o", moved_o)
            for g in range(2):
                split_h(g, g)
            move(0, "2", moved_2)
            for at, kind in enumerate(PROJ):
                take_piece(kind, at, 0, 0)

            def pair(layer, g, place, parity):
                has_prev, has_next = place != "start", place != "end"
                base = piece_base(g)
                at = 0
                for k in range(UNITS):
                    run = pieces_of(k, has_prev, has_next)
                    if k == 4 and has_prev:
                        split_c(g - 1)
                    exponentials(g, k)
                    if run:
                        take_piece(run[0], at, base, 1 - parity)
                        at += 1
                    if k > 0:
                        take_turned(g, k - 1)
                    elif has_prev:
                        take_turned(g - 1, UNITS - 1)
                    if k == 4 and has_next:
                        split_h(g + 2, parity)
                    if k == 4 and place == "first":
                        act.wait_ge(weights_in, layer * (6 * DMA) + 6 * DMA)
                        act.wait_ge(projected, g)
                        move(layer, "o", moved_o)
                    if run:
                        take_piece(run[1], at, base, 1 - parity)
                        at += 1
                if place == "first":
                    act.wait_ge(fed, g)
                    move(layer, "2", moved_2)

            stream(act, pair)
            g = TOTAL - 1
            take_turned(g, UNITS - 1)
            split_c(g)
            drain_base = piece_base(g) + FS // 2
            for f in range(FS):
                take_piece(FEED[f], f, drain_base, 1)


class Skewed:

    def __init__(self, pairs, unroll, depth):
        self.pairs, self.unroll, self.depth = pairs, unroll, depth

    def run(self, eng, step):
        head = -(-self.depth // self.unroll) * self.unroll
        for i in range(head):
            step(i, i % self.unroll)
        with eng.Fori(head // self.unroll, self.pairs // self.unroll) as r:
            for u in range(self.unroll):
                step(r * self.unroll + u, u)
        for i in range(self.pairs, self.pairs + self.depth):
            step(i, i % self.unroll)

    def has(self, i, lag, back=0):
        return not isinstance(i, int) or back <= i - lag < self.pairs


def norm_stage(nc, prefix, hT, X, ident, eps, recurrent=None, gate=None):
    PAIRS = hT.shape[1] // PAIR
    T = PAIR // P
    NORMS = 2 if recurrent else 1
    skew = Skewed(PAIRS, 4, 4 if gate else 2)
    with ExitStack() as ctx:
        pool = Pools(nc, ctx, prefix)
        centre = pool.sbuf("centre", [P, P])
        mean = pool.sbuf("mean", [P, 1])
        ones = pool.sbuf("ones", [P, P])
        eps_of = [pool.sbuf(f"eps{n}", [P, 1]) for n in range(2)]
        c = [pool.sbuf(f"c{u}", [P, PAIR]) for u in range(4)]
        squared = [pool.sbuf(f"squared{p}", [P, PAIR]) for p in range(2)]
        root = [pool.sbuf(f"root{p}", [P, 2 * T]) for p in range(2)]
        inverse = [pool.sbuf(f"inverse{p}", [P, 2 * T]) for p in range(2)]
        diag = [[pool.sbuf(f"diag{n}{p}", [P, PAIR]) for p in range(2)] for n in range(NORMS)]
        x1 = [pool.sbuf(f"x1{p}", [P, PAIR]) for p in range(2)]
        x2 = [pool.sbuf(f"x2{p}", [P, PAIR]) for p in range(2)]
        c_ps = [pool.bank(f"c{p}") for p in range(2)]
        v_ps = [pool.bank(f"v{p}") for p in range(2)]
        spread_ps = [pool.bank(f"spread{n}") for n in range(NORMS)]
        made = pool.sem("made")
        vectors_in = pool.sem("vectors_in")
        centred = pool.sem("centred")
        c_out = pool.sem("c_out")
        squares = pool.sem("squares")
        varied = pool.sem("varied")
        roots = pool.sem("roots")
        inverses = pool.sem("inverses")
        diagonal = [pool.sem(f"diagonal{n}") for n in range(NORMS)]
        spread = [pool.sem(f"spread{n}") for n in range(NORMS)]
        x_made = [pool.sem(f"x_made{n}") for n in range(NORMS)]
        h_added = pool.sem("h_added")
        X_made = pool.sem("X_made")
        if recurrent:
            w_dram, b_dram = recurrent
            w_col = pool.sbuf("w_col", [P, 1])
            b_col = pool.sbuf("b_col", [P, 1])
        if gate:
            gate_w, gate_b, logits = gate
            E = gate_w.shape[1]
            gate_sb = pool.sbuf("gate_sb", [P, E])
            gate_col = pool.sbuf("gate_col", [E, 1])
            rowed = [pool.sbuf(f"rowed{p}", [E, PAIR]) for p in range(2)]
            l_ps = pool.bank("l")
            t_ps = pool.bank("t")
            l_made = pool.sem("l_made")
            l_out = pool.sem("l_out")
            t_made = pool.sem("t_made")
            t_out = pool.sem("t_out")
        block = ctx.enter_context(nc.Block())

        @block.sync
        def _(sp):
            if recurrent:
                sp.dma_start(w_col[:, :], w_dram.rearrange("(p o) -> p o", o=1)).then_inc(vectors_in, DMA)
                sp.dma_start(b_col[:, :], b_dram.rearrange("(p o) -> p o", o=1)).then_inc(vectors_in, DMA)
            if gate:
                sp.dma_start(gate_sb[:, :], gate_w).then_inc(vectors_in, DMA)
                sp.dma_start(gate_col[:, :], gate_b.rearrange("(p o) -> p o", o=1)).then_inc(vectors_in, DMA)

        @block.gpsimd
        def _(gp):
            if recurrent:
                def step(i, u):
                    if skew.has(i, 2):
                        gp.wait_ge(x_made[0], i - 1)
                        h = columns(hT, (i - 2) * PAIR, PAIR)
                        gp.tensor_tensor(h, h, x1[u % 2][:, :], ALU.add).then_inc(h_added, 1)

                skew.run(gp, step)

        @block.tensor
        def _(pe):
            pe.wait_ge(made, 5)
            pe.wait_ge(vectors_in, 2 * DMA)

            def step(i, u):
                p = u % 2
                if skew.has(i, 0):
                    if skew.has(i, 0, 2):
                        pe.wait_ge(c_out, i - 1)
                    pe.matmul(c_ps[p][:, :], centre[:, :], columns(hT, i * PAIR, PAIR),
                              start=True, stop=True).then_inc(centred, 1)
                if skew.has(i, 2):
                    for n in range(NORMS):
                        if skew.has(i, 2, 1):
                            pe.wait_ge(x_made[n], i - 2)
                        pe.wait_ge(diagonal[n], i - 1)
                        pe.matmul(spread_ps[n][:, :], ones[:, :], diag[n][p][:, :],
                                  start=True, stop=True).then_inc(spread[n], 1)
                if skew.has(i, 1):
                    if skew.has(i, 1, 2):
                        pe.wait_ge(roots, i - 2)
                    pe.wait_ge(squares, i)
                    for t in range(T):
                        last = pe.matmul(v_ps[1 - p][:, t:t + 1], squared[1 - p][:, t * P:(t + 1) * P],
                                         mean[:, :], start=True, stop=True)
                    last.then_inc(varied, 1)
                if gate and skew.has(i, 3):
                    if skew.has(i, 3, 1):
                        pe.wait_ge(l_out, i - 3)
                    pe.wait_ge(x_made[0], i - 2)
                    pe.matmul(l_ps[0:E, :], gate_sb[:, :], columns(X, (i - 3) * PAIR, PAIR),
                              start=True, stop=True).then_inc(l_made, 1)
                if gate and skew.has(i, 4):
                    count = settled(pe, i - 3)
                    count_out = settled(pe, i - 4)
                    pe.wait_ge(vectors_in, 2 * DMA)
                    if skew.has(i, 4, 1):
                        pe.wait_ge(t_out, count_out)
                    pe.wait_ge(l_out, count)
                    for t in range(T):
                        last = pe.transpose(t_ps[:, t * E:(t + 1) * E], rowed[p][:, t * P:(t + 1) * P],
                                            ident[0:E, 0:E])
                    last.then_inc(t_made, 1)

            skew.run(pe, step)

        @block.vector
        def _(dve):
            dve.memset(mean[:, :], 1.0 / P).then_inc(made, 1)
            dve.memset(ones[:, :], 1.0).then_inc(made, 1)
            dve.memset(eps_of[0][:, :], eps).then_inc(made, 1)
            dve.memset(eps_of[1][:, :], eps * eps).then_inc(made, 1)
            dve.tensor_scalar(centre[:, :], ident[:, :], 1.0 / P, None, ALU.subtract).then_inc(made, 1)

            def step(i, u):
                p = u % 2
                if skew.has(i, 2):
                    x_to = [x1[p][:, :] if recurrent else columns(X, (i - 2) * PAIR, PAIR), x2[p][:, :]]
                    if recurrent and skew.has(i, 2, 2):
                        dve.wait_ge(h_added, i - 3)
                        dve.wait_ge(X_made, i - 3)
                    for n in range(NORMS):
                        dve.wait_ge(spread[n], i - 1)
                        dve.tensor_tensor(x_to[n], spread_ps[n][:, :], c[(u + 2) % 4][:, :], ALU.mult)\
                           .then_inc(x_made[n], 1)
                if skew.has(i, 0):
                    dve.wait_ge(centred, i + 1)
                    if skew.has(i, 0, 4):
                        dve.wait_ge(squares, i - 3)
                        for n in range(NORMS):
                            dve.wait_ge(x_made[n], i - 3)
                    dve.tensor_copy(c[u][:, :], c_ps[p][:, :]).then_inc(c_out, 1)
                if skew.has(i, 1):
                    dve.wait_ge(roots, i)
                    if skew.has(i, 1, 2):
                        for n in range(NORMS):
                            dve.wait_ge(diagonal[n], i - 2)
                    dve.reciprocal(inverse[1 - p][:, 0:NORMS * T], root[1 - p][:, 0:NORMS * T]).then_inc(inverses, 1)
                    dve.wait_ge(inverses, i)
                    if skew.has(i, 1, 2):
                        dve.wait_ge(spread[0], i - 2)
                    for t in range(T):
                        last = dve.tensor_scalar(diag[0][1 - p][:, t * P:(t + 1) * P], ident[:, :],
                                                 inverse[1 - p][:, t:t + 1], None, ALU.mult)
                    last.then_inc(diagonal[0], 1)
                if gate and skew.has(i, 4):
                    dve.wait_ge(t_made, i - 3)
                    dve.tensor_copy(logits[:, bass.ds((i - 4) * (T * E), T * E)], t_ps[:, 0:T * E])\
                       .then_inc(t_out, 1)

            skew.run(dve, step)

        @block.scalar
        def _(act):
            act.wait_ge(made, 5)
            act.wait_ge(vectors_in, 2 * DMA)

            def step(i, u):
                p = u % 2
                if skew.has(i, 1):
                    act.wait_ge(varied, i)
                    if skew.has(i, 1, 2):
                        act.wait_ge(inverses, i - 2)
                    for n in range(NORMS):
                        last = act.activation(root[1 - p][:, n * T:(n + 1) * T], v_ps[1 - p][:, 0:T], ACT.Sqrt,
                                              bias=eps_of[n][:, :], scale=1.0 + n * eps)
                    last.then_inc(roots, 1)
                if skew.has(i, 0):
                    act.wait_ge(c_out, i + 1)
                    if skew.has(i, 0, 2):
                        act.wait_ge(varied, i - 1)
                    act.activation(squared[p][:, :], c[u][:, :], ACT.Square).then_inc(squares, 1)
                if recurrent and skew.has(i, 1):
                    act.wait_ge(inverses, i)
                    if skew.has(i, 1, 2):
                        act.wait_ge(spread[1], i - 2)
                    for t in range(T):
                        last = act.activation(diag[1][1 - p][:, t * P:(t + 1) * P], ident[:, :], ACT.Copy,
                                              scale=inverse[1 - p][:, T + t:T + t + 1])
                    last.then_inc(diagonal[1], 1)
                if recurrent and skew.has(i, 2):
                    act.wait_ge(x_made[1], i - 1)
                    act.activation(columns(X, (i - 2) * PAIR, PAIR), x2[p][:, :], ACT.Identity,
                                   bias=b_col[:, :], scale=w_col[:, :]).then_inc(X_made, 1)
                if gate and skew.has(i, 3):
                    act.wait_ge(l_made, i - 2)
                    if skew.has(i, 3, 2):
                        act.wait_ge(t_made, i - 4)
                    act.activation(rowed[1 - p][:, :], l_ps[0:E, :], ACT.Identity, bias=gate_col[:, :])\
                       .then_inc(l_out, 1)

            skew.run(act, step)


def recurrent_stage(nc, hT, X, ident, weights):
    W_in, conv_w, conv_b, nu_log, theta_log, gamma_log, B_re, B_im, C_re, C_im, W_out, b_out = weights
    N = B_re.shape[0]
    TAPS = conv_w.shape[2]
    BEFORE = (TAPS - 1) // 2
    PADDED = SEQ + TAPS - 1
    PAIRS = hT.shape[1] // PAIR
    TWO_PI_HI = 6.28125
    TWO_PI_LO = 0.0019353071795864769
    skew = Skewed(PAIRS, 4, 3)
    with ExitStack() as ctx:
        pool = Pools(nc, ctx, "rec")
        w_in = pool.sbuf("w_in", [P, P])
        w_inT = pool.sbuf("w_inT", [P, P])
        w_out = pool.sbuf("w_out", [P, N])
        w_outT = pool.sbuf("w_outT", [P, P])
        B = pool.sbuf("B", [P, N])
        BT = pool.sbuf("BT", [N, P])
        conv = pool.sbuf("conv", [N, N, TAPS])
        conv_bias = pool.sbuf("conv_bias", [N, 1])
        taps = [pool.sbuf(f"taps{t}", [P, P]) for t in range(3)]
        C_rows = [pool.sbuf(f"C_rows{t}", [N, P]) for t in range(2)]
        C_cos = pool.sbuf("C_cos", [P, N])
        C_sin = pool.sbuf("C_sin", [P, N])
        out_bias = pool.sbuf("out_bias", [P, 1])
        nu = pool.sbuf("nu", [P, 1])
        theta = pool.sbuf("theta", [P, 1])
        gamma = pool.sbuf("gamma", [P, 1])
        tiny = [pool.sbuf(f"tiny{t}", [P, 1]) for t in range(8)]
        turns_i = pool.sbuf("turns_i", [P, 1], I32)
        sign = pool.sbuf("sign", [P, 1])
        cos = pool.sbuf("cos", [P, 2, SEQ])
        sin = pool.sbuf("sin", [P, 2, SEQ])
        part = [pool.sbuf(f"part{t}", [P, SEQ]) for t in range(2)]
        decay = pool.sbuf("decay", [P, 2, SEQ])
        bias_B = pool.sbuf("bias_B", [P, 1])
        bias_im = pool.sbuf("bias_im", [P, 1])
        bias_re = pool.sbuf("bias_re", [P, 1])

        v_pad = [pool.sbuf(f"v_pad{u}", [P, 2, PADDED]) for u in range(2)]
        gated = [pool.sbuf(f"gated{u}", [N, PAIR]) for u in range(4)]
        Bv = [pool.sbuf(f"Bv{u}", [P, PAIR]) for u in range(2)]
        Bv_turned = [pool.sbuf(f"Bv_turned{u}", [P, PAIR]) for u in range(2)]
        drive_c = pool.sbuf("drive_c", [P, PAIR])
        drive_s = [pool.sbuf(f"drive_s{u}", [P, PAIR]) for u in range(2)]
        drive = pool.sbuf("drive", [P, PAIR])
        state = [pool.sbuf(f"state{u}", [P, PAIR]) for u in range(2)]
        state_c = [pool.sbuf(f"state_c{u}", [P, PAIR]) for u in range(2)]
        state_s = [pool.sbuf(f"state_s{u}", [P, PAIR]) for u in range(2)]
        product = [pool.sbuf(f"product{u}", [P, PAIR]) for u in range(2)]
        in_ps = [pool.bank(f"in{u}") for u in range(2)]
        B_ps = [pool.bank(f"B{u}") for u in range(2)]
        y_ps = [pool.bank(f"y{u}") for u in range(2)]
        o_ps = [pool.bank(f"o{u}") for u in range(2)]

        loaded = pool.sem("loaded")
        exped = pool.sem("exped")
        chain = pool.sem("chain")
        sined = pool.sem("sined")
        folded = pool.sem("folded")
        angles = pool.sem("angles")
        tabled = pool.sem("tabled")
        zeroed = pool.sem("zeroed")
        projected = pool.sem("projected")
        gelued = pool.sem("gelued")
        v_low = pool.sem("v_low")
        v_high = pool.sem("v_high")
        driven = pool.sem("driven")
        Bv_made = pool.sem("Bv_made")
        cos_made = pool.sem("cos_made")
        sin_made = pool.sem("sin_made")
        drive_made = pool.sem("drive_made")
        scanned = pool.sem("scanned")
        state_c_made = pool.sem("state_c_made")
        state_s_made = pool.sem("state_s_made")
        y_made = pool.sem("y_made")
        product_made = pool.sem("product_made")
        o_made = pool.sem("o_made")
        h_made = pool.sem("h_made")
        LOADS = 17
        block = ctx.enter_context(nc.Block())

        def column(v):
            return v.rearrange("(p o) -> p o", o=1)

        @block.sync
        def _(sp):
            for dst, src in (
                (w_in[:, :], W_in), (w_out[:, :], W_out), (B[0:N, :], B_re), (B[N:P, :], B_im),
                (conv[:, :, :], conv_w), (conv_bias[:, :], column(conv_b)),
                (C_rows[0][:, 0:N], C_re), (C_rows[0][:, N:P], C_im),
                (C_rows[1][:, 0:N], C_im), (C_rows[1][:, N:P], C_re), (out_bias[:, :], column(b_out)),
                (nu[0:N, :], column(nu_log)), (nu[N:P, :], column(nu_log)),
                (theta[0:N, :], column(theta_log)), (theta[N:P, :], column(theta_log)),
                (gamma[0:N, :], column(gamma_log)), (gamma[N:P, :], column(gamma_log)),
            ):
                sp.dma_start(dst, src).then_inc(loaded, DMA)

        @block.gpsimd
        def _(gp):
            for u in range(2):
                gp.memset(v_pad[u][:, :, :], 0.0).then_inc(zeroed, 1)
                gp.memset(product[u][:, :], 0.0).then_inc(zeroed, 1)
            gp.memset(w_outT[:, :], 0.0).then_inc(zeroed, 1)
            gp.memset(taps[2][:, :], 0.0).then_inc(zeroed, 1)
            gp.wait_ge(tabled, 3)

            def step(i, u):
                p = u % 2
                if skew.has(i, 2):
                    gp.wait_ge(Bv_made, (i - 1) * 3)
                    if skew.has(i, 2, 2):
                        gp.wait_ge(drive_made, i - 3)
                    gp.tensor_tensor(drive_s[p][:, :], Bv_turned[p][:, :],
                                     sin[:, :, :].rearrange("p s t -> p (s t)"), ALU.mult).then_inc(sin_made, 1)
                    gp.wait_ge(scanned, i - 1)
                    if skew.has(i, 2, 2):
                        gp.wait_ge(y_made, i - 3)
                    gp.tensor_tensor(state_s[p][:, :], state[p][:, :],
                                     sin[:, :, :].rearrange("p s t -> p (s t)"), ALU.mult).then_inc(state_s_made, 1)

            skew.run(gp, step)

        @block.scalar
        def _(act):
            act.wait_ge(loaded, LOADS * DMA)
            act.activation(tiny[0][:, :], nu[:, :], ACT.Exp).then_inc(exped, 1)
            act.activation(theta[:, :], theta[:, :], ACT.Exp).then_inc(exped, 1)
            act.activation(gamma[:, :], gamma[:, :], ACT.Exp).then_inc(exped, 1)
            act.wait_ge(exped, 3)
            act.activation(nu[:, :], tiny[0][:, :], ACT.Exp, scale=-1.0).then_inc(exped, 1)
            act.wait_ge(angles, 1)
            act.activation(tiny[1][:, :], theta[:, :], ACT.Sin, scale=0.5).then_inc(sined, 1)
            act.activation(tiny[2][:, :], theta[:, :], ACT.Sin, scale=0.25).then_inc(sined, 1)
            act.wait_ge(tabled, 3)

            def step(i, u):
                p = u % 2
                if skew.has(i, 0):
                    act.wait_ge(projected, i + 1)
                    if skew.has(i, 0, 4):
                        act.wait_ge(product_made, i - 3)
                    act.activation(gated[u][:, :], in_ps[p][0:N, :], ACT.Gelu).then_inc(gelued, 1)
                    act.wait_ge(v_low, i + 1)
                    act.activation(v_pad[p][N:P, :, BEFORE - 1:BEFORE - 1 + SEQ],
                                   v_pad[p][0:N, :, BEFORE:BEFORE + SEQ], ACT.Copy).then_inc(v_high, 1)
                if skew.has(i, 1):
                    q = 1 - p
                    act.wait_ge(driven, i)
                    if skew.has(i, 1, 2):
                        act.wait_ge(cos_made, i - 2)
                        act.wait_ge(sin_made, i - 2)
                    act.activation(Bv[q][:, :], B_ps[q][:, :], ACT.Identity, bias=bias_B[:, :]).then_inc(Bv_made, 1)
                    act.activation(Bv_turned[q][0:N, :], B_ps[q][N:P, :], ACT.Identity,
                                   bias=bias_im[N:P, :]).then_inc(Bv_made, 1)
                    act.activation(Bv_turned[q][N:P, :], B_ps[q][0:N, :], ACT.Identity,
                                   bias=bias_re[0:N, :], scale=-1.0).then_inc(Bv_made, 1)

            skew.run(act, step)

        @block.tensor
        def _(pe):
            pe.wait_ge(loaded, LOADS * DMA)
            pe.transpose(in_ps[0][:, 0:P], w_in[:, :], ident[:, :]).then_inc(folded, 1)
            pe.transpose(in_ps[1][0:N, 0:P], w_out[:, :], ident[:, :]).then_inc(folded, 1)
            pe.transpose(y_ps[0][:, 0:N], C_rows[0][:, :], ident[0:N, 0:N]).then_inc(folded, 1)
            pe.transpose(y_ps[1][:, 0:N], C_rows[1][:, :], ident[0:N, 0:N]).then_inc(folded, 1)
            pe.wait_ge(tabled, 1)
            pe.transpose(B_ps[0][0:N, 0:P], B[:, :], ident[:, :]).then_inc(folded, 1)
            pe.wait_ge(tabled, 2)
            for k in range(TAPS):
                bank, at = (o_ps[0], k * P) if k < 4 else (o_ps[1], 0)
                last = pe.matmul(bank[0:N, at:at + P], conv[:, :, k], BT[:, :], start=True, stop=True)
            pe.matmul(B_ps[1][:, 0:1], BT[:, :], conv_bias[:, :], start=True, stop=True).then_inc(folded, 1)
            pe.wait_ge(tabled, 3)

            def step(i, u):
                p = u % 2
                q = 1 - p
                if skew.has(i, 3):
                    if skew.has(i, 3, 2):
                        pe.wait_ge(product_made, i - 4)
                    pe.wait_ge(state_c_made, i - 2)
                    pe.wait_ge(state_s_made, i - 2)
                    pe.matmul(y_ps[q][0:N, :], C_cos[:, :], state_c[q][:, :], start=True, stop=False)
                    pe.matmul(y_ps[q][0:N, :], C_sin[:, :], state_s[q][:, :], start=False, stop=True)\
                      .then_inc(y_made, 1)
                if skew.has(i, 0):
                    if skew.has(i, 0, 2):
                        pe.wait_ge(gelued, i - 1)
                        pe.wait_ge(v_high, i - 1)
                        pe.wait_ge(v_low, i - 1)
                    pe.matmul(in_ps[p][:, :], w_inT[:, :], columns(X, i * PAIR, PAIR),
                              start=True, stop=True).then_inc(projected, 1)
                if skew.has(i, 3):
                    if skew.has(i, 3, 2):
                        pe.wait_ge(h_made, i - 4)
                    pe.wait_ge(product_made, i - 2)
                    pe.matmul(o_ps[q][:, :], w_outT[:, :], product[q][:, :], start=True, stop=True)\
                      .then_inc(o_made, 1)
                if skew.has(i, 1):
                    if skew.has(i, 1, 2):
                        pe.wait_ge(Bv_made, (i - 2) * 3)
                    pe.wait_ge(v_high, i)
                    pe.wait_ge(v_low, i)
                    for t in range(3):
                        last = pe.matmul(B_ps[q][:, :], taps[t][:, :], v_pad[q][:, :, 2 * t:2 * t + SEQ],
                                         start=(t == 0), stop=(t == 2))
                    last.then_inc(driven, 1)

            skew.run(pe, step)

        @block.vector
        def _(dve):
            count = [0]

            def chained(instruction):
                count[0] += 1
                instruction.then_inc(chain, 1)
                dve.wait_ge(chain, count[0])

            dve.wait_ge(exped, 4)
            dve.tensor_scalar(B[:, :], B[:, :], gamma[:, 0:1], None, ALU.mult).then_inc(tabled, 1)
            chained(dve.tensor_scalar(tiny[3][:, :], theta[:, :], 1.0 / (TWO_PI_HI + TWO_PI_LO), None, ALU.mult))
            chained(dve.tensor_copy(turns_i[:, :], tiny[3][:, :]))
            chained(dve.tensor_copy(tiny[3][:, :], turns_i[:, :]))
            chained(dve.tensor_scalar(tiny[4][:, :], tiny[3][:, :], TWO_PI_HI, None, ALU.mult))
            chained(dve.tensor_tensor(theta[:, :], theta[:, :], tiny[4][:, :], ALU.subtract))
            chained(dve.tensor_scalar(tiny[4][:, :], tiny[3][:, :], TWO_PI_LO, None, ALU.mult))
            dve.tensor_tensor(theta[:, :], theta[:, :], tiny[4][:, :], ALU.subtract).then_inc(angles, 1)
            dve.wait_ge(sined, 2)
            half_sin, quarter_sin, half_cos, c_step, s_step, spare = (tiny[t] for t in (1, 2, 3, 4, 5, 6))
            chained(dve.tensor_tensor(spare[:, :], quarter_sin[:, :], quarter_sin[:, :], ALU.mult))
            chained(dve.tensor_scalar(half_cos[:, :], spare[:, :], -2.0, 1.0, ALU.mult, ALU.add))
            chained(dve.scalar_tensor_tensor(out=s_step[:, :], in0=half_sin[:, :], scalar=2.0,
                                             in1=half_cos[:, :], op0=ALU.mult, op1=ALU.mult))
            chained(dve.tensor_tensor(spare[:, :], half_sin[:, :], half_sin[:, :], ALU.mult))
            chained(dve.tensor_scalar(c_step[:, :], spare[:, :], -2.0, 1.0, ALU.mult, ALU.add))
            chained(dve.memset(cos[:, 0, 0:1], 1.0))
            chained(dve.memset(sin[:, 0, 0:1], 0.0))
            width = 1
            while width < SEQ:
                c0, s0 = cos[:, 0, 0:width], sin[:, 0, 0:width]
                c1, s1 = cos[:, 0, width:2 * width], sin[:, 0, width:2 * width]
                chained(dve.tensor_scalar(part[0][:, 0:width], s0, s_step[:, 0:1], None, ALU.mult))
                chained(dve.scalar_tensor_tensor(out=c1, in0=c0, scalar=c_step[:, 0:1],
                                                 in1=part[0][:, 0:width], op0=ALU.mult, op1=ALU.subtract))
                chained(dve.tensor_scalar(part[1][:, 0:width], c0, s_step[:, 0:1], None, ALU.mult))
                chained(dve.scalar_tensor_tensor(out=s1, in0=s0, scalar=c_step[:, 0:1],
                                                 in1=part[1][:, 0:width], op0=ALU.mult, op1=ALU.add))
                chained(dve.tensor_tensor(spare[:, :], s_step[:, :], s_step[:, :], ALU.mult))
                chained(dve.scalar_tensor_tensor(out=s_step[:, :], in0=s_step[:, :], scalar=2.0,
                                                 in1=c_step[:, :], op0=ALU.mult, op1=ALU.mult))
                chained(dve.tensor_scalar(c_step[:, :], spare[:, :], -2.0, 1.0, ALU.mult, ALU.add))
                width *= 2
            chained(dve.tensor_copy(cos[:, 1, :], cos[:, 0, :]))
            chained(dve.tensor_copy(sin[:, 1, :], sin[:, 0, :]))
            chained(dve.memset(decay[:, :, :], 1.0))
            chained(dve.tensor_scalar(decay[:, :, :], decay[:, :, :], nu[:, 0:1], None, ALU.mult))
            chained(dve.memset(decay[:, :, 0:1], 0.0))
            dve.wait_ge(folded, 5)
            dve.tensor_copy(BT[:, :], B_ps[0][0:N, 0:P]).then_inc(tabled, 1)
            dve.wait_ge(zeroed, 6)
            dve.tensor_copy(w_inT[:, :], in_ps[0][:, 0:P])
            dve.tensor_copy(w_outT[0:N, :], in_ps[1][0:N, 0:P])
            dve.tensor_copy(C_cos[0:N, :], y_ps[0][0:N, 0:N])
            dve.tensor_scalar(C_cos[N:P, :], y_ps[0][N:P, 0:N], -1.0, None, ALU.mult)
            dve.tensor_scalar(C_sin[:, :], y_ps[1][:, 0:N], -1.0, None, ALU.mult)
            dve.wait_ge(folded, 6)
            for k in range(TAPS):
                bank, at = (o_ps[0], k * P) if k < 4 else (o_ps[1], 0)
                low = k % 2 * N
                dve.tensor_copy(taps[k // 2][low:low + N, :], bank[0:N, at:at + P])
            dve.tensor_copy(bias_B[:, :], B_ps[1][:, 0:1])
            for low in (0, N):
                dve.tensor_copy(bias_im[low:low + N, :], B_ps[1][N:P, 0:1])
                last = dve.tensor_scalar(bias_re[low:low + N, :], B_ps[1][0:N, 0:1], -1.0, None, ALU.mult)
            last.then_inc(tabled, 1)

            cos_flat = cos[:, :, :].rearrange("p s t -> p (s t)")
            decay_flat = decay[:, :, :].rearrange("p s t -> p (s t)")

            def step(i, u):
                p = u % 2
                q = 1 - p
                if skew.has(i, 3):
                    dve.wait_ge(y_made, i - 2)
                    if skew.has(i, 3, 2):
                        dve.wait_ge(o_made, i - 4)
                    dve.tensor_tensor(product[q][0:N, :], y_ps[q][0:N, :], gated[(u + 1) % 4][:, :], ALU.mult)\
                       .then_inc(product_made, 1)
                if skew.has(i, 0):
                    dve.wait_ge(projected, i + 1)
                    dve.tensor_copy(v_pad[p][0:N, :, BEFORE:BEFORE + SEQ],
                                    in_ps[p][N:P, :].rearrange("p (s t) -> p s t", s=2)).then_inc(v_low, 1)
                if skew.has(i, 2):
                    dve.wait_ge(Bv_made, (i - 1) * 3)
                    dve.tensor_tensor(drive_c[:, :], Bv[p][:, :], cos_flat, ALU.mult).then_inc(cos_made, 1)
                    dve.wait_ge(cos_made, i - 1)
                    dve.wait_ge(sin_made, i - 1)
                    dve.tensor_tensor(drive[:, :], drive_c[:, :], drive_s[p][:, :], ALU.add).then_inc(drive_made, 1)
                    dve.wait_ge(drive_made, i - 1)
                    if skew.has(i, 2, 2):
                        dve.wait_ge(state_s_made, i - 3)
                    dve.tensor_tensor_scan(state[p][:, :], decay_flat, drive[:, :], 0.0, ALU.mult, ALU.add)\
                       .then_inc(scanned, 1)
                    dve.wait_ge(scanned, i - 1)
                    if skew.has(i, 2, 2):
                        dve.wait_ge(y_made, i - 3)
                    dve.tensor_tensor(state_c[p][:, :], state[p][:, :], cos_flat, ALU.mult)\
                       .then_inc(state_c_made, 1)
                if skew.has(i, 3):
                    dve.wait_ge(o_made, i - 2)
                    h = columns(hT, (i - 3) * PAIR, PAIR)
                    dve.scalar_tensor_tensor(out=h, in0=o_ps[q][:, :], scalar=out_bias[:, 0:1], in1=h,
                                             op0=ALU.add, op1=ALU.add).then_inc(h_made, 1)

            skew.run(dve, step)


def routing_stage(nc, logits, routes, tiles, E):
    with ExitStack() as ctx:
        pool = Pools(nc, ctx, "rou")
        W = tiles * E
        rank_i = pool.sbuf("rank_i", [P, W], I32)
        rank = pool.sbuf("rank", [P, W])
        reaches = pool.sbuf("reaches", [P, W])
        taken = pool.sbuf("taken", [P, W])
        rest = pool.sbuf("rest", [P, W])
        second = pool.sbuf("second", [P, W])
        top = [pool.sbuf(f"top{n}", [P, tiles]) for n in range(2)]
        best = pool.sbuf("best", [P, tiles])
        gap = pool.sbuf("gap", [P, tiles])
        ratio = pool.sbuf("ratio", [P, tiles])
        total = pool.sbuf("total", [P, tiles])
        share = [pool.sbuf(f"share{n}", [P, tiles]) for n in range(2)]
        ranked = pool.sem("ranked")
        chain = pool.sem("chain")
        gaps = pool.sem("gaps")
        ratios = pool.sem("ratios")
        block = ctx.enter_context(nc.Block())

        def by_tile(x):
            return x[:, :].rearrange("p (t e) -> p t e", e=E)

        def spread(x):
            return x[:, :].unsqueeze(2).to_broadcast([P, tiles, E])

        @block.gpsimd
        def _(gp):
            gp.iota(by_tile(rank_i), pattern=[[0, tiles], [-1, E]], base=E, channel_multiplier=0).then_inc(ranked, 1)

        @block.scalar
        def _(act):
            act.wait_ge(gaps, 1)
            act.activation(ratio[:, :], gap[:, :], ACT.Exp).then_inc(ratios, 1)

        @block.vector
        def _(dve):
            count = [0]

            def chained(instruction):
                count[0] += 1
                instruction.then_inc(chain, 1)
                dve.wait_ge(chain, count[0])

            def take_best(values, n, out):
                chained(dve.tensor_reduce(top[n][:, :], by_tile(values), AX.X, ALU.max))
                chained(dve.tensor_tensor(by_tile(reaches), by_tile(values), spread(top[n]), ALU.is_equal))
                chained(dve.tensor_tensor(reaches[:, :], reaches[:, :], rank[:, :], ALU.mult))
                chained(dve.tensor_reduce(best[:, :], by_tile(reaches), AX.X, ALU.max))
                chained(dve.tensor_tensor(by_tile(out), by_tile(rank), spread(best), ALU.is_equal))

            dve.wait_ge(ranked, 1)
            chained(dve.tensor_copy(rank[:, :], rank_i[:, :]))
            take_best(logits, 0, taken)
            chained(dve.scalar_tensor_tensor(out=rest[:, :], in0=taken[:, :], scalar=-3.0e38, in1=logits[:, :],
                                             op0=ALU.mult, op1=ALU.add))
            take_best(rest, 1, second)
            dve.tensor_tensor(gap[:, :], top[1][:, :], top[0][:, :], ALU.subtract).then_inc(gaps, 1)
            dve.wait_ge(ratios, 1)
            chained(dve.tensor_scalar(total[:, :], ratio[:, :], 1.0, None, ALU.add))
            chained(dve.reciprocal(share[0][:, :], total[:, :]))
            chained(dve.tensor_tensor(share[1][:, :], share[0][:, :], ratio[:, :], ALU.mult))
            chained(dve.tensor_tensor(by_tile(taken), by_tile(taken), spread(share[0]), ALU.mult))
            chained(dve.tensor_tensor(by_tile(second), by_tile(second), spread(share[1]), ALU.mult))
            chained(dve.tensor_tensor(routes[:, :], taken[:, :], second[:, :], ALU.add))


def experts_stage(nc, hT, X, routes, ident, weights, out):
    w1, b1, w2, b2 = weights
    E, D, F2 = w1.shape
    FS = F2 // P
    T = PAIR // P
    PAIRS = hT.shape[1] // PAIR
    assert FS == 2 and T * E <= P
    out_v = out.rearrange("(i t p) d -> i p t d", t=T, p=P)
    with ExitStack() as ctx:
        pool = Pools(nc, ctx, "exp")
        w1_raw = pool.sbuf("w1_raw", [P, E, F2])
        w1_hi = pool.sbuf("w1_hi", [P, E, F2], F32R)
        w1_lo = pool.sbuf("w1_lo", [P, E, F2], F32R)
        w2_sb = pool.sbuf("w2", [P, E, FS, P])
        b1_rows = pool.sbuf("b1_rows", [E * FS, P])
        b1_col = pool.sbuf("b1_col", [P, E * FS])
        b2_tiles = pool.sbuf("b2_tiles", [P, T, P])
        x_hi = [pool.sbuf(f"x_hi{p}", [P, PAIR], F32R) for p in range(2)]
        x_lo = [pool.sbuf(f"x_lo{p}", [P, PAIR], F32R) for p in range(2)]
        h_now = [pool.sbuf(f"h_now{p}", [P, PAIR]) for p in range(2)]
        route_now = [pool.sbuf(f"route_now{p}", [P, P]) for p in range(2)]
        routeT = [pool.sbuf(f"routeT{p}", [P, P]) for p in range(2)]
        hidden = [[pool.sbuf(f"hidden{p}{f}", [P, PAIR]) for f in range(FS)] for p in range(2)]
        total = [pool.sbuf(f"total{p}", [P, T, P]) for p in range(2)]
        hidden_ps = [[pool.bank(f"hidden{p}{f}") for f in range(FS)] for p in range(2)]
        y_ps = [pool.bank(f"y{p}") for p in range(2)]
        start_ps = pool.bank("start")
        route_ps = pool.bank("route")

        weights_in = pool.sem("weights_in")
        zeroed = pool.sem("zeroed")
        b2_in = pool.sem("b2_in")
        b1_turned = pool.sem("b1_turned")
        hi_made = pool.sem("hi_made")
        ready = pool.sem("ready")
        x_hi_made = pool.sem("x_hi_made")
        x_lo_made = pool.sem("x_lo_made")
        now_made = pool.sem("now_made")
        route_turned = pool.sem("route_turned")
        routeT_made = pool.sem("routeT_made")
        started = pool.sem("started")
        start_out = pool.sem("start_out")
        hidden_run = pool.sem("hidden_run")
        hidden_out = pool.sem("hidden_out")
        y_run = pool.sem("y_run")
        y_added = pool.sem("y_added")
        stored = [pool.sem(f"stored{p}") for p in range(2)]
        block = ctx.enter_context(nc.Block())

        def rounds(eng, pair):
            pair(0, 0)
            pair(1, 1)
            with eng.Fori(1, PAIRS // 2) as r:
                pair(r * 2, 0)
                pair(r * 2 + 1, 1)

        def known(i):
            return isinstance(i, int)

        @block.sync
        def _(sp):
            sp.dma_start(w1_raw[:, :, :], w1.rearrange("e d f -> d e f")).then_inc(weights_in, DMA)
            sp.dma_start(b1_rows[:, :], b1.rearrange("e (f p) -> (e f) p", p=P)).then_inc(weights_in, DMA)
            for e in range(E):
                sp.dma_start(w2_sb[:, e, :, :], w2[e].rearrange("(f p) d -> p f d", p=P)).then_inc(weights_in, DMA)
            sp.wait_ge(zeroed, 3)
            for t in range(T):
                sp.dma_start(b2_tiles[t * E:(t + 1) * E, t, :], b2).then_inc(b2_in, DMA)

            def pair(i, p):
                sp.wait_ge(y_added, i * (E * T) + E * T)
                sp.dma_start(out_v[bass.ds(i, 1), :, :, :].rearrange("i p t d -> p (i t) d"),
                             total[p][:, :, :]).then_inc(stored[p], DMA)

            rounds(sp, pair)
            for p in range(2):
                sp.wait_ge(stored[p], PAIRS // 2 * DMA)

        @block.gpsimd
        def _(gp):
            gp.memset(b2_tiles[:, :, :], 0.0).then_inc(zeroed, 1)
            for p in range(2):
                gp.memset(route_now[p][:, :], 0.0).then_inc(zeroed, 1)
            gp.wait_ge(zeroed, 3)

            def pair(i, p):
                if not known(i):
                    gp.wait_ge(started, i - 1)
                    gp.wait_ge(y_added, i * (E * T) - E * T)
                gp.tensor_copy(h_now[p][:, :], columns(hT, i * PAIR, PAIR)).then_inc(now_made, 1)
                gp.tensor_copy(route_now[p][:, 0:T * E], columns(routes, i * (T * E), T * E)).then_inc(now_made, 1)

            rounds(gp, pair)

        @block.tensor
        def _(pe):
            def begin(i, p):
                pe.wait_ge(now_made, i * 2 + 2)
                if not (known(i) and i == 0):
                    pe.wait_ge(routeT_made, i)
                pe.transpose(route_ps[:, 0:P], route_now[p][:, :], ident[:, :]).then_inc(route_turned, 1)

            def start(i, p):
                if not (known(i) and i == 0):
                    pe.wait_ge(start_out, i)
                pe.wait_ge(routeT_made, i + 1)
                for t in range(T):
                    tile = start_ps[:, t * P:(t + 1) * P]
                    pe.matmul(tile, routeT[p][:, :], b2_tiles[:, t, :], start=True, stop=False)
                    last = pe.matmul(tile, h_now[p][:, t * P:(t + 1) * P], ident[:, :], start=False, stop=True)
                last.then_inc(started, 1)

            def first(i, e, p, f):
                unit = i * E + e
                if f == 0 and e == 0:
                    pe.wait_ge(x_hi_made, i + 1)
                    pe.wait_ge(x_lo_made, i + 1)
                if not (known(i) and unit < 2):
                    pe.wait_ge(hidden_out, unit * 2 + (f - 3))
                cols = slice(f * P, (f + 1) * P)
                bank = hidden_ps[e % 2][f][:, :]
                pe.matmul(bank, w1_hi[:, e, cols], x_hi[p][:, :], start=True, stop=False)
                pe.matmul(bank, w1_hi[:, e, cols], x_lo[p][:, :], start=False, stop=False)
                pe.matmul(bank, w1_lo[:, e, cols], x_hi[p][:, :], start=False, stop=True).then_inc(hidden_run, 1)

            def second(i, e, tiles):
                unit = i * E + e
                if tiles[0] == 0:
                    pe.wait_ge(hidden_out, unit * 2 + 2)
                    if not (known(i) and unit < 2):
                        pe.wait_ge(y_added, unit * T + (T - 2 * T))
                for t in tiles:
                    for f in range(FS):
                        last = pe.matmul(y_ps[e % 2][:, t * P:(t + 1) * P],
                                         hidden[e % 2][f][:, t * P:(t + 1) * P], w2_sb[:, e, f, :],
                                         start=(f == 0), stop=(f == FS - 1))
                if tiles[-1] == T - 1:
                    last.then_inc(y_run, 1)

            pe.wait_ge(weights_in, (2 + E) * DMA)
            pe.transpose(start_ps[:, 0:E * FS], b1_rows[:, :], ident[0:E * FS, 0:E * FS]).then_inc(b1_turned, 1)
            pe.wait_ge(ready, 1)
            pe.wait_ge(b2_in, T * DMA)

            def pair(i, p):
                begin(i, p)
                for e in range(E):
                    before = (i, e - 1) if e > 0 else (None if known(i) and i == 0 else (i - 1, E - 1))
                    first(i, e, p, 0)
                    if before:
                        second(*before, [0, 1])
                    first(i, e, p, 1)
                    if e == 0:
                        start(i, p)
                    if before:
                        second(*before, [2, 3])

            rounds(pe, pair)
            second(PAIRS - 1, E - 1, list(range(T)))

        @block.scalar
        def _(act):
            act.wait_ge(ready, 1)

            def split(i, p):
                if not known(i):
                    act.wait_ge(hidden_run, i * (E * 2) - E * 2)
                act.activation(x_hi[p][:, :], columns(X, i * PAIR, PAIR), ACT.Copy).then_inc(x_hi_made, 1)

            split(0, 0)

            def pair(i, p):
                act.wait_ge(route_turned, i + 1)
                act.activation(routeT[p][:, :], route_ps[:, 0:P], ACT.Copy).then_inc(routeT_made, 1)
                for e in range(E):
                    unit = i * E + e
                    for f in range(FS):
                        act.wait_ge(hidden_run, unit * 2 + (f + 1))
                        if f == 0 and not (known(i) and unit < 2):
                            act.wait_ge(y_run, unit - 1)
                        act.activation(hidden[e % 2][f][:, :], hidden_ps[e % 2][f][:, :], ACT.Relu,
                                       bias=b1_col[:, e * FS + f:e * FS + f + 1]).then_inc(hidden_out, 1)
                    if e == 4 and not (known(i) and i == PAIRS - 1):
                        split(i + 1, 1 - p)

            pair(0, 0)
            with act.Fori(0, PAIRS // 2 - 1) as r:
                pair(r * 2 + 1, 1)
                pair(r * 2 + 2, 0)
            pair(PAIRS - 1, 1)

        @block.vector
        def _(dve):
            def split(i, p):
                dve.wait_ge(x_hi_made, i + 1)
                dve.tensor_tensor(x_lo[p][:, :], columns(X, i * PAIR, PAIR), x_hi[p][:, :].bitcast(F32),
                                  ALU.subtract).then_inc(x_lo_made, 1)

            def pair(i, p):
                dve.wait_ge(started, i + 1)
                dve.wait_ge(now_made, i * 2 + 2)
                if not (known(i) and i < 2):
                    dve.wait_ge(stored[p], (i - p) * (DMA // 2))
                dve.tensor_copy(total[p][:, :, :], start_ps[:, :].rearrange("p (t d) -> p t d", t=T))\
                   .then_inc(start_out, 1)
                for e in range(E):
                    unit = i * E + e
                    dve.wait_ge(y_run, unit + 1)
                    for t in range(T):
                        if e == 0:
                            if t == 0:
                                dve.wait_ge(start_out, i + 1)
                        else:
                            dve.wait_ge(y_added, unit * T + (t + 1 - T))
                        dve.scalar_tensor_tensor(
                            out=total[p][:, t, :], in0=y_ps[e % 2][:, t * P:(t + 1) * P],
                            scalar=route_by_tile(i, t, e, p), in1=total[p][:, t, :],
                            op0=ALU.mult, op1=ALU.add).then_inc(y_added, 1)
                    if e == 4 and not (known(i) and i == PAIRS - 1):
                        split(i + 1, 1 - p)

            def route_by_tile(i, t, e, p):
                return route_now[p][:, t * E + e:t * E + e + 1]

            dve.wait_ge(weights_in, (2 + E) * DMA)
            dve.tensor_copy(w1_hi[:, :, :], w1_raw[:, :, :]).then_inc(hi_made, 1)
            dve.wait_ge(hi_made, 1)
            dve.tensor_tensor(w1_lo[:, :, :], w1_raw[:, :, :], w1_hi[:, :, :].bitcast(F32), ALU.subtract)
            dve.wait_ge(b1_turned, 1)
            dve.tensor_copy(b1_col[:, :], start_ps[:, 0:E * FS]).then_inc(ready, 1)
            split(0, 0)
            pair(0, 0)
            with dve.Fori(0, PAIRS // 2 - 1) as r:
                pair(r * 2 + 1, 1)
                pair(r * 2 + 2, 0)
            pair(PAIRS - 1, 1)


def tower_program(nc, x, args, out):
    (emb, pos, Wq, bq, Wk, bk, Wv, bv, Wo, bo, W1, b1, W2, b2,
     ln_w, ln_b, W_in, conv_w, conv_b, nu_log, theta_log, gamma_log, B_re, B_im, C_re, C_im, W_out, b_out,
     gate_w, gate_b, e_w1, e_b1, e_w2, e_b2) = args
    tokens = x.shape[0] * x.shape[1]
    E = gate_w.shape[1]
    EPS = 1e-5
    with ExitStack() as ctx:
        whole = Pools(nc, ctx, "all")
        hT = whole.sbuf("hT", [P, tokens])
        ident = whole.sbuf("ident", [P, P])
        embed_stage(nc, hT, ident, x, emb, pos)
        layers_stage(nc, hT, ident, (Wq, bq, Wk, bk, Wv, bv, Wo, bo, W1, b1, W2, b2))
        X = whole.sbuf("X", [P, tokens])
        norm_stage(nc, "nr", hT, X, ident, EPS, recurrent=(ln_w, ln_b))
        recurrent_stage(nc, hT, X, ident, (W_in, conv_w, conv_b, nu_log, theta_log, gamma_log,
                                           B_re, B_im, C_re, C_im, W_out, b_out))
        logits = whole.sbuf("logits", [P, tokens // P * E])
        routes = whole.sbuf("routes", [P, tokens // P * E])
        norm_stage(nc, "ne", hT, X, ident, EPS, gate=(gate_w, gate_b, logits))
        routing_stage(nc, logits, routes, tokens // P, E)
        experts_stage(nc, hT, X, routes, ident, (e_w1, e_b1, e_w2, e_b2), out)


_INS = ["L0_tok_emb", "L0_tok_pos", "L0_tok_Wq", "L0_tok_bq", "L0_tok_Wk", "L0_tok_bk", "L0_tok_Wv", "L0_tok_bv",
        "L0_tok_Wo", "L0_tok_bo", "L0_tok_W1", "L0_tok_b1", "L0_tok_W2", "L0_tok_b2",
        "L0_attn_ln_w", "L0_attn_ln_b", "L0_attn_W_in", "L0_attn_conv_w", "L0_attn_conv_b", "L0_attn_nu_log",
        "L0_attn_theta_log", "L0_attn_gamma_log", "L0_attn_B_re", "L0_attn_B_im", "L0_attn_C_re", "L0_attn_C_im",
        "L0_attn_W_out", "L0_attn_b_out",
        "L0_ffn_gate_w", "L0_ffn_gate_b", "L0_ffn_w1", "L0_ffn_b1", "L0_ffn_w2", "L0_ffn_b2"]


def kernel(**inputs):
    import numpy as _np
    import concourse.bacc as _bacc
    from concourse import mybir as _mybir
    from concourse.bass_utils import run_bass_kernel_spmd as _run

    nc = _bacc.Bacc("TRN2", target_bir_lowering=False, num_devices=1)
    arrays, args = {}, []
    for name in ["x"] + _INS:
        a = _np.ascontiguousarray(inputs[name])
        arrays[f"in_{name}"] = a
        args.append(nc.dram_tensor(f"in_{name}", a.shape, _mybir.dt.from_np(a.dtype), kind="ExternalInput").ap())
    x = args[0]
    B, S = inputs["x"].shape
    D = inputs["L0_tok_emb"].shape[1]
    out = nc.dram_tensor("out", (B * S, D), _mybir.dt.float32, kind="ExternalOutput").ap()
    tower_program(nc, x, args[1:], out)
    r = _run(nc, [arrays], core_ids=[0])
    return r.results[0]["out"].reshape(B, S, D)
```

```python
from contextlib import ExitStack

import concourse.bass as bass
from concourse import mybir

F32 = mybir.dt.float32
F32R = mybir.dt.float32r
I32 = mybir.dt.int32
U32 = mybir.dt.uint32
ALU = mybir.AluOpType
ACT = mybir.ActivationFunctionType
AX = mybir.AxisListType

P = 128
SEQ = 256
PAIR = 2 * SEQ
HEAD = 64
MASKED = -1.0e30
DMA = 16


class Pools:

    def __init__(self, nc, ctx, prefix):
        self.nc, self.ctx, self.prefix = nc, ctx, prefix

    def sbuf(self, name, shape, dtype=F32):
        return self.ctx.enter_context(self.nc.sbuf_tensor(f"{self.prefix}_{name}", shape, dtype))

    def bank(self, name):
        return self.ctx.enter_context(self.nc.psum_tensor(f"{self.prefix}_ps_{name}", [P, 512], F32))

    def sem(self, name):
        return self.ctx.enter_context(self.nc.semaphore(f"{self.prefix}_{name}"))


def settled(engine, value):
    return value if isinstance(value, int) else engine.to_reg(value)


def columns(tensor, start, count):
    return tensor[:, bass.ds(start, count)]


def embed_stage(nc, hT, ident, ids, emb, pos, index, pos_rows, pairs, beside=None):
    vocab = emb.shape[0]
    n_tiles = ids.shape[0] * ids.shape[1] // P
    RING = 4
    with ExitStack() as ctx:
        pool = Pools(nc, ctx, "emb")
        ids_i = pool.sbuf("ids_i", [n_tiles, P], I32)
        ids_f = pool.sbuf("ids_f", [n_tiles, P])
        wrap = pool.sbuf("wrap", [n_tiles, P])
        index_now = [pool.sbuf(f"index_now{t}", [P, 1], U32) for t in range(RING)]
        rows = [pool.sbuf(f"rows{t}", [P, P]) for t in range(RING)]
        posT = pool.sbuf("posT", [P, SEQ])
        turned = [pool.bank(f"turned{t}") for t in range(RING)]
        setup_ps = pool.bank("setup_ps")
        pos_ps = pool.bank("pos_ps")

        ids_in = pool.sem("ids_in")
        pos_in = pool.sem("pos_in")
        ident_made = pool.sem("ident_made")
        ids_ready = pool.sem("ids_ready")
        setup_turned = pool.sem("setup_turned")
        setup_copied = pool.sem("setup_copied")
        index_copied = pool.sem("index_copied")
        gathered = [pool.sem(f"gathered{t}") for t in range(RING)]
        rows_turned = pool.sem("rows_turned")
        bank_free = pool.sem("bank_free")
        block = ctx.enter_context(nc.Block())

        @block.sync
        def _(sp):
            sp.dma_start(ids_i[:, :], ids.rearrange("b (t p) -> (b t) p", p=P)).then_inc(ids_in, DMA)
            sp.dma_start(pos_rows[:, :, :], pos[0:SEQ, :].rearrange("(t p) d -> p t d", p=P)).then_inc(pos_in, DMA)
            if beside:
                beside(sp)

        @block.gpsimd
        def _(pool_e):
            pool_e.memset(ident[:, :], 0.0).then_inc(ident_made, 1)
            pool_e.wait_ge(ident_made, 1)
            pool_e.affine_select(out=ident[:, :], in_=ident[:, :], compare_op=ALU.not_equal, fill=1.0,
                                 base=0, pattern=[[-1, P]], channel_multiplier=1).then_inc(ident_made, 1)
            pool_e.wait_ge(setup_copied, 1)
            with pool_e.Fori(0, pairs) as i:
                for t in range(RING):
                    pool_e.wait_ge(rows_turned, i * RING + (t + 1))
                    pool_e.tensor_copy(index_now[t][:, :], columns(index, i * RING + t, 1)).then_inc(index_copied, 1)
                    count = settled(pool_e, i * RING + (t + 1))
                    pool_e.wait_ge(ident_made, 2)
                    pool_e.wait_ge(index_copied, count)
                    pool_e.indirect_dma_start(
                        rows[t][:, :], None, emb,
                        bass.IndirectOffsetOnAxis(ap=index_now[t][:, 0:1], axis=0)).then_inc(gathered[t], DMA)

        @block.vector
        def _(dve):
            step = [0]

            def chained(instruction):
                step[0] += 1
                instruction.then_inc(ids_ready, 1)
                dve.wait_ge(ids_ready, step[0])

            dve.wait_ge(ids_in, DMA)
            chained(dve.tensor_copy(ids_f[:, :], ids_i[:, :]))
            chained(dve.tensor_scalar(wrap[:, :], ids_f[:, :], 0.0, float(vocab), ALU.is_lt, ALU.mult))
            chained(dve.tensor_tensor(ids_f[:, :], ids_f[:, :], wrap[:, :], ALU.add))
            dve.tensor_scalar(ids_f[:, :], ids_f[:, :], 0.0, float(vocab - 1), ALU.max, ALU.min).then_inc(ids_ready, 1)
            dve.wait_ge(setup_turned, 1)
            dve.tensor_copy(index[:, :], setup_ps[:, 0:n_tiles]).then_inc(setup_copied, 1)
            dve.wait_ge(setup_turned, 2)
            dve.tensor_copy(posT[:, :], pos_ps[:, 0:SEQ]).then_inc(setup_copied, 1)
            dve.wait_ge(setup_copied, 2)
            with dve.Fori(0, pairs) as i:
                for t in range(RING):
                    dve.wait_ge(rows_turned, i * RING + (t + 1 + RING))
                    half = t % 2 * P
                    dve.tensor_tensor(columns(hT, i * (RING * P) + t * P, P), turned[t][:, 0:P],
                                      posT[:, half:half + P], ALU.add).then_inc(bank_free, 1)

        @block.tensor
        def _(pe):
            pe.wait_ge(ident_made, 2)
            pe.wait_ge(ids_ready, 4)
            pe.transpose(setup_ps[:, 0:n_tiles], ids_f[:, :], ident[0:n_tiles, 0:n_tiles]).then_inc(setup_turned, 1)
            pe.wait_ge(pos_in, DMA)
            pe.transpose(pos_ps[:, 0:P], pos_rows[:, 0, :], ident[:, :])
            pe.transpose(pos_ps[:, P:2 * P], pos_rows[:, 1, :], ident[:, :]).then_inc(setup_turned, 1)
            pe.transpose(turned[0][:, 0:P], ident[:, :], ident[:, :]).then_inc(rows_turned, RING)
            pe.transpose(turned[1][:, 0:P], ident[:, :], ident[:, :]).then_inc(bank_free, RING)
            with pe.Fori(0, pairs) as i:
                for t in range(RING):
                    pe.wait_ge(gathered[t], i * DMA + DMA)
                    pe.wait_ge(bank_free, i * RING + (t + 1))
                    pe.transpose(turned[t][:, 0:P], rows[t][:, :], ident[:, :]).then_inc(rows_turned, 1)


class LayerWeights:

    def __init__(self, pool, weights):
        self.dram = weights
        L, _, HK = weights[0].shape
        self.raw = {n: pool.sbuf(f"raw_{n}", [P, HK]) for n in ("q", "k", "v", "1", "o", "2")}
        self.n_bias = 4 * (HK // P) * L + 2 * L
        self.bias_rows = pool.sbuf("bias_rows", [self.n_bias, P])
        self.bias_in = pool.sem("bias_in")
        self.weights_in = pool.sem("weights_in")

    def load_biases(self, sp):
        _, bq, _, bk, _, bv, _, bo, _, b1, _, b2 = self.dram
        L = bo.shape[0]
        n = (self.n_bias - 2 * L) // 4
        for at, b in enumerate((bq, bk, bv, b1)):
            sp.dma_start(self.bias_rows[at * n:(at + 1) * n, :],
                         b.rearrange("l (j p) -> (l j) p", p=P)).then_inc(self.bias_in, DMA)
        for at, b in enumerate((bo, b2)):
            sp.dma_start(self.bias_rows[4 * n + at * L:4 * n + (at + 1) * L, :], b).then_inc(self.bias_in, DMA)

    def load(self, sp, layer):
        Wq, _, Wk, _, Wv, _, Wo, _, W1, _, W2, _ = self.dram
        for name, w in (("q", Wq), ("k", Wk), ("v", Wv), ("1", W1)):
            sp.dma_start(self.raw[name][:, :], w[bass.ds(layer, 1), :, :].rearrange("l p n -> p (l n)"))\
              .then_inc(self.weights_in, DMA)
        for name, w in (("o", Wo), ("2", W2)):
            sp.dma_start(self.raw[name][:, :].rearrange("p (j d) -> p j d", d=P),
                         w[bass.ds(layer, 1), :, :].rearrange("l (j p) d -> p (l j) d", p=P))\
              .then_inc(self.weights_in, DMA)

    def load_first(self, sp):
        self.load_biases(sp)
        self.load(sp, 0)


def layers_stage(nc, hT, ident, weights, emb, index, pos_rows, embedded):
    L, _, HK = weights.dram[0].shape
    FF = weights.dram[8].shape[2]
    PAIRS = hT.shape[1] // PAIR
    JS = HK // P
    FS = FF // P
    UNITS = 2 * JS
    assert UNITS == 8 and JS == FS == 4 and PAIRS % 2 == 0 and PAIRS >= 6 and L >= 3
    SCALE = -float(HEAD) ** -0.5

    OWN = [("k", 3), ("q", 3)]
    SLOTS = {0: OWN, 1: [("v", 0), ("v", 1)], 2: [("k", 0), ("q", 0)], 3: [("v", 2), ("v", 3)],
             4: [("k", 1), ("q", 1)], 5: [("f", 0), ("f", 1)], 6: [("f", 2), ("f", 3)], 7: [("k", 2), ("q", 2)]}
    AHEAD = [("k", 0), ("q", 0), ("v", 0), ("v", 1), ("k", 1), ("q", 1), ("v", 2), ("v", 3), ("k", 2), ("q", 2)]
    PER_PAIR = UNITS * 2
    TOTAL = L * PAIRS

    def known(g, value):
        return isinstance(g, int) and g == value

    def pieces_of(k, has_prev, has_next):
        return [x for x in SLOTS[k] if x in OWN or (has_prev if x[0] == "f" else has_next)]

    def pieces_by_place(has_prev, has_next):
        return [x for k in range(UNITS) for x in pieces_of(k, has_prev, has_next)]

    def piece_base(g):
        if known(g, 0):
            return len(AHEAD) // 2
        return g * (PER_PAIR // 2) + ((len(AHEAD) - FS) // 2)

    def residual(g):
        return columns(hT, g % PAIRS * PAIR, PAIR)

    with ExitStack() as ctx:
        pool = Pools(nc, ctx, "lay")
        raw, bias_rows, bias_in, weights_in = weights.raw, weights.bias_rows, weights.bias_in, weights.weights_in
        w_hi = {n: pool.sbuf(f"w_hi_{n}", [P, HK], F32R) for n in ("v", "q", "k", "1", "o", "2")}
        w_lo = {n: pool.sbuf(f"w_lo_{n}", [P, HK], F32R) for n in w_hi}
        N_BIAS = weights.n_bias
        biasT = pool.sbuf("biasT", [P, N_BIAS])
        bias_qkv = pool.sbuf("bias_qkv", [P, 3, JS])
        bias_1 = pool.sbuf("bias_1", [P, FS])
        bias_2 = pool.sbuf("bias_2", [P, 1])
        bias_o = pool.sbuf("bias_o", [P, 1])
        index_now = [pool.sbuf(f"index_now{t}", [P, 1], U32) for t in range(4)]
        rows = [pool.sbuf(f"rows{t}", [P, P]) for t in range(4)]
        mask = pool.sbuf("mask", [P, 2 * P])
        h_hi = [pool.sbuf(f"h_hi{p}", [P, PAIR], F32R) for p in range(2)]
        h_lo = [pool.sbuf(f"h_lo{p}", [P, PAIR], F32R) for p in range(2)]
        Q = pool.sbuf("Q", [P, JS, PAIR])
        K = [pool.sbuf(f"K{h}", [P, JS, PAIR]) for h in range(2)]
        V = [[pool.sbuf(f"V{p}{t}", [P, HK]) for t in range(4)] for p in range(2)]
        probs = [pool.sbuf(f"probs{p}", [P, 6 * P]) for p in range(2)]
        least = [pool.sbuf(f"least{p}", [P, 4]) for p in range(2)]
        sums = [pool.sbuf(f"sums{p}", [P, 4]) for p in range(2)]
        inverse = [pool.sbuf(f"inverse{p}", [P, 4]) for p in range(2)]
        probsT = [pool.sbuf(f"probsT{p}", [P, 6 * P]) for p in range(2)]
        O = pool.sbuf("O", [P, 2, PAIR])
        O_hi = pool.sbuf("O_hi", [P, JS, PAIR], F32R)
        O_lo = pool.sbuf("O_lo", [P, JS, PAIR], F32R)
        c_hi = pool.sbuf("c_hi", [P, PAIR], F32R)
        c_lo = pool.sbuf("c_lo", [P, PAIR], F32R)
        hidden = pool.sbuf("hidden", [P, 2, PAIR])
        hidden_hi = pool.sbuf("hidden_hi", [P, FS, PAIR], F32R)
        hidden_lo = pool.sbuf("hidden_lo", [P, FS, PAIR], F32R)

        score_ps = [pool.bank(f"score{b}") for b in range(2)]
        turn_ps = [pool.bank(f"turn{b}") for b in range(2)]
        head_ps = pool.bank("head")
        piece_ps = [pool.bank(f"piece{b}") for b in range(2)]
        sum_ps = pool.bank("sum")

        index_copied = pool.sem("index_copied")
        gathered = [pool.sem(f"gathered{t}") for t in range(4)]
        rows_ready = pool.sem("rows_ready")
        zeroed = pool.sem("zeroed")
        K_zeroed = pool.sem("K_zeroed")
        bias_turned = pool.sem("bias_turned")
        setup_done = pool.sem("setup_done")
        split_qk = pool.sem("split_qk")
        split_v = pool.sem("split_v")
        split_1 = pool.sem("split_1")
        hi_o = pool.sem("hi_o")
        hi_2 = pool.sem("hi_2")
        split_o = pool.sem("split_o")
        split_2 = pool.sem("split_2")
        hi_made = pool.sem("hi_made")
        bias_o_run = pool.sem("bias_o_run")
        bias_o_made = pool.sem("bias_o_made")
        h_hi_made = pool.sem("h_hi_made")
        h_lo_made = pool.sem("h_lo_made")
        pieces = pool.sem("pieces")
        piece_free = [pool.sem(f"piece_free{b}") for b in range(2)]
        scored = pool.sem("scored")
        masked = pool.sem("masked")
        exped = pool.sem("exped")
        inverted = pool.sem("inverted")
        normed = pool.sem("normed")
        turned = pool.sem("turned")
        turned_out = [pool.sem(f"turned_out{b}") for b in range(2)]
        headed = pool.sem("headed")
        O_made = pool.sem("O_made")
        O_hi_made = pool.sem("O_hi_made")
        O_lo_made = pool.sem("O_lo_made")
        projected = pool.sem("projected")
        h1_made = pool.sem("h1_made")
        c_hi_made = pool.sem("c_hi_made")
        c_lo_made = pool.sem("c_lo_made")
        hidden_hi_made = pool.sem("hidden_hi_made")
        hidden_lo_made = pool.sem("hidden_lo_made")
        fed = pool.sem("fed")
        h2_made = pool.sem("h2_made")
        block = ctx.enter_context(nc.Block())

        def wait_piece(eng, base, at):
            eng.wait_ge(pieces, base * 2 + (at + 1))

        def wait_copied(eng, base, at):
            eng.wait_ge(piece_free[at % 2], base + (at // 2 + 1))

        def wait_projection(eng, g, kind):
            if kind in OWN:
                wait_copied(eng, piece_base(g), OWN.index(kind))
            elif known(g, 0):
                wait_copied(eng, 0, AHEAD.index(kind))
            else:
                wait_copied(eng, piece_base(g - 1), pieces_by_place(not known(g, 1), True).index(kind))

        def stream(eng, pair):
            def in_register(g):
                return eng.snap(eng.to_reg(g), min_val=1, max_val=TOTAL - 1)

            pair(0, 0, "start", 0, embed=True)
            with eng.Fori(0, PAIRS // 2 - 2) as r:
                pair(0, r * 2 + 1, "", 1, embed=True)
                pair(0, r * 2 + 2, "", 0, embed=True)
            pair(0, PAIRS - 3, "", 1, embed=True)
            pair(0, PAIRS - 2, "", 0)
            pair(0, PAIRS - 1, "last", 1)
            pair(1, PAIRS, "first", 0)
            with eng.Fori(1, L - 1) as layer:
                with eng.Fori(0, PAIRS // 2 - 1) as r:
                    pair(layer, in_register(layer * PAIRS + r * 2 + 1), "", 1)
                    pair(layer, in_register(layer * PAIRS + r * 2 + 2), "", 0)
                pair(layer, in_register(layer * PAIRS + PAIRS - 1), "last", 1)
                pair(layer + 1, in_register(layer * PAIRS + PAIRS), "first", 0)
            with eng.Fori(0, PAIRS // 2 - 1) as r:
                pair(L - 1, in_register(r * 2 + (TOTAL - PAIRS + 1)), "", 1)
                pair(L - 1, in_register(r * 2 + (TOTAL - PAIRS + 2)), "", 0)
            pair(L - 1, TOTAL - 1, "end", 1)

        PARTS = [(0, 2 * P), (2 * P, 4 * P), (4 * P, 5 * P), (5 * P, 6 * P)]

        @block.sync
        def _(sp):
            with sp.Fori(1, L) as layer:
                sp.wait_ge(split_2, layer)
                sp.wait_ge(bias_o_run, layer)
                weights.load(sp, layer)

        @block.gpsimd
        def _(gp):
            gp.memset(mask[:, :], 0.0).then_inc(zeroed, 1)
            gp.wait_ge(zeroed, 1)
            gp.affine_select(out=mask[:, P:2 * P], in_=mask[:, P:2 * P], compare_op=ALU.is_ge,
                             fill=MASKED, base=0, pattern=[[-1, P]], channel_multiplier=1).then_inc(zeroed, 1)

            def O_lo_of(count, j):
                gp.wait_ge(O_hi_made, count + 1)
                gp.tensor_tensor(O_lo[:, j, :], O[:, j % 2, :], O_hi[:, j, :].bitcast(F32),
                                 ALU.subtract).then_inc(O_lo_made, 1)

            def gather(g, t):
                count = settled(gp, g * 4 + (t + 1 - 4 * embedded))
                gp.tensor_copy(index_now[t][:, :], columns(index, g * 4 + t, 1)).then_inc(index_copied, 1)
                gp.wait_ge(zeroed, 2)
                gp.wait_ge(index_copied, count)
                gp.indirect_dma_start(rows[t][:, :], None, emb,
                                      bass.IndirectOffsetOnAxis(ap=index_now[t][:, 0:1], axis=0))\
                  .then_inc(gathered[t], DMA)

            def add_position(g, t):
                gp.wait_ge(gathered[t], (g + (1 - embedded)) * DMA)
                gp.tensor_tensor(rows[t][:, :], rows[t][:, :], pos_rows[:, t % 2, :], ALU.add).then_inc(rows_ready, 1)

            for t in range(4):
                gather(embedded, t)
            for t in range(4):
                add_position(embedded, t)

            def pair(g, has_prev, gathers):
                for k in range(UNITS):
                    count = settled(gp, g * UNITS + (k + 1))
                    gp.wait_ge(zeroed, 2)
                    gp.wait_ge(inverted, count)
                    for q, (a, b) in enumerate(PARTS):
                        gp.tensor_scalar(probs[k % 2][:, a:b], probs[k % 2][:, a:b],
                                         inverse[k % 2][:, q:q + 1], 1.0, ALU.mult, ALU.mult)\
                          .then_inc(normed, 1)
                    if k % 2 == 1 and (k >= 3 or has_prev):
                        j = (k - 3) // 2 if k >= 3 else JS - 1
                        O_lo_of(g * JS + j if k >= 3 else g * JS - 1, j)
                    if gathers and 3 <= k < 7:
                        gp.wait_ge(turned, (g * UNITS + (k - 3)) * 2 + 1)
                        gather(g + 3, k - 3)
                    if gathers and k >= 4:
                        add_position(g + 3, k - 4)

            pair(0, False, True)
            with gp.Fori(1, PAIRS - 3) as g:
                pair(g, True, True)
            with gp.Fori(PAIRS - 3, TOTAL) as g:
                pair(g, True, False)
            O_lo_of(TOTAL * JS - 1, JS - 1)

        @block.tensor
        def _(pe):
            def three_passes(out, lhs_hi, lhs_lo, rhs_hi, rhs_lo, start=True, stop=True):
                pe.matmul(out, lhs_hi, rhs_hi, start=start, stop=False)
                pe.matmul(out, lhs_hi, rhs_lo, start=False, stop=False)
                return pe.matmul(out, lhs_lo, rhs_hi, start=False, stop=stop)

            def piece(kind, at, base, parity, first=False):
                if not first:
                    pe.wait_ge(piece_free[at % 2], base + at // 2)
                bank = piece_ps[at % 2][:, :]
                name, n = kind
                if name == "v":
                    cols = slice(n * P, (n + 1) * P)
                    last = three_passes(bank, h_hi[parity][:, cols], h_lo[parity][:, cols],
                                        w_hi["v"][:, :], w_lo["v"][:, :])
                else:
                    cols = slice(n * P, (n + 1) * P)
                    hi, lo = (c_hi, c_lo) if name == "f" else (h_hi[parity], h_lo[parity])
                    w = "1" if name == "f" else name
                    last = three_passes(bank, w_hi[w][:, cols], w_lo[w][:, cols], hi[:, :], lo[:, :])
                last.then_inc(pieces, 1)

            def scores(g, k, parity):
                j, s = k // 2, k % 2 * SEQ
                unit = g * UNITS + k
                if s == 0:
                    wait_projection(pe, g, ("k", j))
                    wait_projection(pe, g, ("q", j))
                if not (known(g, 0) and k == 0):
                    pe.wait_ge(masked, unit * 4)
                for bank, (first, width) in enumerate(((s + P, SEQ), (s, P))):
                    for h in range(2):
                        last = pe.matmul(score_ps[bank][:, h * width:(h + 1) * width], Q[:, j, first:first + P],
                                         K[h][:, j, s:s + width], start=True, stop=True)
                    last.then_inc(scored, 1)

            def turn(g, k, embed=False):
                unit = g * UNITS + k
                own = probs[k % 2]
                pe.wait_ge(normed, unit * 4 + 2)
                if not (known(g, 0) and k == 0):
                    pe.wait_ge(turned_out[1], unit)
                if embed:
                    pe.wait_ge(rows_ready, g * 4 + (k + 1))
                    pe.transpose(turn_ps[1][:, SEQ:SEQ + P], rows[k][:, :], ident[:, :])
                for h in range(2):
                    last = pe.transpose(turn_ps[1][:, h * P:(h + 1) * P],
                                        own[:, h * SEQ + P:(h + 1) * SEQ], ident[:, :])
                last.then_inc(turned, 1)
                if not (known(g, 0) and k == 0):
                    pe.wait_ge(turned_out[0], unit)
                for h in range(2):
                    pe.transpose(turn_ps[0][:, h * SEQ + P:(h + 1) * SEQ],
                                 own[:, h * SEQ:h * SEQ + P], ident[:, :])
                pe.wait_ge(normed, unit * 4 + 4)
                for h in range(2):
                    last = pe.transpose(turn_ps[0][:, h * SEQ:h * SEQ + P],
                                        own[:, (4 + h) * P:(5 + h) * P], ident[:, :])
                last.then_inc(turned, 1)

            def values(g, k, parity):
                j, s = k // 2, k % 2
                unit = g * UNITS + k
                if k < 2:
                    wait_projection(pe, g, ("v", 2 * s))
                    wait_projection(pe, g, ("v", 2 * s + 1))
                if s == 0 and not (known(g, 0) and k == 0):
                    pe.wait_ge(O_made, g * JS + j)
                pe.wait_ge(turned_out[1], unit + 1)
                pe.wait_ge(turned_out[0], unit + 1)
                PT = probsT[k % 2]
                at = s * SEQ
                for h in range(2):
                    cols = slice((2 * j + h) * HEAD, (2 * j + h + 1) * HEAD)
                    pe.matmul(head_ps[h * HEAD:(h + 1) * HEAD, at:at + SEQ], V[parity][2 * s][:, cols],
                              PT[:, h * SEQ:(h + 1) * SEQ], start=True, stop=False)
                for h in (1, 0):
                    cols = slice((2 * j + h) * HEAD, (2 * j + h + 1) * HEAD)
                    last = pe.matmul(head_ps[h * HEAD:(h + 1) * HEAD, at + P:at + SEQ],
                                     V[parity][2 * s + 1][:, cols], PT[:, (4 + h) * P:(5 + h) * P],
                                     start=False, stop=True)
                if s == 1:
                    last.then_inc(headed, 1)

            def output_projection(g, sets, js):
                for j in js:
                    if j == 0:
                        pe.wait_ge(split_o, sets)
                        pe.wait_ge(bias_o_made, sets)
                        pe.wait_ge(h2_made, g + PAIRS)
                    pe.wait_ge(O_lo_made, g * JS + (j + 1))
                    cols = slice(j * P, (j + 1) * P)
                    last = three_passes(sum_ps[:, :], w_hi["o"][:, cols], w_lo["o"][:, cols], O_hi[:, j, :],
                                        O_lo[:, j, :], start=(j == 0), stop=(j == JS - 1))
                if js[-1] == JS - 1:
                    last.then_inc(projected, 1)

            def run_bias_o(sets):
                pe.wait_ge(weights_in, sets * (6 * DMA))
                pe.wait_ge(split_qk, sets)
                for j in range(JS):
                    last = pe.matmul(sum_ps[:, 0:1], raw["o"][:, j * P:(j + 1) * P], bias_qkv[:, 2, j:j + 1],
                                     start=(j == 0), stop=(j == JS - 1))
                last.then_inc(bias_o_run, 1)

            def feed_sum(g, sets, fs):
                for f in fs:
                    if f == 0:
                        pe.wait_ge(h1_made, g + 1)
                        pe.wait_ge(split_2, sets)
                    pe.wait_ge(hidden_lo_made, g * FS + (f + 1))
                    cols = slice(f * P, (f + 1) * P)
                    last = three_passes(sum_ps[:, :], w_hi["2"][:, cols], w_lo["2"][:, cols], hidden_hi[:, f, :],
                                        hidden_lo[:, f, :], start=(f == 0), stop=(f == FS - 1))
                if fs[-1] == FS - 1:
                    last.then_inc(fed, 1)

            def wait_c(g):
                pe.wait_ge(c_hi_made, g + 1)
                pe.wait_ge(c_lo_made, g + 1)

            def wait_h(g):
                pe.wait_ge(h_hi_made, g + 1)
                pe.wait_ge(h_lo_made, g + 1)

            pe.wait_ge(bias_in, 6 * DMA)
            pe.transpose(sum_ps[:, 0:N_BIAS], bias_rows[:, :], ident[0:N_BIAS, 0:N_BIAS]).then_inc(bias_turned, 1)
            pe.wait_ge(K_zeroed, 2)
            run_bias_o(1)
            wait_h(0)
            pe.wait_ge(split_v, 1)
            for at, kind in enumerate(AHEAD):
                piece(kind, at, 0, 0, first=at < 2)

            def pair(layer, g, place, parity, embed=False):
                has_prev, has_next = place != "start", place != "end"
                base = piece_base(g)
                old_sets = layer + (0 if place == "first" else 1)
                new_sets = layer + (2 if place == "last" else 1)
                at = 0
                for k in range(UNITS):
                    run = pieces_of(k, has_prev, has_next)
                    scores(g, k, parity)
                    of_pair = parity if run == OWN else 1 - parity
                    if run:
                        if run[0] == ("f", 0):
                            wait_c(g - 1)
                            pe.wait_ge(split_1, old_sets)
                        elif run[0] == ("k", 0):
                            pe.wait_ge(split_qk, new_sets)
                        elif run[0] == ("v", 0):
                            wait_h(g + 1)
                            pe.wait_ge(split_v, new_sets)
                        piece(run[0], at, base, of_pair)
                        at += 1
                    if k > 0:
                        turn(g, k - 1, embed and k <= 4)
                    elif has_prev:
                        turn(g - 1, UNITS - 1)
                    if has_prev:
                        if k in (2, 3):
                            output_projection(g - 1, old_sets, [2 * (k - 2), 2 * (k - 2) + 1])
                    if k >= 2:
                        values(g, k - 2, parity)
                    elif has_prev:
                        values(g - 1, UNITS - 2 + k, 1 - parity)
                    if k == 6 and place == "first":
                        pe.wait_ge(bias_o_made, layer + 1)
                    if k in (6, 7) and has_prev:
                        feed_sum(g - 1, old_sets, [2 * (k - 6), 2 * (k - 6) + 1])
                    if run:
                        piece(run[1], at, base, of_pair)
                        at += 1
                    if k == 5 and place == "first":
                        run_bias_o(layer + 1)

            stream(pe, pair)
            g, sets = TOTAL - 1, L
            turn(g, UNITS - 1)
            values(g, UNITS - 2, 1)
            values(g, UNITS - 1, 1)
            output_projection(g, sets, list(range(JS)))
            wait_c(g)
            drain_base = piece_base(g) + (len(OWN) + FS) // 2
            for f in range(FS):
                piece(("f", f), f, drain_base, 1)
            feed_sum(g, sets, list(range(FS)))

        @block.vector
        def _(dve):
            def take_piece(kind, at, base, parity, of=None):
                name, n = kind
                bank = piece_ps[at % 2]
                if name == "k":
                    wait_piece(dve, base, at)
                    for h, rows in enumerate((slice(0, HEAD), slice(HEAD, P))):
                        last = dve.tensor_scalar(K[h][rows, n, :], bank[rows, :], bias_qkv[rows, 1, n:n + 1],
                                                 None, ALU.add)
                    last.then_inc(piece_free[at % 2], 1)
                elif kind == ("v", 3):
                    wait_piece(dve, base, at)
                    dve.tensor_copy(V[parity][n][:, :], bank[:, :]).then_inc(piece_free[at % 2], 1)
                elif name == "f":
                    wait_piece(dve, base, at)
                    if n < 2:
                        dve.wait_ge(c_lo_made, of + 1)
                    else:
                        dve.wait_ge(hidden_lo_made, of * FS + (n - 1))
                    dve.tensor_scalar(hidden[:, n % 2, :], bank[:, :], bias_1[:, n:n + 1], 0.0, ALU.add, ALU.max)\
                       .then_inc(piece_free[at % 2], 1)

            def hidden_lo_of(g, n):
                dve.wait_ge(hidden_hi_made, g * FS + (n + 1))
                dve.tensor_tensor(hidden_lo[:, n, :], hidden[:, n % 2, :], hidden_hi[:, n, :].bitcast(F32),
                                  ALU.subtract).then_inc(hidden_lo_made, 1)

            def mask_scores(g, k):
                unit = g * UNITS + k
                for q, (a, b) in enumerate(PARTS):
                    if q % 2 == 0:
                        count = settled(dve, unit * 2 + (q // 2 + 1))
                        dve.wait_ge(zeroed, 2)
                        dve.wait_ge(scored, count)
                    bank = score_ps[q // 2]
                    width = b - a
                    own = q % 2 * width
                    dve.tensor_tensor_reduce(
                        out=probs[k % 2][:, a:b], in0=bank[:, own:own + width], in1=mask[:, 2 * P - width:2 * P],
                        scale=SCALE, scalar=3.0e38, op0=ALU.add, op1=ALU.min,
                        accum_out=least[k % 2][:, q:q + 1]).then_inc(masked, 1)

            def invert(g, k):
                unit = g * UNITS + k
                dve.wait_ge(exped, unit * 4 + 4)
                dve.reciprocal(inverse[k % 2][:, :], sums[k % 2][:, :]).then_inc(inverted, 1)

            def take_turned(g, k):
                unit = g * UNITS + k
                dve.wait_ge(turned, unit * 2 + 2)
                dve.tensor_copy(probsT[k % 2][:, 0:4 * P], turn_ps[0][:, :]).then_inc(turned_out[0], 1)

            def take_heads(g, j):
                dve.wait_ge(headed, g * JS + (j + 1))
                if not (known(g, 0) and j < 2):
                    dve.wait_ge(O_lo_made, g * JS + (j - 1))
                dve.tensor_copy(O[:, j % 2, :], head_ps[:, :]).then_inc(O_made, 1)

            def residual_1(g):
                h = residual(g)
                dve.wait_ge(projected, g + 1)
                dve.scalar_tensor_tensor(out=h, in0=sum_ps[:, :], scalar=bias_o[:, 0:1], in1=h,
                                         op0=ALU.add, op1=ALU.add).then_inc(h1_made, 1)

            def split_c(g):
                dve.wait_ge(c_hi_made, g + 1)
                dve.tensor_tensor(c_lo[:, :], residual(g), c_hi[:, :].bitcast(F32),
                                  ALU.subtract).then_inc(c_lo_made, 1)

            def residual_2(g):
                h = residual(g)
                dve.wait_ge(fed, g + 1)
                dve.scalar_tensor_tensor(out=h, in0=sum_ps[:, :], scalar=bias_2[:, 0:1], in1=h,
                                         op0=ALU.add, op1=ALU.add).then_inc(h2_made, 1)

            def split_h(g, parity):
                dve.wait_ge(h_hi_made, g + 1)
                dve.tensor_tensor(h_lo[parity][:, :], residual(g),
                                  h_hi[parity][:, :].bitcast(F32), ALU.subtract).then_inc(h_lo_made, 1)

            n_j = JS * L
            by_kind = biasT[:, 0:4 * n_j].rearrange("p (t n) -> p t n", t=4)

            def split(layer, name):
                order = ("v", "q", "k", "1").index(name)
                dve.tensor_copy(w_hi[name][:, :], raw[name][:, :]).then_inc(hi_made, 1)
                dve.wait_ge(hi_made, layer * 4 + (order + 1))
                return dve.tensor_tensor(w_lo[name][:, :], raw[name][:, :], w_hi[name][:, :].bitcast(F32),
                                         ALU.subtract)

            def change_qk(layer, last_read=None):
                dve.wait_ge(weights_in, layer * (6 * DMA) + 6 * DMA)
                if last_read:
                    base, at = last_read
                    wait_copied(dve, base, at - 1)
                    wait_copied(dve, base, at)
                dve.tensor_copy(bias_qkv[:, :, :], by_kind[:, 0:3, bass.ds(layer * JS, JS)])
                split(layer, "q")
                split(layer, "k").then_inc(split_qk, 1)
                dve.wait_ge(split_qk, layer + 1)

            def change_v(layer):
                dve.wait_ge(weights_in, layer * (6 * DMA) + 6 * DMA)
                split(layer, "v").then_inc(split_v, 1)

            def split_rest(layer, name, hi, done):
                dve.wait_ge(hi, layer + 1)
                dve.tensor_tensor(w_lo[name][:, :], raw[name][:, :], w_hi[name][:, :].bitcast(F32),
                                  ALU.subtract).then_inc(done, 1)

            def change_1(layer, tiles=None):
                if tiles is not None:
                    dve.wait_ge(hidden_lo_made, tiles)
                dve.tensor_copy(bias_1[:, :], by_kind[:, 3, bass.ds(layer * JS, JS)])
                dve.tensor_copy(bias_2[:, :], columns(biasT, layer + (4 * n_j + L), 1))
                split(layer, "1").then_inc(split_1, 1)
                dve.wait_ge(split_1, layer + 1)

            def make_bias_o(layer):
                dve.wait_ge(bias_o_run, layer + 1)
                dve.tensor_tensor(bias_o[:, :], sum_ps[:, 0:1], columns(biasT, layer + 4 * n_j, 1), ALU.add)\
                   .then_inc(bias_o_made, 1)
                dve.wait_ge(bias_o_made, layer + 1)

            dve.memset(K[0][HEAD:P, :, :], 0.0).then_inc(K_zeroed, 1)
            dve.memset(K[1][0:HEAD, :, :], 0.0).then_inc(K_zeroed, 1)
            dve.memset(bias_o[:, :], 0.0).then_inc(h2_made, PAIRS)
            dve.wait_ge(h2_made, PAIRS)
            dve.wait_ge(K_zeroed, 2)
            dve.wait_ge(zeroed, 2)
            dve.wait_ge(bias_turned, 1)
            dve.tensor_copy(biasT[:, :], sum_ps[:, 0:N_BIAS]).then_inc(setup_done, 1)
            dve.wait_ge(setup_done, 1)
            change_v(0)
            change_qk(0)
            for g in range(2):
                split_h(g, g)
            change_1(0)
            split_rest(0, "o", hi_o, split_o)
            split_rest(0, "2", hi_2, split_2)
            make_bias_o(0)
            for at, kind in enumerate(AHEAD):
                take_piece(kind, at, 0, 0)

            def pair(layer, g, place, parity, embed=False):
                has_prev, has_next = place != "start", place != "end"
                base = piece_base(g)
                at = 0
                if place == "last":
                    change_v(layer + 1)
                for k in range(UNITS):
                    run = pieces_of(k, has_prev, has_next)
                    mask_scores(g, k)
                    if k in (6, 7) and has_prev:
                        hidden_lo_of(g - 1, 2 * (k - 6) + 1)
                    if run:
                        take_piece(run[0], at, base, 1 - parity, g - 1)
                        at += 1
                    if k > 0:
                        take_turned(g, k - 1)
                    elif has_prev:
                        take_turned(g - 1, UNITS - 1)
                    invert(g, k)
                    if k == 4 and has_prev:
                        split_c(g - 1)
                    if k == 5 and has_next:
                        split_h(g + 2, parity)
                    if k % 2 == 1:
                        if k >= 3:
                            take_heads(g, (k - 3) // 2)
                        elif has_prev:
                            take_heads(g - 1, JS - 1)
                    if k in (5, 6) and has_prev:
                        hidden_lo_of(g - 1, 2 * (k - 5))
                    if run:
                        take_piece(run[1], at, base, 1 - parity, g - 1)
                        at += 1
                    if k == 3 and has_prev:
                        residual_1(g - 1)
                    if k == 0 and place == "last":
                        change_qk(layer + 1, last_read=(base, OWN.index(("q", 3))))
                    if k == 5 and place == "first":
                        split_rest(layer, "o", hi_o, split_o)
                        make_bias_o(layer)
                    if k == 7 and has_prev:
                        residual_2(g - 1)
                if place == "first":
                    dve.wait_ge(h2_made, g + PAIRS)
                    change_1(layer, tiles=g * FS)
                    split_rest(layer, "2", hi_2, split_2)

            stream(dve, pair)
            g = TOTAL - 1
            take_turned(g, UNITS - 1)
            take_heads(g, JS - 1)
            residual_1(g)
            split_c(g)
            drain_base = piece_base(g) + (len(OWN) + FS) // 2
            for f in range(FS):
                take_piece(("f", f), f, drain_base, 1, g)
                hidden_lo_of(g, f)
            residual_2(g)

        @block.scalar
        def _(act):
            def take_piece(kind, at, base, parity, of=None):
                name, n = kind
                bank = piece_ps[at % 2]
                if name == "q":
                    wait_piece(act, base, at)
                    act.activation(Q[:, n, :], bank[:, :], ACT.Identity, bias=bias_qkv[:, 0, n:n + 1])\
                       .then_inc(piece_free[at % 2], 1)
                elif name == "v" and n < 3:
                    wait_piece(act, base, at)
                    act.activation(V[parity][n][:, :], bank[:, :], ACT.Copy).then_inc(piece_free[at % 2], 1)
                elif name == "f":
                    wait_copied(act, base, at)
                    act.activation(hidden_hi[:, n, :], hidden[:, n % 2, :], ACT.Copy).then_inc(hidden_hi_made, 1)

            def exponentials(g, k):
                unit = g * UNITS + k
                for q, (a, b) in enumerate(PARTS):
                    act.wait_ge(masked, unit * 4 + (q + 1))
                    own = probs[k % 2][:, a:b]
                    act.activation(own, own, ACT.Exp, bias=least[k % 2][:, q:q + 1], scale=-1.0,
                                   accum_out=sums[k % 2][:, q:q + 1]).then_inc(exped, 1)

            def take_turned(g, k, embed=False):
                unit = g * UNITS + k
                act.wait_ge(turned, unit * 2 + 1)
                if embed:
                    act.activation(columns(hT, g * PAIR + (2 * PAIR + k * P), P), turn_ps[1][:, SEQ:SEQ + P], ACT.Copy)
                act.activation(probsT[k % 2][:, 4 * P:6 * P], turn_ps[1][:, 0:2 * P], ACT.Copy)\
                   .then_inc(turned_out[1], 1)

            def split_c(g):
                act.wait_ge(h1_made, g + 1)
                act.activation(c_hi[:, :], residual(g), ACT.Copy).then_inc(c_hi_made, 1)

            def split_h(g, parity):
                act.wait_ge(h2_made, g + 1)
                act.activation(h_hi[parity][:, :], residual(g), ACT.Copy).then_inc(h_hi_made, 1)

            def take_heads(g, j):
                act.wait_ge(O_made, g * JS + (j + 1))
                act.activation(O_hi[:, j, :], O[:, j % 2, :], ACT.Copy).then_inc(O_hi_made, 1)

            def make_hi(name, made):
                act.activation(w_hi[name][:, :], raw[name][:, :], ACT.Copy).then_inc(made, 1)

            act.wait_ge(weights_in, 6 * DMA)
            make_hi("o", hi_o)
            for g in range(2):
                split_h(g, g)
            make_hi("2", hi_2)
            for at, kind in enumerate(AHEAD):
                take_piece(kind, at, 0, 0)

            def pair(layer, g, place, parity, embed=False):
                has_prev, has_next = place != "start", place != "end"
                base = piece_base(g)
                at = 0
                for k in range(UNITS):
                    run = pieces_of(k, has_prev, has_next)
                    exponentials(g, k)
                    if run:
                        take_piece(run[0], at, base, 1 - parity, g - 1)
                        at += 1
                    if k > 0:
                        take_turned(g, k - 1, embed and k <= 4)
                    elif has_prev:
                        take_turned(g - 1, UNITS - 1)
                    if k == 4 and has_prev:
                        split_c(g - 1)
                    if k == 4 and embed:
                        act.wait_ge(turned_out[1], g * UNITS + 4)
                    if k == 4 and has_next:
                        split_h(g + 2, parity)
                    if k == 4 and place == "first":
                        act.wait_ge(weights_in, layer * (6 * DMA) + 6 * DMA)
                        act.wait_ge(projected, g)
                        make_hi("o", hi_o)
                    if run:
                        take_piece(run[1], at, base, 1 - parity, g - 1)
                        at += 1
                    if k % 2 == 1 and (k >= 3 or has_prev):
                        take_heads(*((g, (k - 3) // 2) if k >= 3 else (g - 1, JS - 1)))
                if place == "first":
                    act.wait_ge(fed, g)
                    make_hi("2", hi_2)

            stream(act, pair)
            g = TOTAL - 1
            take_turned(g, UNITS - 1)
            take_heads(g, JS - 1)
            split_c(g)
            drain_base = piece_base(g) + (len(OWN) + FS) // 2
            for f in range(FS):
                take_piece(("f", f), f, drain_base, 1, g)


class Skewed:

    def __init__(self, pairs, unroll, depth):
        self.pairs, self.unroll, self.depth = pairs, unroll, depth

    def run(self, eng, step):
        head = -(-self.depth // self.unroll) * self.unroll
        for i in range(head):
            step(i, i % self.unroll)
        with eng.Fori(head // self.unroll, self.pairs // self.unroll) as r:
            for u in range(self.unroll):
                step(r * self.unroll + u, u)
        for i in range(self.pairs, self.pairs + self.depth):
            step(i, i % self.unroll)

    def has(self, i, lag, back=0):
        return not isinstance(i, int) or back <= i - lag < self.pairs


def norm_stage(nc, prefix, hT, X, ident, eps, recurrent=None, gate=None, beside=None):
    PAIRS = hT.shape[1] // PAIR
    T = PAIR // P
    NORMS = 2 if recurrent else 1
    skew = Skewed(PAIRS, 4, 4 if gate else 2)
    with ExitStack() as ctx:
        pool = Pools(nc, ctx, prefix)
        centre = pool.sbuf("centre", [P, P])
        mean = pool.sbuf("mean", [P, 1])
        ones = pool.sbuf("ones", [P, P])
        eps_of = [pool.sbuf(f"eps{n}", [P, 1]) for n in range(2)]
        c = [pool.sbuf(f"c{u}", [P, PAIR]) for u in range(4)]
        squared = [pool.sbuf(f"squared{p}", [P, PAIR]) for p in range(2)]
        root = [pool.sbuf(f"root{p}", [P, 2 * T]) for p in range(2)]
        inverse = [pool.sbuf(f"inverse{p}", [P, 2 * T]) for p in range(2)]
        diag = [[pool.sbuf(f"diag{n}{p}", [P, PAIR]) for p in range(2)] for n in range(NORMS)]
        x1 = [pool.sbuf(f"x1{p}", [P, PAIR]) for p in range(2)]
        x2 = [pool.sbuf(f"x2{p}", [P, PAIR]) for p in range(2)]
        c_ps = [pool.bank(f"c{p}") for p in range(2)]
        v_ps = [pool.bank(f"v{p}") for p in range(2)]
        spread_ps = [pool.bank(f"spread{n}") for n in range(NORMS)]
        made = pool.sem("made")
        vectors_in = pool.sem("vectors_in")
        centred = pool.sem("centred")
        c_out = pool.sem("c_out")
        squares = pool.sem("squares")
        varied = pool.sem("varied")
        roots = pool.sem("roots")
        inverses = pool.sem("inverses")
        diagonal = [pool.sem(f"diagonal{n}") for n in range(NORMS)]
        spread = [pool.sem(f"spread{n}") for n in range(NORMS)]
        x_made = [pool.sem(f"x_made{n}") for n in range(NORMS)]
        h_added = pool.sem("h_added")
        X_made = pool.sem("X_made")
        if recurrent:
            w_dram, b_dram = recurrent
            w_col = pool.sbuf("w_col", [P, 1])
            b_col = pool.sbuf("b_col", [P, 1])
        if gate:
            gate_w, gate_b, logits = gate
            E = gate_w.shape[1]
            gate_sb = pool.sbuf("gate_sb", [P, E])
            gate_col = pool.sbuf("gate_col", [E, 1])
            rowed = [pool.sbuf(f"rowed{p}", [E, PAIR]) for p in range(2)]
            l_ps = pool.bank("l")
            t_ps = pool.bank("t")
            l_made = pool.sem("l_made")
            l_out = pool.sem("l_out")
            t_made = pool.sem("t_made")
            t_out = pool.sem("t_out")
        block = ctx.enter_context(nc.Block())

        @block.sync
        def _(sp):
            if recurrent:
                sp.dma_start(w_col[:, :], w_dram.rearrange("(p o) -> p o", o=1)).then_inc(vectors_in, DMA)
                sp.dma_start(b_col[:, :], b_dram.rearrange("(p o) -> p o", o=1)).then_inc(vectors_in, DMA)
            if gate:
                sp.dma_start(gate_sb[:, :], gate_w).then_inc(vectors_in, DMA)
                sp.dma_start(gate_col[:, :], gate_b.rearrange("(p o) -> p o", o=1)).then_inc(vectors_in, DMA)
            if beside:
                beside(sp)

        @block.gpsimd
        def _(gp):
            if recurrent:
                def step(i, u):
                    if skew.has(i, 2):
                        gp.wait_ge(x_made[0], i - 1)
                        h = columns(hT, (i - 2) * PAIR, PAIR)
                        gp.tensor_tensor(h, h, x1[u % 2][:, :], ALU.add).then_inc(h_added, 1)

                skew.run(gp, step)

        @block.tensor
        def _(pe):
            pe.wait_ge(made, 5)
            pe.wait_ge(vectors_in, 2 * DMA)

            def step(i, u):
                p = u % 2
                if skew.has(i, 0):
                    if skew.has(i, 0, 2):
                        pe.wait_ge(c_out, i - 1)
                    pe.matmul(c_ps[p][:, :], centre[:, :], columns(hT, i * PAIR, PAIR),
                              start=True, stop=True).then_inc(centred, 1)
                if skew.has(i, 2):
                    for n in range(NORMS):
                        if skew.has(i, 2, 1):
                            pe.wait_ge(x_made[n], i - 2)
                        pe.wait_ge(diagonal[n], i - 1)
                        pe.matmul(spread_ps[n][:, :], ones[:, :], diag[n][p][:, :],
                                  start=True, stop=True).then_inc(spread[n], 1)
                if skew.has(i, 1):
                    if skew.has(i, 1, 2):
                        pe.wait_ge(roots, i - 2)
                    pe.wait_ge(squares, i)
                    for t in range(T):
                        last = pe.matmul(v_ps[1 - p][:, t:t + 1], squared[1 - p][:, t * P:(t + 1) * P],
                                         mean[:, :], start=True, stop=True)
                    last.then_inc(varied, 1)
                if gate and skew.has(i, 3):
                    if skew.has(i, 3, 1):
                        pe.wait_ge(l_out, i - 3)
                    pe.wait_ge(x_made[0], i - 2)
                    pe.matmul(l_ps[0:E, :], gate_sb[:, :], columns(X, (i - 3) * PAIR, PAIR),
                              start=True, stop=True).then_inc(l_made, 1)
                if gate and skew.has(i, 4):
                    count = settled(pe, i - 3)
                    count_out = settled(pe, i - 4)
                    pe.wait_ge(vectors_in, 2 * DMA)
                    if skew.has(i, 4, 1):
                        pe.wait_ge(t_out, count_out)
                    pe.wait_ge(l_out, count)
                    for t in range(T):
                        last = pe.transpose(t_ps[:, t * E:(t + 1) * E], rowed[p][:, t * P:(t + 1) * P],
                                            ident[0:E, 0:E])
                    last.then_inc(t_made, 1)

            skew.run(pe, step)

        @block.vector
        def _(dve):
            dve.memset(mean[:, :], 1.0 / P).then_inc(made, 1)
            dve.memset(ones[:, :], 1.0).then_inc(made, 1)
            dve.memset(eps_of[0][:, :], eps).then_inc(made, 1)
            dve.memset(eps_of[1][:, :], eps * eps).then_inc(made, 1)
            dve.tensor_scalar(centre[:, :], ident[:, :], 1.0 / P, None, ALU.subtract).then_inc(made, 1)

            def step(i, u):
                p = u % 2
                if skew.has(i, 2):
                    x_to = [x1[p][:, :] if recurrent else columns(X, (i - 2) * PAIR, PAIR), x2[p][:, :]]
                    if recurrent and skew.has(i, 2, 2):
                        dve.wait_ge(h_added, i - 3)
                        dve.wait_ge(X_made, i - 3)
                    for n in range(NORMS):
                        dve.wait_ge(spread[n], i - 1)
                        dve.tensor_tensor(x_to[n], spread_ps[n][:, :], c[(u + 2) % 4][:, :], ALU.mult)\
                           .then_inc(x_made[n], 1)
                if skew.has(i, 0):
                    dve.wait_ge(centred, i + 1)
                    if skew.has(i, 0, 4):
                        dve.wait_ge(squares, i - 3)
                        for n in range(NORMS):
                            dve.wait_ge(x_made[n], i - 3)
                    dve.tensor_copy(c[u][:, :], c_ps[p][:, :]).then_inc(c_out, 1)
                if skew.has(i, 1):
                    dve.wait_ge(roots, i)
                    if skew.has(i, 1, 2):
                        for n in range(NORMS):
                            dve.wait_ge(diagonal[n], i - 2)
                    dve.reciprocal(inverse[1 - p][:, 0:NORMS * T], root[1 - p][:, 0:NORMS * T]).then_inc(inverses, 1)
                    dve.wait_ge(inverses, i)
                    if skew.has(i, 1, 2):
                        dve.wait_ge(spread[0], i - 2)
                    for t in range(T):
                        last = dve.tensor_scalar(diag[0][1 - p][:, t * P:(t + 1) * P], ident[:, :],
                                                 inverse[1 - p][:, t:t + 1], None, ALU.mult)
                    last.then_inc(diagonal[0], 1)
                if gate and skew.has(i, 4):
                    dve.wait_ge(t_made, i - 3)
                    dve.tensor_copy(logits[:, bass.ds((i - 4) * (T * E), T * E)], t_ps[:, 0:T * E])\
                       .then_inc(t_out, 1)

            skew.run(dve, step)

        @block.scalar
        def _(act):
            act.wait_ge(made, 5)
            act.wait_ge(vectors_in, 2 * DMA)

            def step(i, u):
                p = u % 2
                if skew.has(i, 1):
                    act.wait_ge(varied, i)
                    if skew.has(i, 1, 2):
                        act.wait_ge(inverses, i - 2)
                    for n in range(NORMS):
                        last = act.activation(root[1 - p][:, n * T:(n + 1) * T], v_ps[1 - p][:, 0:T], ACT.Sqrt,
                                              bias=eps_of[n][:, :], scale=1.0 + n * eps)
                    last.then_inc(roots, 1)
                if skew.has(i, 0):
                    act.wait_ge(c_out, i + 1)
                    if skew.has(i, 0, 2):
                        act.wait_ge(varied, i - 1)
                    act.activation(squared[p][:, :], c[u][:, :], ACT.Square).then_inc(squares, 1)
                if recurrent and skew.has(i, 1):
                    act.wait_ge(inverses, i)
                    if skew.has(i, 1, 2):
                        act.wait_ge(spread[1], i - 2)
                    for t in range(T):
                        last = act.activation(diag[1][1 - p][:, t * P:(t + 1) * P], ident[:, :], ACT.Copy,
                                              scale=inverse[1 - p][:, T + t:T + t + 1])
                    last.then_inc(diagonal[1], 1)
                if recurrent and skew.has(i, 2):
                    act.wait_ge(x_made[1], i - 1)
                    act.activation(columns(X, (i - 2) * PAIR, PAIR), x2[p][:, :], ACT.Identity,
                                   bias=b_col[:, :], scale=w_col[:, :]).then_inc(X_made, 1)
                if gate and skew.has(i, 3):
                    act.wait_ge(l_made, i - 2)
                    if skew.has(i, 3, 2):
                        act.wait_ge(t_made, i - 4)
                    act.activation(rowed[1 - p][:, :], l_ps[0:E, :], ACT.Identity, bias=gate_col[:, :])\
                       .then_inc(l_out, 1)

            skew.run(act, step)


class RecurrentWeights:

    def __init__(self, pool, weights):
        self.dram = weights
        N = weights[6].shape[0]
        TAPS = weights[1].shape[2]
        self.w_in = pool.sbuf("w_in", [P, P])
        self.w_out = pool.sbuf("w_out", [P, N])
        self.B = pool.sbuf("B", [P, N])
        self.conv = pool.sbuf("conv", [N, N, TAPS])
        self.conv_bias = pool.sbuf("conv_bias", [N, 1])
        self.C_rows = [pool.sbuf(f"C_rows{t}", [N, P]) for t in range(2)]
        self.out_bias = pool.sbuf("out_bias", [P, 1])
        self.nu, self.theta, self.gamma = (pool.sbuf(name, [P, 1]) for name in ("nu", "theta", "gamma"))
        self.loaded = pool.sem("loaded")
        self.loads = 17

    def load(self, sp):
        W_in, conv_w, conv_b, nu_log, theta_log, gamma_log, B_re, B_im, C_re, C_im, W_out, b_out = self.dram
        N = B_re.shape[0]

        def column(v):
            return v.rearrange("(p o) -> p o", o=1)

        for dst, src in (
            (self.w_in[:, :], W_in), (self.w_out[:, :], W_out), (self.B[0:N, :], B_re), (self.B[N:P, :], B_im),
            (self.conv[:, :, :], conv_w), (self.conv_bias[:, :], column(conv_b)),
            (self.C_rows[0][:, 0:N], C_re), (self.C_rows[0][:, N:P], C_im),
            (self.C_rows[1][:, 0:N], C_im), (self.C_rows[1][:, N:P], C_re), (self.out_bias[:, :], column(b_out)),
            (self.nu[0:N, :], column(nu_log)), (self.nu[N:P, :], column(nu_log)),
            (self.theta[0:N, :], column(theta_log)), (self.theta[N:P, :], column(theta_log)),
            (self.gamma[0:N, :], column(gamma_log)), (self.gamma[N:P, :], column(gamma_log)),
        ):
            sp.dma_start(dst, src).then_inc(self.loaded, DMA)


def recurrent_stage(nc, hT, X, ident, weights):
    N = weights.B.shape[1]
    TAPS = weights.conv.shape[2]
    BEFORE = (TAPS - 1) // 2
    PADDED = SEQ + TAPS - 1
    PAIRS = hT.shape[1] // PAIR
    TWO_PI_HI = 6.28125
    TWO_PI_LO = 0.0019353071795864769
    skew = Skewed(PAIRS, 4, 3)
    with ExitStack() as ctx:
        pool = Pools(nc, ctx, "rec")
        w_in, w_out, B, conv, conv_bias = weights.w_in, weights.w_out, weights.B, weights.conv, weights.conv_bias
        C_rows, out_bias = weights.C_rows, weights.out_bias
        nu, theta, gamma, loaded = weights.nu, weights.theta, weights.gamma, weights.loaded
        w_inT = pool.sbuf("w_inT", [P, P])
        w_outT = pool.sbuf("w_outT", [P, P])
        BT = pool.sbuf("BT", [N, P])
        taps = [pool.sbuf(f"taps{t}", [P, P]) for t in range(3)]
        C_cos = pool.sbuf("C_cos", [P, N])
        C_sin = pool.sbuf("C_sin", [P, N])
        tiny = [pool.sbuf(f"tiny{t}", [P, 1]) for t in range(8)]
        turns_i = pool.sbuf("turns_i", [P, 1], I32)
        cos = pool.sbuf("cos", [P, 2, SEQ])
        sin = pool.sbuf("sin", [P, 2, SEQ])
        part = [pool.sbuf(f"part{t}", [P, SEQ]) for t in range(2)]
        decay = pool.sbuf("decay", [P, 2, SEQ])
        bias_B = pool.sbuf("bias_B", [P, 1])
        bias_im = pool.sbuf("bias_im", [P, 1])
        bias_re = pool.sbuf("bias_re", [P, 1])

        v_pad = [pool.sbuf(f"v_pad{u}", [P, 2, PADDED]) for u in range(2)]
        gated = [pool.sbuf(f"gated{u}", [N, PAIR]) for u in range(4)]
        Bv = [pool.sbuf(f"Bv{u}", [P, PAIR]) for u in range(2)]
        Bv_turned = [pool.sbuf(f"Bv_turned{u}", [P, PAIR]) for u in range(2)]
        drive_c = pool.sbuf("drive_c", [P, PAIR])
        drive_s = [pool.sbuf(f"drive_s{u}", [P, PAIR]) for u in range(2)]
        drive = pool.sbuf("drive", [P, PAIR])
        state = [pool.sbuf(f"state{u}", [P, PAIR]) for u in range(2)]
        state_c = [pool.sbuf(f"state_c{u}", [P, PAIR]) for u in range(2)]
        state_s = [pool.sbuf(f"state_s{u}", [P, PAIR]) for u in range(2)]
        product = [pool.sbuf(f"product{u}", [P, PAIR]) for u in range(2)]
        in_ps = [pool.bank(f"in{u}") for u in range(2)]
        B_ps = [pool.bank(f"B{u}") for u in range(2)]
        y_ps = [pool.bank(f"y{u}") for u in range(2)]
        o_ps = [pool.bank(f"o{u}") for u in range(2)]

        exped = pool.sem("exped")
        chain = pool.sem("chain")
        sined = pool.sem("sined")
        folded = pool.sem("folded")
        angles = pool.sem("angles")
        tabled = pool.sem("tabled")
        zeroed = pool.sem("zeroed")
        projected = pool.sem("projected")
        gelued = pool.sem("gelued")
        v_low = pool.sem("v_low")
        v_high = pool.sem("v_high")
        driven = pool.sem("driven")
        Bv_made = pool.sem("Bv_made")
        cos_made = pool.sem("cos_made")
        sin_made = pool.sem("sin_made")
        drive_made = pool.sem("drive_made")
        scanned = pool.sem("scanned")
        state_c_made = pool.sem("state_c_made")
        state_s_made = pool.sem("state_s_made")
        y_made = pool.sem("y_made")
        product_made = pool.sem("product_made")
        o_made = pool.sem("o_made")
        h_made = pool.sem("h_made")
        block = ctx.enter_context(nc.Block())

        @block.gpsimd
        def _(gp):
            for u in range(2):
                gp.memset(v_pad[u][:, :, :], 0.0).then_inc(zeroed, 1)
                gp.memset(product[u][:, :], 0.0).then_inc(zeroed, 1)
            gp.memset(w_outT[:, :], 0.0).then_inc(zeroed, 1)
            gp.memset(taps[2][:, :], 0.0).then_inc(zeroed, 1)
            gp.wait_ge(tabled, 3)

            def step(i, u):
                p = u % 2
                if skew.has(i, 2):
                    gp.wait_ge(Bv_made, (i - 1) * 3)
                    if skew.has(i, 2, 2):
                        gp.wait_ge(drive_made, i - 3)
                    gp.tensor_tensor(drive_s[p][:, :], Bv_turned[p][:, :],
                                     sin[:, :, :].rearrange("p s t -> p (s t)"), ALU.mult).then_inc(sin_made, 1)
                    gp.wait_ge(scanned, i - 1)
                    if skew.has(i, 2, 2):
                        gp.wait_ge(y_made, i - 3)
                    gp.tensor_tensor(state_s[p][:, :], state[p][:, :],
                                     sin[:, :, :].rearrange("p s t -> p (s t)"), ALU.mult).then_inc(state_s_made, 1)

            skew.run(gp, step)

        @block.scalar
        def _(act):
            act.wait_ge(loaded, weights.loads * DMA)
            act.activation(tiny[0][:, :], nu[:, :], ACT.Exp).then_inc(exped, 1)
            act.activation(theta[:, :], theta[:, :], ACT.Exp).then_inc(exped, 1)
            act.activation(gamma[:, :], gamma[:, :], ACT.Exp).then_inc(exped, 1)
            act.wait_ge(exped, 3)
            act.activation(nu[:, :], tiny[0][:, :], ACT.Exp, scale=-1.0).then_inc(exped, 1)
            act.wait_ge(angles, 1)
            act.activation(tiny[1][:, :], theta[:, :], ACT.Sin, scale=0.5).then_inc(sined, 1)
            act.activation(tiny[2][:, :], theta[:, :], ACT.Sin, scale=0.25).then_inc(sined, 1)
            act.wait_ge(tabled, 3)

            def step(i, u):
                p = u % 2
                if skew.has(i, 0):
                    act.wait_ge(projected, i + 1)
                    if skew.has(i, 0, 4):
                        act.wait_ge(product_made, i - 3)
                    act.activation(gated[u][:, :], in_ps[p][0:N, :], ACT.Gelu).then_inc(gelued, 1)
                    act.wait_ge(v_low, i + 1)
                    act.activation(v_pad[p][N:P, :, BEFORE - 1:BEFORE - 1 + SEQ],
                                   v_pad[p][0:N, :, BEFORE:BEFORE + SEQ], ACT.Copy).then_inc(v_high, 1)
                if skew.has(i, 1):
                    q = 1 - p
                    act.wait_ge(driven, i)
                    if skew.has(i, 1, 2):
                        act.wait_ge(cos_made, i - 2)
                        act.wait_ge(sin_made, i - 2)
                    act.activation(Bv[q][:, :], B_ps[q][:, :], ACT.Identity, bias=bias_B[:, :]).then_inc(Bv_made, 1)
                    act.activation(Bv_turned[q][0:N, :], B_ps[q][N:P, :], ACT.Identity,
                                   bias=bias_im[N:P, :]).then_inc(Bv_made, 1)
                    act.activation(Bv_turned[q][N:P, :], B_ps[q][0:N, :], ACT.Identity,
                                   bias=bias_re[0:N, :], scale=-1.0).then_inc(Bv_made, 1)

            skew.run(act, step)

        @block.tensor
        def _(pe):
            pe.wait_ge(loaded, weights.loads * DMA)
            pe.transpose(in_ps[0][:, 0:P], w_in[:, :], ident[:, :]).then_inc(folded, 1)
            pe.transpose(in_ps[1][0:N, 0:P], w_out[:, :], ident[:, :]).then_inc(folded, 1)
            pe.transpose(y_ps[0][:, 0:N], C_rows[0][:, :], ident[0:N, 0:N]).then_inc(folded, 1)
            pe.transpose(y_ps[1][:, 0:N], C_rows[1][:, :], ident[0:N, 0:N]).then_inc(folded, 1)
            pe.wait_ge(tabled, 1)
            pe.transpose(B_ps[0][0:N, 0:P], B[:, :], ident[:, :]).then_inc(folded, 1)
            pe.wait_ge(tabled, 2)
            for k in range(TAPS):
                bank, at = (o_ps[0], k * P) if k < 4 else (o_ps[1], 0)
                last = pe.matmul(bank[0:N, at:at + P], conv[:, :, k], BT[:, :], start=True, stop=True)
            pe.matmul(B_ps[1][:, 0:1], BT[:, :], conv_bias[:, :], start=True, stop=True).then_inc(folded, 1)
            pe.wait_ge(tabled, 3)

            def step(i, u):
                p = u % 2
                q = 1 - p
                if skew.has(i, 3):
                    if skew.has(i, 3, 2):
                        pe.wait_ge(product_made, i - 4)
                    pe.wait_ge(state_c_made, i - 2)
                    pe.wait_ge(state_s_made, i - 2)
                    pe.matmul(y_ps[q][0:N, :], C_cos[:, :], state_c[q][:, :], start=True, stop=False)
                    pe.matmul(y_ps[q][0:N, :], C_sin[:, :], state_s[q][:, :], start=False, stop=True)\
                      .then_inc(y_made, 1)
                if skew.has(i, 0):
                    if skew.has(i, 0, 2):
                        pe.wait_ge(gelued, i - 1)
                        pe.wait_ge(v_high, i - 1)
                        pe.wait_ge(v_low, i - 1)
                    pe.matmul(in_ps[p][:, :], w_inT[:, :], columns(X, i * PAIR, PAIR),
                              start=True, stop=True).then_inc(projected, 1)
                if skew.has(i, 3):
                    if skew.has(i, 3, 2):
                        pe.wait_ge(h_made, i - 4)
                    pe.wait_ge(product_made, i - 2)
                    pe.matmul(o_ps[q][:, :], w_outT[:, :], product[q][:, :], start=True, stop=True)\
                      .then_inc(o_made, 1)
                if skew.has(i, 1):
                    if skew.has(i, 1, 2):
                        pe.wait_ge(Bv_made, (i - 2) * 3)
                    pe.wait_ge(v_high, i)
                    pe.wait_ge(v_low, i)
                    for t in range(3):
                        last = pe.matmul(B_ps[q][:, :], taps[t][:, :], v_pad[q][:, :, 2 * t:2 * t + SEQ],
                                         start=(t == 0), stop=(t == 2))
                    last.then_inc(driven, 1)

            skew.run(pe, step)

        @block.vector
        def _(dve):
            count = [0]

            def chained(instruction):
                count[0] += 1
                instruction.then_inc(chain, 1)
                dve.wait_ge(chain, count[0])

            dve.wait_ge(exped, 4)
            dve.tensor_scalar(B[:, :], B[:, :], gamma[:, 0:1], None, ALU.mult).then_inc(tabled, 1)
            chained(dve.tensor_scalar(tiny[3][:, :], theta[:, :], 1.0 / (TWO_PI_HI + TWO_PI_LO), None, ALU.mult))
            chained(dve.tensor_copy(turns_i[:, :], tiny[3][:, :]))
            chained(dve.tensor_copy(tiny[3][:, :], turns_i[:, :]))
            chained(dve.tensor_scalar(tiny[4][:, :], tiny[3][:, :], TWO_PI_HI, None, ALU.mult))
            chained(dve.tensor_tensor(theta[:, :], theta[:, :], tiny[4][:, :], ALU.subtract))
            chained(dve.tensor_scalar(tiny[4][:, :], tiny[3][:, :], TWO_PI_LO, None, ALU.mult))
            dve.tensor_tensor(theta[:, :], theta[:, :], tiny[4][:, :], ALU.subtract).then_inc(angles, 1)
            dve.wait_ge(sined, 2)
            half_sin, quarter_sin, half_cos, c_step, s_step, spare = (tiny[t] for t in (1, 2, 3, 4, 5, 6))
            chained(dve.tensor_tensor(spare[:, :], quarter_sin[:, :], quarter_sin[:, :], ALU.mult))
            chained(dve.tensor_scalar(half_cos[:, :], spare[:, :], -2.0, 1.0, ALU.mult, ALU.add))
            chained(dve.scalar_tensor_tensor(out=s_step[:, :], in0=half_sin[:, :], scalar=2.0,
                                             in1=half_cos[:, :], op0=ALU.mult, op1=ALU.mult))
            chained(dve.tensor_tensor(spare[:, :], half_sin[:, :], half_sin[:, :], ALU.mult))
            chained(dve.tensor_scalar(c_step[:, :], spare[:, :], -2.0, 1.0, ALU.mult, ALU.add))
            chained(dve.memset(cos[:, 0, 0:1], 1.0))
            chained(dve.memset(sin[:, 0, 0:1], 0.0))
            width = 1
            while width < SEQ:
                c0, s0 = cos[:, 0, 0:width], sin[:, 0, 0:width]
                c1, s1 = cos[:, 0, width:2 * width], sin[:, 0, width:2 * width]
                chained(dve.tensor_scalar(part[0][:, 0:width], s0, s_step[:, 0:1], None, ALU.mult))
                chained(dve.scalar_tensor_tensor(out=c1, in0=c0, scalar=c_step[:, 0:1],
                                                 in1=part[0][:, 0:width], op0=ALU.mult, op1=ALU.subtract))
                chained(dve.tensor_scalar(part[1][:, 0:width], c0, s_step[:, 0:1], None, ALU.mult))
                chained(dve.scalar_tensor_tensor(out=s1, in0=s0, scalar=c_step[:, 0:1],
                                                 in1=part[1][:, 0:width], op0=ALU.mult, op1=ALU.add))
                chained(dve.tensor_tensor(spare[:, :], s_step[:, :], s_step[:, :], ALU.mult))
                chained(dve.scalar_tensor_tensor(out=s_step[:, :], in0=s_step[:, :], scalar=2.0,
                                                 in1=c_step[:, :], op0=ALU.mult, op1=ALU.mult))
                chained(dve.tensor_scalar(c_step[:, :], spare[:, :], -2.0, 1.0, ALU.mult, ALU.add))
                width *= 2
            chained(dve.tensor_copy(cos[:, 1, :], cos[:, 0, :]))
            chained(dve.tensor_copy(sin[:, 1, :], sin[:, 0, :]))
            chained(dve.memset(decay[:, :, :], 1.0))
            chained(dve.tensor_scalar(decay[:, :, :], decay[:, :, :], nu[:, 0:1], None, ALU.mult))
            chained(dve.memset(decay[:, :, 0:1], 0.0))
            dve.wait_ge(folded, 5)
            dve.tensor_copy(BT[:, :], B_ps[0][0:N, 0:P]).then_inc(tabled, 1)
            dve.wait_ge(zeroed, 6)
            dve.tensor_copy(w_inT[:, :], in_ps[0][:, 0:P])
            dve.tensor_copy(w_outT[0:N, :], in_ps[1][0:N, 0:P])
            dve.tensor_copy(C_cos[0:N, :], y_ps[0][0:N, 0:N])
            dve.tensor_scalar(C_cos[N:P, :], y_ps[0][N:P, 0:N], -1.0, None, ALU.mult)
            dve.tensor_scalar(C_sin[:, :], y_ps[1][:, 0:N], -1.0, None, ALU.mult)
            dve.wait_ge(folded, 6)
            for k in range(TAPS):
                bank, at = (o_ps[0], k * P) if k < 4 else (o_ps[1], 0)
                low = k % 2 * N
                dve.tensor_copy(taps[k // 2][low:low + N, :], bank[0:N, at:at + P])
            dve.tensor_copy(bias_B[:, :], B_ps[1][:, 0:1])
            for low in (0, N):
                dve.tensor_copy(bias_im[low:low + N, :], B_ps[1][N:P, 0:1])
                last = dve.tensor_scalar(bias_re[low:low + N, :], B_ps[1][0:N, 0:1], -1.0, None, ALU.mult)
            last.then_inc(tabled, 1)

            cos_flat = cos[:, :, :].rearrange("p s t -> p (s t)")
            decay_flat = decay[:, :, :].rearrange("p s t -> p (s t)")

            def step(i, u):
                p = u % 2
                q = 1 - p
                if skew.has(i, 3):
                    dve.wait_ge(y_made, i - 2)
                    if skew.has(i, 3, 2):
                        dve.wait_ge(o_made, i - 4)
                    dve.tensor_tensor(product[q][0:N, :], y_ps[q][0:N, :], gated[(u + 1) % 4][:, :], ALU.mult)\
                       .then_inc(product_made, 1)
                if skew.has(i, 0):
                    dve.wait_ge(projected, i + 1)
                    dve.tensor_copy(v_pad[p][0:N, :, BEFORE:BEFORE + SEQ],
                                    in_ps[p][N:P, :].rearrange("p (s t) -> p s t", s=2)).then_inc(v_low, 1)
                if skew.has(i, 2):
                    dve.wait_ge(Bv_made, (i - 1) * 3)
                    dve.tensor_tensor(drive_c[:, :], Bv[p][:, :], cos_flat, ALU.mult).then_inc(cos_made, 1)
                    dve.wait_ge(cos_made, i - 1)
                    dve.wait_ge(sin_made, i - 1)
                    dve.tensor_tensor(drive[:, :], drive_c[:, :], drive_s[p][:, :], ALU.add).then_inc(drive_made, 1)
                    dve.wait_ge(drive_made, i - 1)
                    if skew.has(i, 2, 2):
                        dve.wait_ge(state_s_made, i - 3)
                    dve.tensor_tensor_scan(state[p][:, :], decay_flat, drive[:, :], 0.0, ALU.mult, ALU.add)\
                       .then_inc(scanned, 1)
                    dve.wait_ge(scanned, i - 1)
                    if skew.has(i, 2, 2):
                        dve.wait_ge(y_made, i - 3)
                    dve.tensor_tensor(state_c[p][:, :], state[p][:, :], cos_flat, ALU.mult)\
                       .then_inc(state_c_made, 1)
                if skew.has(i, 3):
                    dve.wait_ge(o_made, i - 2)
                    h = columns(hT, (i - 3) * PAIR, PAIR)
                    dve.scalar_tensor_tensor(out=h, in0=o_ps[q][:, :], scalar=out_bias[:, 0:1], in1=h,
                                             op0=ALU.add, op1=ALU.add).then_inc(h_made, 1)

            skew.run(dve, step)


def routing_stage(nc, logits, routes, tiles, E):
    with ExitStack() as ctx:
        pool = Pools(nc, ctx, "rou")
        W = tiles * E
        rank_i = pool.sbuf("rank_i", [P, W], I32)
        rank = pool.sbuf("rank", [P, W])
        reaches = pool.sbuf("reaches", [P, W])
        taken = pool.sbuf("taken", [P, W])
        rest = pool.sbuf("rest", [P, W])
        second = pool.sbuf("second", [P, W])
        top = [pool.sbuf(f"top{n}", [P, tiles]) for n in range(2)]
        best = pool.sbuf("best", [P, tiles])
        gap = pool.sbuf("gap", [P, tiles])
        ratio = pool.sbuf("ratio", [P, tiles])
        total = pool.sbuf("total", [P, tiles])
        share = [pool.sbuf(f"share{n}", [P, tiles]) for n in range(2)]
        ranked = pool.sem("ranked")
        chain = pool.sem("chain")
        gaps = pool.sem("gaps")
        ratios = pool.sem("ratios")
        block = ctx.enter_context(nc.Block())

        def by_tile(x):
            return x[:, :].rearrange("p (t e) -> p t e", e=E)

        def spread(x):
            return x[:, :].unsqueeze(2).to_broadcast([P, tiles, E])

        @block.gpsimd
        def _(gp):
            gp.iota(by_tile(rank_i), pattern=[[0, tiles], [-1, E]], base=E, channel_multiplier=0).then_inc(ranked, 1)

        @block.scalar
        def _(act):
            act.wait_ge(gaps, 1)
            act.activation(ratio[:, :], gap[:, :], ACT.Exp).then_inc(ratios, 1)

        @block.vector
        def _(dve):
            count = [0]

            def chained(instruction):
                count[0] += 1
                instruction.then_inc(chain, 1)
                dve.wait_ge(chain, count[0])

            def take_best(values, n, out):
                chained(dve.tensor_reduce(top[n][:, :], by_tile(values), AX.X, ALU.max))
                chained(dve.tensor_tensor(by_tile(reaches), by_tile(values), spread(top[n]), ALU.is_equal))
                chained(dve.tensor_tensor(reaches[:, :], reaches[:, :], rank[:, :], ALU.mult))
                chained(dve.tensor_reduce(best[:, :], by_tile(reaches), AX.X, ALU.max))
                chained(dve.tensor_tensor(by_tile(out), by_tile(rank), spread(best), ALU.is_equal))

            dve.wait_ge(ranked, 1)
            chained(dve.tensor_copy(rank[:, :], rank_i[:, :]))
            take_best(logits, 0, taken)
            chained(dve.scalar_tensor_tensor(out=rest[:, :], in0=taken[:, :], scalar=-3.0e38, in1=logits[:, :],
                                             op0=ALU.mult, op1=ALU.add))
            take_best(rest, 1, second)
            dve.tensor_tensor(gap[:, :], top[1][:, :], top[0][:, :], ALU.subtract).then_inc(gaps, 1)
            dve.wait_ge(ratios, 1)
            chained(dve.tensor_scalar(total[:, :], ratio[:, :], 1.0, None, ALU.add))
            chained(dve.reciprocal(share[0][:, :], total[:, :]))
            chained(dve.tensor_tensor(share[1][:, :], share[0][:, :], ratio[:, :], ALU.mult))
            chained(dve.tensor_tensor(by_tile(taken), by_tile(taken), spread(share[0]), ALU.mult))
            chained(dve.tensor_tensor(by_tile(second), by_tile(second), spread(share[1]), ALU.mult))
            chained(dve.tensor_tensor(routes[:, :], taken[:, :], second[:, :], ALU.add))


class ExpertWeights:

    def __init__(self, pool, weights):
        self.dram = weights
        w1, b1, w2, b2 = weights
        E, _, F2 = w1.shape
        FS = F2 // P
        self.w1 = pool.sbuf("expert_w1", [P, E, F2])
        self.b1_rows = pool.sbuf("expert_b1", [E * FS, P])
        self.w2 = pool.sbuf("expert_w2", [P, E, FS, P])
        self.loaded = pool.sem("expert_weights_in")
        self.loads = 2 + E

    def load(self, sp):
        w1, b1, w2, b2 = self.dram
        sp.dma_start(self.w1[:, :, :], w1.rearrange("e d f -> d e f")).then_inc(self.loaded, DMA)
        sp.dma_start(self.b1_rows[:, :], b1.rearrange("e (f p) -> (e f) p", p=P)).then_inc(self.loaded, DMA)
        for e in range(self.w1.shape[1]):
            sp.dma_start(self.w2[:, e, :, :], w2[e].rearrange("(f p) d -> p f d", p=P)).then_inc(self.loaded, DMA)


def experts_stage(nc, hT, X, routes, ident, weights, out):
    w1, b1, w2, b2 = weights.dram
    E, D, F2 = w1.shape
    FS = F2 // P
    T = PAIR // P
    PAIRS = hT.shape[1] // PAIR
    assert FS == 2 and T * E <= P
    out_v = out.rearrange("(i t p) d -> i p t d", t=T, p=P)
    with ExitStack() as ctx:
        pool = Pools(nc, ctx, "exp")
        w1_raw, b1_rows, w2_sb = weights.w1, weights.b1_rows, weights.w2
        w1_hi = pool.sbuf("w1_hi", [P, E, F2], F32R)
        w1_lo = pool.sbuf("w1_lo", [P, E, F2], F32R)
        b1_col = pool.sbuf("b1_col", [P, E * FS])
        b2_tiles = pool.sbuf("b2_tiles", [P, T, P])
        x_hi = [pool.sbuf(f"x_hi{p}", [P, PAIR], F32R) for p in range(2)]
        x_lo = [pool.sbuf(f"x_lo{p}", [P, PAIR], F32R) for p in range(2)]
        h_now = [pool.sbuf(f"h_now{p}", [P, PAIR]) for p in range(2)]
        route_now = [pool.sbuf(f"route_now{p}", [P, P]) for p in range(2)]
        routeT = [pool.sbuf(f"routeT{p}", [P, P]) for p in range(2)]
        hidden = [[pool.sbuf(f"hidden{p}{f}", [P, PAIR]) for f in range(FS)] for p in range(2)]
        total = [pool.sbuf(f"total{p}", [P, T, P]) for p in range(2)]
        hidden_ps = [[pool.bank(f"hidden{p}{f}") for f in range(FS)] for p in range(2)]
        y_ps = [pool.bank(f"y{p}") for p in range(2)]
        start_ps = pool.bank("start")
        route_ps = pool.bank("route")

        zeroed = pool.sem("zeroed")
        b2_in = pool.sem("b2_in")
        b1_turned = pool.sem("b1_turned")
        hi_made = pool.sem("hi_made")
        ready = pool.sem("ready")
        x_hi_made = pool.sem("x_hi_made")
        x_lo_made = pool.sem("x_lo_made")
        now_made = pool.sem("now_made")
        route_turned = pool.sem("route_turned")
        routeT_made = pool.sem("routeT_made")
        started = pool.sem("started")
        start_out = pool.sem("start_out")
        hidden_run = pool.sem("hidden_run")
        hidden_out = pool.sem("hidden_out")
        y_run = pool.sem("y_run")
        y_added = pool.sem("y_added")
        stored = [pool.sem(f"stored{p}") for p in range(2)]
        block = ctx.enter_context(nc.Block())

        def rounds(eng, pair):
            pair(0, 0)
            pair(1, 1)
            with eng.Fori(1, PAIRS // 2) as r:
                pair(r * 2, 0)
                pair(r * 2 + 1, 1)

        def known(i):
            return isinstance(i, int)

        @block.sync
        def _(sp):
            sp.wait_ge(zeroed, 3)
            for t in range(T):
                sp.dma_start(b2_tiles[t * E:(t + 1) * E, t, :], b2).then_inc(b2_in, DMA)

            def pair(i, p):
                sp.wait_ge(y_added, i * (E * T) + E * T)
                sp.dma_start(out_v[bass.ds(i, 1), :, :, :].rearrange("i p t d -> p (i t) d"),
                             total[p][:, :, :]).then_inc(stored[p], DMA)

            rounds(sp, pair)
            for p in range(2):
                sp.wait_ge(stored[p], PAIRS // 2 * DMA)

        @block.gpsimd
        def _(gp):
            gp.memset(b2_tiles[:, :, :], 0.0).then_inc(zeroed, 1)
            for p in range(2):
                gp.memset(route_now[p][:, :], 0.0).then_inc(zeroed, 1)
            gp.wait_ge(zeroed, 3)

            def pair(i, p):
                if not known(i):
                    gp.wait_ge(started, i - 1)
                    gp.wait_ge(y_added, i * (E * T) - E * T)
                gp.tensor_copy(h_now[p][:, :], columns(hT, i * PAIR, PAIR)).then_inc(now_made, 1)
                gp.tensor_copy(route_now[p][:, 0:T * E], columns(routes, i * (T * E), T * E)).then_inc(now_made, 1)

            rounds(gp, pair)

        @block.tensor
        def _(pe):
            def begin(i, p):
                pe.wait_ge(now_made, i * 2 + 2)
                if not (known(i) and i == 0):
                    pe.wait_ge(routeT_made, i)
                pe.transpose(route_ps[:, 0:P], route_now[p][:, :], ident[:, :]).then_inc(route_turned, 1)

            def start(i, p):
                if not (known(i) and i == 0):
                    pe.wait_ge(start_out, i)
                pe.wait_ge(routeT_made, i + 1)
                for t in range(T):
                    tile = start_ps[:, t * P:(t + 1) * P]
                    pe.matmul(tile, routeT[p][:, :], b2_tiles[:, t, :], start=True, stop=False)
                    last = pe.matmul(tile, h_now[p][:, t * P:(t + 1) * P], ident[:, :], start=False, stop=True)
                last.then_inc(started, 1)

            def first(i, e, p, f):
                unit = i * E + e
                if f == 0 and e == 0:
                    pe.wait_ge(x_hi_made, i + 1)
                    pe.wait_ge(x_lo_made, i + 1)
                if not (known(i) and unit < 2):
                    pe.wait_ge(hidden_out, unit * 2 + (f - 3))
                cols = slice(f * P, (f + 1) * P)
                bank = hidden_ps[e % 2][f][:, :]
                pe.matmul(bank, w1_hi[:, e, cols], x_hi[p][:, :], start=True, stop=False)
                pe.matmul(bank, w1_hi[:, e, cols], x_lo[p][:, :], start=False, stop=False)
                pe.matmul(bank, w1_lo[:, e, cols], x_hi[p][:, :], start=False, stop=True).then_inc(hidden_run, 1)

            def second(i, e, tiles):
                unit = i * E + e
                if tiles[0] == 0:
                    pe.wait_ge(hidden_out, unit * 2 + 2)
                    if not (known(i) and unit < 2):
                        pe.wait_ge(y_added, unit * T + (T - 2 * T))
                for t in tiles:
                    for f in range(FS):
                        last = pe.matmul(y_ps[e % 2][:, t * P:(t + 1) * P],
                                         hidden[e % 2][f][:, t * P:(t + 1) * P], w2_sb[:, e, f, :],
                                         start=(f == 0), stop=(f == FS - 1))
                if tiles[-1] == T - 1:
                    last.then_inc(y_run, 1)

            pe.wait_ge(weights.loaded, weights.loads * DMA)
            pe.transpose(start_ps[:, 0:E * FS], b1_rows[:, :], ident[0:E * FS, 0:E * FS]).then_inc(b1_turned, 1)
            pe.wait_ge(ready, 1)
            pe.wait_ge(b2_in, T * DMA)

            def pair(i, p):
                begin(i, p)
                for e in range(E):
                    before = (i, e - 1) if e > 0 else (None if known(i) and i == 0 else (i - 1, E - 1))
                    first(i, e, p, 0)
                    if before:
                        second(*before, [0, 1])
                    first(i, e, p, 1)
                    if e == 0:
                        start(i, p)
                    if before:
                        second(*before, [2, 3])

            rounds(pe, pair)
            second(PAIRS - 1, E - 1, list(range(T)))

        @block.scalar
        def _(act):
            act.wait_ge(ready, 1)

            def split(i, p):
                if not known(i):
                    act.wait_ge(hidden_run, i * (E * 2) - E * 2)
                act.activation(x_hi[p][:, :], columns(X, i * PAIR, PAIR), ACT.Copy).then_inc(x_hi_made, 1)

            split(0, 0)

            def pair(i, p):
                act.wait_ge(route_turned, i + 1)
                act.activation(routeT[p][:, :], route_ps[:, 0:P], ACT.Copy).then_inc(routeT_made, 1)
                for e in range(E):
                    unit = i * E + e
                    for f in range(FS):
                        act.wait_ge(hidden_run, unit * 2 + (f + 1))
                        if f == 0 and not (known(i) and unit < 2):
                            act.wait_ge(y_run, unit - 1)
                        act.activation(hidden[e % 2][f][:, :], hidden_ps[e % 2][f][:, :], ACT.Relu,
                                       bias=b1_col[:, e * FS + f:e * FS + f + 1]).then_inc(hidden_out, 1)
                    if e == 4 and not (known(i) and i == PAIRS - 1):
                        split(i + 1, 1 - p)

            pair(0, 0)
            with act.Fori(0, PAIRS // 2 - 1) as r:
                pair(r * 2 + 1, 1)
                pair(r * 2 + 2, 0)
            pair(PAIRS - 1, 1)

        @block.vector
        def _(dve):
            def split(i, p):
                dve.wait_ge(x_hi_made, i + 1)
                dve.tensor_tensor(x_lo[p][:, :], columns(X, i * PAIR, PAIR), x_hi[p][:, :].bitcast(F32),
                                  ALU.subtract).then_inc(x_lo_made, 1)

            def pair(i, p):
                dve.wait_ge(started, i + 1)
                dve.wait_ge(now_made, i * 2 + 2)
                if not (known(i) and i < 2):
                    dve.wait_ge(stored[p], (i - p) * (DMA // 2))
                dve.tensor_copy(total[p][:, :, :], start_ps[:, :].rearrange("p (t d) -> p t d", t=T))\
                   .then_inc(start_out, 1)
                for e in range(E):
                    unit = i * E + e
                    dve.wait_ge(y_run, unit + 1)
                    for t in range(T):
                        if e == 0:
                            if t == 0:
                                dve.wait_ge(start_out, i + 1)
                        else:
                            dve.wait_ge(y_added, unit * T + (t + 1 - T))
                        dve.scalar_tensor_tensor(
                            out=total[p][:, t, :], in0=y_ps[e % 2][:, t * P:(t + 1) * P],
                            scalar=route_by_tile(i, t, e, p), in1=total[p][:, t, :],
                            op0=ALU.mult, op1=ALU.add).then_inc(y_added, 1)
                    if e == 4 and not (known(i) and i == PAIRS - 1):
                        split(i + 1, 1 - p)

            def route_by_tile(i, t, e, p):
                return route_now[p][:, t * E + e:t * E + e + 1]

            dve.wait_ge(weights.loaded, weights.loads * DMA)
            dve.tensor_copy(w1_hi[:, :, :], w1_raw[:, :, :]).then_inc(hi_made, 1)
            dve.wait_ge(hi_made, 1)
            dve.tensor_tensor(w1_lo[:, :, :], w1_raw[:, :, :], w1_hi[:, :, :].bitcast(F32), ALU.subtract)
            dve.wait_ge(b1_turned, 1)
            dve.tensor_copy(b1_col[:, :], start_ps[:, 0:E * FS]).then_inc(ready, 1)
            split(0, 0)
            pair(0, 0)
            with dve.Fori(0, PAIRS // 2 - 1) as r:
                pair(r * 2 + 1, 1)
                pair(r * 2 + 2, 0)
            pair(PAIRS - 1, 1)


def tower_program(nc, x, args, out):
    (emb, pos, Wq, bq, Wk, bk, Wv, bv, Wo, bo, W1, b1, W2, b2,
     ln_w, ln_b, W_in, conv_w, conv_b, nu_log, theta_log, gamma_log, B_re, B_im, C_re, C_im, W_out, b_out,
     gate_w, gate_b, e_w1, e_b1, e_w2, e_b2) = args
    tokens = x.shape[0] * x.shape[1]
    E = gate_w.shape[1]
    EPS = 1e-5
    with ExitStack() as ctx:
        whole = Pools(nc, ctx, "all")
        hT = whole.sbuf("hT", [P, tokens])
        ident = whole.sbuf("ident", [P, P])
        with ExitStack() as early:
            first = Pools(nc, early, "first")
            index = first.sbuf("index", [P, tokens // P], U32)
            pos_rows = first.sbuf("pos_rows", [P, 2, P])
            weights = LayerWeights(first, (Wq, bq, Wk, bk, Wv, bv, Wo, bo, W1, b1, W2, b2))
            embed_stage(nc, hT, ident, x, emb, pos, index, pos_rows, 2, beside=weights.load_first)
            layers_stage(nc, hT, ident, weights, emb, index, pos_rows, 2)
        X = whole.sbuf("X", [P, tokens])
        with ExitStack() as middle:
            weights = RecurrentWeights(Pools(nc, middle, "recw"),
                                       (W_in, conv_w, conv_b, nu_log, theta_log, gamma_log,
                                        B_re, B_im, C_re, C_im, W_out, b_out))
            norm_stage(nc, "nr", hT, X, ident, EPS, recurrent=(ln_w, ln_b), beside=weights.load)
            recurrent_stage(nc, hT, X, ident, weights)
        logits = whole.sbuf("logits", [P, tokens // P * E])
        routes = whole.sbuf("routes", [P, tokens // P * E])
        expert_weights = ExpertWeights(whole, (e_w1, e_b1, e_w2, e_b2))
        norm_stage(nc, "ne", hT, X, ident, EPS, gate=(gate_w, gate_b, logits), beside=expert_weights.load)
        routing_stage(nc, logits, routes, tokens // P, E)
        experts_stage(nc, hT, X, routes, ident, expert_weights, out)


_INS = ["L0_tok_emb", "L0_tok_pos", "L0_tok_Wq", "L0_tok_bq", "L0_tok_Wk", "L0_tok_bk", "L0_tok_Wv", "L0_tok_bv",
        "L0_tok_Wo", "L0_tok_bo", "L0_tok_W1", "L0_tok_b1", "L0_tok_W2", "L0_tok_b2",
        "L0_attn_ln_w", "L0_attn_ln_b", "L0_attn_W_in", "L0_attn_conv_w", "L0_attn_conv_b", "L0_attn_nu_log",
        "L0_attn_theta_log", "L0_attn_gamma_log", "L0_attn_B_re", "L0_attn_B_im", "L0_attn_C_re", "L0_attn_C_im",
        "L0_attn_W_out", "L0_attn_b_out",
        "L0_ffn_gate_w", "L0_ffn_gate_b", "L0_ffn_w1", "L0_ffn_b1", "L0_ffn_w2", "L0_ffn_b2"]


def kernel(**inputs):
    import numpy as _np
    import concourse.bacc as _bacc
    from concourse import mybir as _mybir
    from concourse.bass_utils import run_bass_kernel_spmd as _run

    nc = _bacc.Bacc("TRN2", target_bir_lowering=False, num_devices=1)
    arrays, args = {}, []
    for name in ["x"] + _INS:
        a = _np.ascontiguousarray(inputs[name])
        arrays[f"in_{name}"] = a
        args.append(nc.dram_tensor(f"in_{name}", a.shape, _mybir.dt.from_np(a.dtype), kind="ExternalInput").ap())
    x = args[0]
    B, S = inputs["x"].shape
    D = inputs["L0_tok_emb"].shape[1]
    out = nc.dram_tensor("out", (B * S, D), _mybir.dt.float32, kind="ExternalOutput").ap()
    tower_program(nc, x, args[1:], out)
    r = _run(nc, [arrays], core_ids=[0])
    return r.results[0]["out"].reshape(B, S, D)
```
